# Optimizing a Trainium2 kernel written in Bass

```python
import numpy as np
import jax
import jax.numpy as jnp

def _softmax(x, axis=-1):
    return jax.nn.softmax(x, axis=axis)

def _gelu(x):
    return jax.nn.gelu(x, approximate=True)

def _silu(x):
    return jax.nn.silu(x)

def _sigmoid(x):
    return jax.nn.sigmoid(x)

def _layernorm(x, axis=-1, eps=1e-05):
    m = jnp.mean(x, axis=axis, keepdims=True)
    v = jnp.var(x, axis=axis, keepdims=True)
    return (x - m) / jnp.sqrt(v + eps)

def _scatter_add(tgt, idx, src, axis=0):
    return tgt.at[idx].add(src)

def _segment_sum(src, seg, n):
    return jax.ops.segment_sum(src, seg, n)
kernel_name = 'mk_hybrid_d2_jaxref_r8_9ab205'

def setup_inputs(seed: int=0):
    np.random.seed(seed)
    _w = jnp.asarray

    def _L0_attn_a_setup():
        import jax, jax.numpy as jnp
        import numpy as np
        HID, H, B, T = (128, 16, 4, 256)
        D = HID // H
        BETA_MIN, BETA_MAX, EPS = (0.8, 0.999, 1e-06)

        def _rope_cache(T, D):
            inv_freq = 1.0 / 10000.0 ** (jnp.arange(0, D, 2, dtype=jnp.float32) / D)
            t = jnp.arange(T, dtype=jnp.float32)
            freqs = t[:, None] * inv_freq[None, :]
            emb = jnp.concatenate([freqs, freqs], axis=-1)
            return (jnp.cos(emb)[None, :, None, :], jnp.sin(emb)[None, :, None, :])

        def _apply_rope(u, cos, sin):
            u1, u2 = jnp.split(u, 2, axis=-1)
            rot = jnp.concatenate([-u2, u1], axis=-1)
            return u * cos + rot * sin

        def _phi(u):
            return jax.nn.elu(u) + 1.0
        key = jax.random.key(seed)
        ks = jax.random.split(key, 8)
        s = 1.0 / np.sqrt(HID)
        x = jax.random.normal(ks[0], (B, T, HID), dtype=jnp.float32)
        Wq = jax.random.normal(ks[1], (HID, HID), dtype=jnp.float32) * s
        Wk = jax.random.normal(ks[2], (HID, HID), dtype=jnp.float32) * s
        Wv = jax.random.normal(ks[3], (HID, HID), dtype=jnp.float32) * s
        Wb = jax.random.normal(ks[4], (H, HID), dtype=jnp.float32) * s
        bb = jnp.full((H,), float(np.log(0.95 / 0.05)), dtype=jnp.float32)
        Wo = jax.random.normal(ks[5], (HID, HID), dtype=jnp.float32) * s
        bo = jnp.zeros((HID,), dtype=jnp.float32)
        scale = jnp.ones((HID,), dtype=jnp.float32)
        return {'x': x, 'Wq': Wq, 'Wk': Wk, 'Wv': Wv, 'Wb': Wb, 'bb': bb, 'Wo': Wo, 'bo': bo, 'scale': scale}
    _L0_attn_a_in = _L0_attn_a_setup()

    def _L0_attn_b_setup():
        import jax, jax.numpy as jnp
        import numpy as np
        D_MODEL = 128
        HEAD_DIM = 32
        CHUNK = 64
        N_HEADS = D_MODEL // HEAD_DIM
        MEM_ALPHA = 0.03

        def _forward(out, Ww, Wr, decay, log_alpha):
            B, T, D = out.shape
            H, d, C = (N_HEADS, HEAD_DIM, CHUNK)
            x = out.astype(jnp.float32)
            gamma = jax.nn.sigmoid(decay)
            log_gamma = jnp.log(gamma)
            v = (x @ Ww.T).reshape(B, T, H, d).transpose(0, 2, 1, 3)
            xh = x.reshape(B, T, H, d)
            rk = xh / jnp.maximum(jnp.linalg.norm(xh, axis=-1, keepdims=True), 1e-12)
            rk = rk.transpose(0, 2, 1, 3)
            wk = jnp.concatenate([jnp.zeros((B, H, 1, d), jnp.float32), rk[:, :, :-1]], axis=2)
            BH = B * H
            gamma_bh = jnp.tile(gamma, B)
            log_gamma_bh = jnp.tile(log_gamma, B)
            v = v.reshape(BH, T, d)
            rk = rk.reshape(BH, T, d)
            wk = wk.reshape(BH, T, d)
            pad = -T % C
            if pad:
                z = ((0, 0), (0, pad), (0, 0))
                v, rk, wk = (jnp.pad(v, z), jnp.pad(rk, z), jnp.pad(wk, z))
            T_pad = T + pad
            N = T_pad // C
            v = v.reshape(BH, N, C, d)
            rk = rk.reshape(BH, N, C, d)
            wk = wk.reshape(BH, N, C, d)
            p = jnp.arange(C)
            diffs = jnp.maximum(p[:, None] - p[None, :], 0).astype(jnp.float32)
            L = jnp.tril(jnp.exp(diffs * log_gamma_bh[:, None, None]))
            strict = jnp.tril(jnp.ones((C, C), bool), -1)
            A0 = -jnp.where(strict, jnp.einsum('bnid,bnjd->bnij', wk, wk) * L[:, None], 0.0)
            eye = jnp.eye(C, dtype=jnp.float32)
            A = jnp.linalg.inv(eye - A0)
            gp = gamma_bh[:, None, None] ** p[None, :, None]
            gp_tail = gamma_bh[:, None, None] ** (C - 1 - p)[None, :, None]
            gamma_C = (gamma_bh ** C)[:, None, None]
            intra = jnp.where(strict, jnp.einsum('bnid,bnjd->bnij', rk, wk) * L[:, None], 0.0)
            rk_g = rk * gp[:, None]
            wk_g = (wk * gp_tail[:, None]).transpose(0, 1, 3, 2)

            def step(S, inp):
                A_i, v_i, wk_i, rkg_i, wkg_i, intra_i = inp
                v_corr = A_i @ v_i
                wk_corr = A_i @ wk_i
                v_new = v_corr - wk_corr @ S
                o_i = rkg_i @ S + intra_i @ v_new
                S = gamma_C * S + wkg_i @ v_new
                return (S, o_i)
            mv = lambda a: jnp.moveaxis(a, 1, 0)
            S0 = jnp.zeros((BH, d, d), jnp.float32)
            _, o = jax.lax.scan(step, S0, (mv(A), mv(v), mv(wk), mv(rk_g), mv(wk_g), mv(intra)))
            o = jnp.moveaxis(o, 0, 1).reshape(B, H, T_pad, d)
            alpha = jnp.exp(log_alpha)[None, :, None, None]
            o = (alpha * o).transpose(0, 2, 1, 3).reshape(B, T_pad, D)[:, :T]
            return out + (o @ Wr.T).astype(out.dtype)
        key = jax.random.key(seed)
        k0, k1, k2 = jax.random.split(key, 3)
        B, T = (2, 1024)
        out = jax.random.normal(k0, (B, T, D_MODEL), jnp.float32)
        Ww = jax.random.normal(k1, (D_MODEL, D_MODEL), jnp.float32) * 0.02
        Wr = jax.random.normal(k2, (D_MODEL, D_MODEL), jnp.float32) * 0.02
        decay = jnp.full((N_HEADS,), 4.6, jnp.float32)
        log_alpha = jnp.log(jnp.full((N_HEADS,), MEM_ALPHA, jnp.float32))
        return {'out': out, 'Ww': Ww, 'Wr': Wr, 'decay': decay, 'log_alpha': log_alpha}
    _L0_attn_b_in = _L0_attn_b_setup()

    def _L0_ffn_setup():
        import jax, jax.numpy as jnp
        import numpy as np
        B, S, H, F, G = (8, 256, 128, 512, 128)
        EPS = 1e-05

        def _dequant(q, scales, g):
            K, N = q.shape
            w = (q.astype(jnp.float32) - 128.0).reshape(K // g, g, N) * scales[:, None, :]
            return w.reshape(K, N)
        key = jax.random.key(seed)
        ks = jax.random.split(key, 8)
        x = jax.random.normal(ks[0], (B, S, H), dtype=jnp.float32)
        ln_gamma = jnp.ones((H,), jnp.float32)
        ln_beta = jnp.zeros((H,), jnp.float32)
        fc1_q = jax.random.randint(ks[1], (H, F), 0, 32, dtype=jnp.int32)
        fc2_q = jax.random.randint(ks[2], (F, H), 0, 32, dtype=jnp.int32)
        fc1_scales = jax.random.uniform(ks[3], (H // G, F), jnp.float32) * 0.02 + 0.001
        fc2_scales = jax.random.uniform(ks[4], (F // G, H), jnp.float32) * 0.02 + 0.001
        fc1_bias = jax.random.normal(ks[5], (F,), jnp.float32) * 0.02
        fc2_bias = jax.random.normal(ks[6], (H,), jnp.float32) * 0.02
        return {'x': x, 'ln_gamma': ln_gamma, 'ln_beta': ln_beta, 'fc1_q': fc1_q, 'fc1_scales': fc1_scales, 'fc1_bias': fc1_bias, 'fc2_q': fc2_q, 'fc2_scales': fc2_scales, 'fc2_bias': fc2_bias}
    _L0_ffn_in = _L0_ffn_setup()

    def _L1_attn_a_setup():
        import jax, jax.numpy as jnp
        import numpy as np
        key = jax.random.key(seed)
        ks = jax.random.split(key, 5)
        B, T, C = (2, 256, 128)
        x = jax.random.normal(ks[0], (B, T, C), dtype=jnp.float32)
        Wqkv = jax.random.normal(ks[1], (C, 3 * C), dtype=jnp.float32) * C ** (-0.5)
        bqkv = jax.random.normal(ks[2], (3 * C,), dtype=jnp.float32) * 0.02
        Wproj = jax.random.normal(ks[3], (C, C), dtype=jnp.float32) * C ** (-0.5)
        bproj = jax.random.normal(ks[4], (C,), dtype=jnp.float32) * 0.02
        return {'x': x, 'Wqkv': Wqkv, 'bqkv': bqkv, 'Wproj': Wproj, 'bproj': bproj}
    _L1_attn_a_in = _L1_attn_a_setup()

    def _L1_attn_b_setup():
        import jax, jax.numpy as jnp
        import numpy as np
        DIM = 128
        HEADS = 16
        DHEAD = 64
        INNER = HEADS * DHEAD
        B, N = (1, 256)
        ROPE_BASE = 10000.0
        LN_EPS = 1e-05

        def rope_tables(seq_len, d, dtype):
            theta = 1.0 / ROPE_BASE ** (jnp.arange(0, d, 2, dtype=dtype) / d)
            pos = jnp.arange(seq_len, dtype=dtype)
            freqs = pos[:, None] * theta[None, :]
            emb = jnp.concatenate([freqs, freqs], axis=-1)
            return (jnp.cos(emb), jnp.sin(emb))

        def apply_rotary(x, cos, sin):
            x1, x2 = (x[..., ::2], x[..., 1::2])
            x_rot = jnp.stack([-x2, x1], axis=-1).reshape(x.shape)
            return x * cos + x_rot * sin
        key = jax.random.key(seed)
        ks = jax.random.split(key, 6)
        x = jax.random.normal(ks[0], (B, N, DIM), dtype=jnp.float32)
        gamma = jnp.ones((DIM,), dtype=jnp.float32)
        Wq = jax.random.normal(ks[1], (DIM, INNER), dtype=jnp.float32) * 0.02
        Wkv = jax.random.normal(ks[2], (DIM, 2 * INNER), dtype=jnp.float32) * 0.02
        W_bilinear = jnp.eye(DHEAD, dtype=jnp.float32)[None] + jax.random.normal(ks[3], (HEADS, DHEAD, DHEAD), dtype=jnp.float32) * 0.02
        Wo = jax.random.normal(ks[4], (INNER, DIM), dtype=jnp.float32) * 0.02
        return {'x': x, 'gamma': gamma, 'Wq': Wq, 'Wkv': Wkv, 'W_bilinear': W_bilinear, 'Wo': Wo}
    _L1_attn_b_in = _L1_attn_b_setup()

    def _L1_ffn_setup():
        import jax, jax.numpy as jnp
        import numpy as np
        DIM = 128
        N_EXPERTS = 16
        TOP_K = 4
        N_GROUP = 4
        TOPK_GROUP = 2
        MOE_INTER = 64
        SHARED_INTER = 256
        ROUTED_SCALE = 2.5

        def relu2(x):
            return jnp.square(jax.nn.relu(x))

        def _router(x2, gate_w, bias_e):
            T = x2.shape[0]
            logits = x2 @ gate_w.T
            scores = jax.nn.sigmoid(logits)
            sc = jax.lax.stop_gradient(scores + bias_e[None, :])
            grp = sc.reshape(T, N_GROUP, N_EXPERTS // N_GROUP)
            top2, _ = jax.lax.top_k(grp, 2)
            group_scores = top2.sum(-1)
            _, gidx = jax.lax.top_k(group_scores, TOPK_GROUP)
            rows = jnp.arange(T)[:, None]
            gmask = jnp.zeros((T, N_GROUP), dtype=sc.dtype).at[rows, gidx].set(1.0)
            smask = jnp.repeat(gmask, N_EXPERTS // N_GROUP, axis=1)
            masked = jnp.where(smask > 0, sc, 0.0)
            _, topk_idx = jax.lax.top_k(masked, TOP_K)
            topk_w = jnp.take_along_axis(scores, topk_idx, axis=1)
            topk_w = topk_w / (topk_w.sum(-1, keepdims=True) + 1e-20)
            topk_w = topk_w * ROUTED_SCALE
            return (topk_idx, topk_w)
        key = jax.random.key(seed)
        ks = jax.random.split(key, 6)
        hidden_states = jax.random.normal(ks[0], (2, 256, DIM), dtype=jnp.float32)
        gate_w = jax.random.normal(ks[1], (N_EXPERTS, DIM), dtype=jnp.float32) * 0.02
        bias_e = jnp.zeros((N_EXPERTS,), dtype=jnp.float32)
        up_w = jax.random.normal(ks[2], (N_EXPERTS, MOE_INTER, DIM), dtype=jnp.float32) * 0.02
        down_w = jax.random.normal(ks[3], (N_EXPERTS, DIM, MOE_INTER), dtype=jnp.float32) * 0.02
        shared_up = jax.random.normal(ks[4], (SHARED_INTER, DIM), dtype=jnp.float32) * 0.02
        shared_down = jax.random.normal(ks[5], (DIM, SHARED_INTER), dtype=jnp.float32) * 0.02
        return {'hidden_states': hidden_states, 'gate_w': gate_w, 'bias_e': bias_e, 'up_w': up_w, 'down_w': down_w, 'shared_up': shared_up, 'shared_down': shared_down}
    _L1_ffn_in = _L1_ffn_setup()
    _d = {'L0_attn_a_x': _L0_attn_a_in['x'], 'L0_attn_a_Wq': _L0_attn_a_in['Wq'], 'L0_attn_a_Wk': _L0_attn_a_in['Wk'], 'L0_attn_a_Wv': _L0_attn_a_in['Wv'], 'L0_attn_a_Wb': _L0_attn_a_in['Wb'], 'L0_attn_a_bb': _L0_attn_a_in['bb'], 'L0_attn_a_Wo': _L0_attn_a_in['Wo'], 'L0_attn_a_bo': _L0_attn_a_in['bo'], 'L0_attn_a_scale': _L0_attn_a_in['scale'], 'L0_attn_b_Ww': _L0_attn_b_in['Ww'], 'L0_attn_b_Wr': _L0_attn_b_in['Wr'], 'L0_attn_b_decay': _L0_attn_b_in['decay'], 'L0_attn_b_log_alpha': _L0_attn_b_in['log_alpha'], 'L0_ffn_ln_gamma': _L0_ffn_in['ln_gamma'], 'L0_ffn_ln_beta': _L0_ffn_in['ln_beta'], 'L0_ffn_fc1_q': _L0_ffn_in['fc1_q'], 'L0_ffn_fc1_scales': _L0_ffn_in['fc1_scales'], 'L0_ffn_fc1_bias': _L0_ffn_in['fc1_bias'], 'L0_ffn_fc2_q': _L0_ffn_in['fc2_q'], 'L0_ffn_fc2_scales': _L0_ffn_in['fc2_scales'], 'L0_ffn_fc2_bias': _L0_ffn_in['fc2_bias'], 'L1_attn_a_Wqkv': _L1_attn_a_in['Wqkv'], 'L1_attn_a_bqkv': _L1_attn_a_in['bqkv'], 'L1_attn_a_Wproj': _L1_attn_a_in['Wproj'], 'L1_attn_a_bproj': _L1_attn_a_in['bproj'], 'L1_attn_b_gamma': _L1_attn_b_in['gamma'], 'L1_attn_b_Wq': _L1_attn_b_in['Wq'], 'L1_attn_b_Wkv': _L1_attn_b_in['Wkv'], 'L1_attn_b_W_bilinear': _L1_attn_b_in['W_bilinear'], 'L1_attn_b_Wo': _L1_attn_b_in['Wo'], 'L1_ffn_gate_w': _L1_ffn_in['gate_w'], 'L1_ffn_bias_e': _L1_ffn_in['bias_e'], 'L1_ffn_up_w': _L1_ffn_in['up_w'], 'L1_ffn_down_w': _L1_ffn_in['down_w'], 'L1_ffn_shared_up': _L1_ffn_in['shared_up'], 'L1_ffn_shared_down': _L1_ffn_in['shared_down']}
    _x0 = _d['L0_attn_a_x']
    _d['L0_attn_a_x'] = jax.random.normal(jax.random.fold_in(jax.random.key(seed), 1), (1, 2048, 128), dtype=_x0.dtype)
    del _x0
    return _d

def reference(L0_attn_a_x, L0_attn_a_Wq, L0_attn_a_Wk, L0_attn_a_Wv, L0_attn_a_Wb, L0_attn_a_bb, L0_attn_a_Wo, L0_attn_a_bo, L0_attn_a_scale, L0_attn_b_Ww, L0_attn_b_Wr, L0_attn_b_decay, L0_attn_b_log_alpha, L0_ffn_ln_gamma, L0_ffn_ln_beta, L0_ffn_fc1_q, L0_ffn_fc1_scales, L0_ffn_fc1_bias, L0_ffn_fc2_q, L0_ffn_fc2_scales, L0_ffn_fc2_bias, L1_attn_a_Wqkv, L1_attn_a_bqkv, L1_attn_a_Wproj, L1_attn_a_bproj, L1_attn_b_gamma, L1_attn_b_Wq, L1_attn_b_Wkv, L1_attn_b_W_bilinear, L1_attn_b_Wo, L1_ffn_gate_w, L1_ffn_bias_e, L1_ffn_up_w, L1_ffn_down_w, L1_ffn_shared_up, L1_ffn_shared_down):

    def _L0_attn_a_ref(x, Wq, Wk, Wv, Wb, bb, Wo, bo, scale):
        import jax, jax.numpy as jnp
        import numpy as np
        HID, H, B, T = (128, 16, 4, 256)
        D = HID // H
        BETA_MIN, BETA_MAX, EPS = (0.8, 0.999, 1e-06)

        def _rope_cache(T, D):
            inv_freq = 1.0 / 10000.0 ** (jnp.arange(0, D, 2, dtype=jnp.float32) / D)
            t = jnp.arange(T, dtype=jnp.float32)
            freqs = t[:, None] * inv_freq[None, :]
            emb = jnp.concatenate([freqs, freqs], axis=-1)
            return (jnp.cos(emb)[None, :, None, :], jnp.sin(emb)[None, :, None, :])

        def _apply_rope(u, cos, sin):
            u1, u2 = jnp.split(u, 2, axis=-1)
            rot = jnp.concatenate([-u2, u1], axis=-1)
            return u * cos + rot * sin

        def _phi(u):
            return jax.nn.elu(u) + 1.0
        Bx, Tx, hid = x.shape
        q = (x @ Wq.T).reshape(Bx, Tx, H, D)
        k = (x @ Wk.T).reshape(Bx, Tx, H, D)
        v = (x @ Wv.T).reshape(Bx, Tx, H, D)
        beta = jax.nn.sigmoid(x @ Wb.T + bb)
        beta = jnp.clip(beta, BETA_MIN, BETA_MAX).astype(jnp.float32)
        cos, sin = _rope_cache(Tx, D)
        phi_q = _phi(_apply_rope(q, cos, sin)).astype(jnp.float32)
        phi_k = _phi(_apply_rope(k, cos, sin)).astype(jnp.float32)
        v32 = v.astype(jnp.float32)
        pq = jnp.swapaxes(phi_q, 0, 1)
        pk = jnp.swapaxes(phi_k, 0, 1)
        vv = jnp.swapaxes(v32, 0, 1)
        bt = jnp.swapaxes(beta, 0, 1)

        def step(carry, inp):
            S, z = carry
            pqt, pkt, vt, b = inp
            S = b[..., None, None] * S + pkt[..., :, None] * vt[..., None, :]
            z = b[..., None] * z + pkt
            num = jnp.einsum('bhd,bhde->bhe', pqt, S)
            den = jnp.einsum('bhd,bhd->bh', pqt, z) + EPS
            return ((S, z), num / den[..., None])
        S0 = jnp.zeros((Bx, H, D, D), jnp.float32)
        z0 = jnp.zeros((Bx, H, D), jnp.float32)
        _, outs = jax.lax.scan(step, (S0, z0), (pq, pk, vv, bt))
        attn = jnp.swapaxes(outs, 0, 1).reshape(Bx, Tx, hid).astype(x.dtype)
        y = attn @ Wo.T + bo
        h = x + y
        rms = jnp.sqrt(jnp.mean(h * h, axis=-1, keepdims=True) + EPS)
        return h / rms * scale

    def _L0_attn_b_ref(out, Ww, Wr, decay, log_alpha):
        import jax, jax.numpy as jnp
        import numpy as np
        D_MODEL = 128
        HEAD_DIM = 32
        CHUNK = 64
        N_HEADS = D_MODEL // HEAD_DIM
        MEM_ALPHA = 0.03

        def _forward(out, Ww, Wr, decay, log_alpha):
            B, T, D = out.shape
            H, d, C = (N_HEADS, HEAD_DIM, CHUNK)
            x = out.astype(jnp.float32)
            gamma = jax.nn.sigmoid(decay)
            log_gamma = jnp.log(gamma)
            v = (x @ Ww.T).reshape(B, T, H, d).transpose(0, 2, 1, 3)
            xh = x.reshape(B, T, H, d)
            rk = xh / jnp.maximum(jnp.linalg.norm(xh, axis=-1, keepdims=True), 1e-12)
            rk = rk.transpose(0, 2, 1, 3)
            wk = jnp.concatenate([jnp.zeros((B, H, 1, d), jnp.float32), rk[:, :, :-1]], axis=2)
            BH = B * H
            gamma_bh = jnp.tile(gamma, B)
            log_gamma_bh = jnp.tile(log_gamma, B)
            v = v.reshape(BH, T, d)
            rk = rk.reshape(BH, T, d)
            wk = wk.reshape(BH, T, d)
            pad = -T % C
            if pad:
                z = ((0, 0), (0, pad), (0, 0))
                v, rk, wk = (jnp.pad(v, z), jnp.pad(rk, z), jnp.pad(wk, z))
            T_pad = T + pad
            N = T_pad // C
            v = v.reshape(BH, N, C, d)
            rk = rk.reshape(BH, N, C, d)
            wk = wk.reshape(BH, N, C, d)
            p = jnp.arange(C)
            diffs = jnp.maximum(p[:, None] - p[None, :], 0).astype(jnp.float32)
            L = jnp.tril(jnp.exp(diffs * log_gamma_bh[:, None, None]))
            strict = jnp.tril(jnp.ones((C, C), bool), -1)
            A0 = -jnp.where(strict, jnp.einsum('bnid,bnjd->bnij', wk, wk) * L[:, None], 0.0)
            eye = jnp.eye(C, dtype=jnp.float32)
            A = jnp.linalg.inv(eye - A0)
            gp = gamma_bh[:, None, None] ** p[None, :, None]
            gp_tail = gamma_bh[:, None, None] ** (C - 1 - p)[None, :, None]
            gamma_C = (gamma_bh ** C)[:, None, None]
            intra = jnp.where(strict, jnp.einsum('bnid,bnjd->bnij', rk, wk) * L[:, None], 0.0)
            rk_g = rk * gp[:, None]
            wk_g = (wk * gp_tail[:, None]).transpose(0, 1, 3, 2)

            def step(S, inp):
                A_i, v_i, wk_i, rkg_i, wkg_i, intra_i = inp
                v_corr = A_i @ v_i
                wk_corr = A_i @ wk_i
                v_new = v_corr - wk_corr @ S
                o_i = rkg_i @ S + intra_i @ v_new
                S = gamma_C * S + wkg_i @ v_new
                return (S, o_i)
            mv = lambda a: jnp.moveaxis(a, 1, 0)
            S0 = jnp.zeros((BH, d, d), jnp.float32)
            _, o = jax.lax.scan(step, S0, (mv(A), mv(v), mv(wk), mv(rk_g), mv(wk_g), mv(intra)))
            o = jnp.moveaxis(o, 0, 1).reshape(B, H, T_pad, d)
            alpha = jnp.exp(log_alpha)[None, :, None, None]
            o = (alpha * o).transpose(0, 2, 1, 3).reshape(B, T_pad, D)[:, :T]
            return out + (o @ Wr.T).astype(out.dtype)
        return _forward(out, Ww, Wr, decay, log_alpha)

    def _L0_ffn_ref(x, ln_gamma, ln_beta, fc1_q, fc1_scales, fc1_bias, fc2_q, fc2_scales, fc2_bias):
        import jax, jax.numpy as jnp
        import numpy as np
        B, S, H, F, G = (8, 256, 128, 512, 128)
        EPS = 1e-05

        def _dequant(q, scales, g):
            K, N = q.shape
            w = (q.astype(jnp.float32) - 128.0).reshape(K // g, g, N) * scales[:, None, :]
            return w.reshape(K, N)
        residual = x
        mu = jnp.mean(x, axis=-1, keepdims=True)
        var = jnp.mean(jnp.square(x - mu), axis=-1, keepdims=True)
        h = (x - mu) * jax.lax.rsqrt(var + EPS) * ln_gamma + ln_beta
        hf = h.reshape(-1, H)
        w1 = _dequant(fc1_q, fc1_scales, G)
        y = hf @ w1 + fc1_bias
        y = jax.nn.silu(y)
        w2 = _dequant(fc2_q, fc2_scales, G)
        z = y @ w2 + fc2_bias
        return residual + 0.5 * z.reshape(residual.shape)

    def _L1_attn_a_ref(x, Wqkv, bqkv, Wproj, bproj):
        import jax, jax.numpy as jnp
        import numpy as np
        B, T, C = x.shape
        n_head = 16
        hd = C // n_head
        x_proj = x @ Wqkv + bqkv
        q = x_proj[:, :, :C].reshape(B, n_head, T, hd)
        k = x_proj[:, :, C:2 * C].reshape(B, n_head, T, hd)
        v = x_proj[:, :, 2 * C:].reshape(B, n_head, T, hd)
        att = jnp.einsum('bhtd,bhsd->bhts', q, k) * (1.0 / jnp.sqrt(jnp.float32(hd)))
        causal = jnp.tril(jnp.ones((T, T), dtype=bool))
        att = jnp.where(causal, att, jnp.float32(-jnp.inf))
        att = jax.nn.softmax(att, axis=-1)
        y = att @ v
        y = jnp.transpose(y, (0, 2, 1, 3)).reshape(B, T, C)
        return y @ Wproj + bproj

    def _L1_attn_b_ref(x, gamma, Wq, Wkv, W_bilinear, Wo):
        import jax, jax.numpy as jnp
        import numpy as np
        DIM = 128
        HEADS = 16
        DHEAD = 64
        INNER = HEADS * DHEAD
        B, N = (1, 256)
        ROPE_BASE = 10000.0
        LN_EPS = 1e-05

        def rope_tables(seq_len, d, dtype):
            theta = 1.0 / ROPE_BASE ** (jnp.arange(0, d, 2, dtype=dtype) / d)
            pos = jnp.arange(seq_len, dtype=dtype)
            freqs = pos[:, None] * theta[None, :]
            emb = jnp.concatenate([freqs, freqs], axis=-1)
            return (jnp.cos(emb), jnp.sin(emb))

        def apply_rotary(x, cos, sin):
            x1, x2 = (x[..., ::2], x[..., 1::2])
            x_rot = jnp.stack([-x2, x1], axis=-1).reshape(x.shape)
            return x * cos + x_rot * sin
        b, n, _ = x.shape
        mu = jnp.mean(x, axis=-1, keepdims=True)
        var = jnp.var(x, axis=-1, keepdims=True)
        xn = (x - mu) / jnp.sqrt(var + LN_EPS) * gamma
        q = xn @ Wq
        kv = xn @ Wkv
        k, v = jnp.split(kv, 2, axis=-1)

        def to_heads(t):
            return t.reshape(b, n, HEADS, DHEAD).transpose(0, 2, 1, 3)
        q, k, v = map(to_heads, (q, k, v))
        cos, sin = rope_tables(n, DHEAD, x.dtype)
        q = apply_rotary(q, cos, sin) * DHEAD ** (-0.5)
        k = apply_rotary(k, cos, sin)
        kt = jnp.einsum('bhnd,hde->bhne', k, W_bilinear)
        sim = jnp.einsum('bhid,bhjd->bhij', q, kt)
        attn = jax.nn.softmax(sim, axis=-1)
        out = jnp.einsum('bhij,bhjd->bhid', attn, v)
        out = out.transpose(0, 2, 1, 3).reshape(b, n, INNER)
        return out @ Wo

    def _L1_ffn_ref(hidden_states, gate_w, bias_e, up_w, down_w, shared_up, shared_down):
        import jax, jax.numpy as jnp
        import numpy as np
        DIM = 128
        N_EXPERTS = 16
        TOP_K = 4
        N_GROUP = 4
        TOPK_GROUP = 2
        MOE_INTER = 64
        SHARED_INTER = 256
        ROUTED_SCALE = 2.5

        def relu2(x):
            return jnp.square(jax.nn.relu(x))

        def _router(x2, gate_w, bias_e):
            T = x2.shape[0]
            logits = x2 @ gate_w.T
            scores = jax.nn.sigmoid(logits)
            sc = jax.lax.stop_gradient(scores + bias_e[None, :])
            grp = sc.reshape(T, N_GROUP, N_EXPERTS // N_GROUP)
            top2, _ = jax.lax.top_k(grp, 2)
            group_scores = top2.sum(-1)
            _, gidx = jax.lax.top_k(group_scores, TOPK_GROUP)
            rows = jnp.arange(T)[:, None]
            gmask = jnp.zeros((T, N_GROUP), dtype=sc.dtype).at[rows, gidx].set(1.0)
            smask = jnp.repeat(gmask, N_EXPERTS // N_GROUP, axis=1)
            masked = jnp.where(smask > 0, sc, 0.0)
            _, topk_idx = jax.lax.top_k(masked, TOP_K)
            topk_w = jnp.take_along_axis(scores, topk_idx, axis=1)
            topk_w = topk_w / (topk_w.sum(-1, keepdims=True) + 1e-20)
            topk_w = topk_w * ROUTED_SCALE
            return (topk_idx, topk_w)
        B, S, D = hidden_states.shape
        x2 = hidden_states.reshape(-1, D)
        T = x2.shape[0]
        topk_idx, topk_w = _router(x2, gate_w, bias_e)
        rows = jnp.arange(T)[:, None]
        combine = jnp.zeros((T, N_EXPERTS), dtype=topk_w.dtype).at[rows, topk_idx].add(topk_w)

        def body(acc, inp):
            wu, wd, cw = inp
            y = relu2(x2 @ wu.T) @ wd.T
            return (acc + cw[:, None] * y, None)
        routed, _ = jax.lax.scan(body, jnp.zeros_like(x2), (up_w, down_w, combine.T))
        shared = relu2(x2 @ shared_up.T) @ shared_down.T
        out = routed + shared
        return out.reshape(B, S, D)
    x = L0_attn_a_x
    x = x + _L0_attn_a_ref(_layernorm(x, axis=-1), L0_attn_a_Wq, L0_attn_a_Wk, L0_attn_a_Wv, L0_attn_a_Wb, L0_attn_a_bb, L0_attn_a_Wo, L0_attn_a_bo, L0_attn_a_scale)
    x = x + _L0_ffn_ref(_layernorm(x, axis=-1), L0_ffn_ln_gamma, L0_ffn_ln_beta, L0_ffn_fc1_q, L0_ffn_fc1_scales, L0_ffn_fc1_bias, L0_ffn_fc2_q, L0_ffn_fc2_scales, L0_ffn_fc2_bias)
    x = x + _L0_attn_b_ref(_layernorm(x, axis=-1), L0_attn_b_Ww, L0_attn_b_Wr, L0_attn_b_decay, L0_attn_b_log_alpha)
    x = x + _L0_ffn_ref(_layernorm(x, axis=-1), L0_ffn_ln_gamma, L0_ffn_ln_beta, L0_ffn_fc1_q, L0_ffn_fc1_scales, L0_ffn_fc1_bias, L0_ffn_fc2_q, L0_ffn_fc2_scales, L0_ffn_fc2_bias)
    x = x + _L1_attn_a_ref(_layernorm(x, axis=-1), L1_attn_a_Wqkv, L1_attn_a_bqkv, L1_attn_a_Wproj, L1_attn_a_bproj)
    x = x + _L1_ffn_ref(_layernorm(x, axis=-1), L1_ffn_gate_w, L1_ffn_bias_e, L1_ffn_up_w, L1_ffn_down_w, L1_ffn_shared_up, L1_ffn_shared_down)
    x = x + _L1_attn_b_ref(_layernorm(x, axis=-1), L1_attn_b_gamma, L1_attn_b_Wq, L1_attn_b_Wkv, L1_attn_b_W_bilinear, L1_attn_b_Wo)
    x = x + _L1_ffn_ref(_layernorm(x, axis=-1), L1_ffn_gate_w, L1_ffn_bias_e, L1_ffn_up_w, L1_ffn_down_w, L1_ffn_shared_up, L1_ffn_shared_down)
    return x

_drawn_inputs = setup_inputs


def setup_inputs(seed=0):
    import zlib

    import numpy as np

    out = dict(_drawn_inputs(seed))
    spreads = {'L0_attn_a_bb': (2.944438934326172, 0.537),
     'L0_attn_a_bo': (0.0, 0.8),
     'L0_attn_a_scale': (1.0, 0.2),
     'L0_attn_b_decay': (4.599999904632568, 0.6),
     'L0_attn_b_log_alpha': (-3.5065579414367676, 0.6),
     'L0_ffn_ln_gamma': (1.0, 0.2),
     'L0_ffn_ln_beta': (0.0, 0.1),
     'L1_attn_b_gamma': (1.0, 0.6),
     'L1_ffn_bias_e': (0.0, 0.8)}
    factors = {'L0_attn_a_Wq': 3.557,
     'L0_attn_a_Wb': 4.597,
     'L0_attn_b_Ww': 8.0,
     'L0_attn_b_Wr': 8.0,
     'L0_ffn_fc1_bias': 8.0,
     'L0_ffn_fc2_bias': 8.0,
     'L1_attn_a_Wqkv': 8.0,
     'L1_attn_a_bqkv': 8.0,
     'L1_attn_a_Wproj': 8.0,
     'L1_attn_a_bproj': 64.0,
     'L1_attn_b_Wq': 8.0,
     'L1_attn_b_Wkv': 8.0,
     'L1_attn_b_W_bilinear': 8.0,
     'L1_attn_b_Wo': 8.0,
     'L1_ffn_gate_w': 22.797,
     'L1_ffn_up_w': 8.0,
     'L1_ffn_down_w': 8.0,
     'L1_ffn_shared_up': 8.0,
     'L1_ffn_shared_down': 8.0}
    for name, (base, spread) in spreads.items():
        noise = np.random.default_rng([zlib.crc32(name.encode()), seed]).standard_normal(out[name].shape)
        drawn = base * np.exp(spread * noise) if base else spread * noise
        out[name] = jnp.asarray(drawn.astype(out[name].dtype))
    for name, factor in factors.items():
        out[name] = (out[name] * factor).astype(out[name].dtype)
    return out
```

```python
from contextlib import ExitStack

import concourse.bass as bass
from concourse import mybir

ALU = mybir.AluOpType
ACT = mybir.ActivationFunctionType
AX = mybir.AxisListType
F32 = mybir.dt.float32
BF16 = mybir.dt.bfloat16
I32 = mybir.dt.int32

P = 128
T = 2048
NT = T // P
CH = 512
NC = T // CH
TC = CH // P
LN_EPS = 1e-5


class Stage:

    def __init__(self, nc, name):
        self.nc, self.name, self.sems, self.stack = nc, name, {}, ExitStack()

    def __enter__(self):
        return self

    def __exit__(self, *e):
        self.stack.close()
        self.nc.clear_and_free_semaphores(list(self.sems.values()))
        self.nc.all_engine_barrier()

    def sb(self, name, shape, dt=F32):
        return self.stack.enter_context(self.nc.sbuf_tensor(f"{self.name}_{name}", shape, dt))

    def ps(self, name, shape, dt=F32):
        return self.stack.enter_context(self.nc.psum_tensor(f"{self.name}_{name}", shape, dt))

    def __call__(self, name):
        if name not in self.sems:
            self.sems[name] = self.nc.alloc_semaphore(f"{self.name}_{name}")
        return self.sems[name]


class InOrder:

    def __init__(self, eng, S, c=0, per={}, start={}):
        self.eng, self.S, self.c, self.per, self.start, self.seen = eng, S, c, per, start, {}

    def __call__(self, instruction, name):
        self.seen[name] = self.seen.get(name, 0) + 1
        instruction.then_inc(self.S(name), 1)
        self.eng.wait_ge(self.S(name), self.c * self.per.get(name, 1) + self.start.get(name, 0) + self.seen[name])


def layernorm(nc, G, name, loads, inner, gain=None, shift=None, sums=None):
    X, U, UT, ident, mhalf = G["X"], G["U"], G["UT"], G["ident"], G["mhalf"]
    with Stage(nc, name) as S:
        stats = S.sb("stats", [P, NT, 6])
        mean, var, rstd = S.sb("mean", [P, NT]), S.sb("var", [P, NT]), S.sb("rstd", [P, NT])
        a, b, c, ve = (S.sb(n, [P, NT]) for n in ("a", "b", "c", "ve"))
        rstd2 = S.sb("rstd2", [P, NT])
        H = S.sb("H", [P, NT, P]) if inner else U
        turned = S.ps("turned", [P, NC, CH])
        with nc.Block() as block:
            @block.sync
            def _(sp):
                for dst, src in loads:
                    sp.dma_start(dst, src).then_inc(S("loaded"), 16)
                if loads:
                    sp.wait_ge(S("loaded"), 16 * len(loads))

            @block.vector
            def _(dve):
                o = InOrder(dve, S)
                for i in range(NT):
                    o(nc.vector.bn_stats(stats[:, i, :], X[:, i, :]), "stats")
                o(nc.vector.tensor_tensor(a[:, :], stats[:, :, 1], stats[:, :, 4], ALU.add), "halves")
                o(nc.vector.tensor_tensor(b[:, :], stats[:, :, 1], stats[:, :, 4], ALU.subtract), "halves")
                o(nc.vector.tensor_tensor(c[:, :], stats[:, :, 2], stats[:, :, 5], ALU.add), "halves")
                o(nc.vector.tensor_scalar(mean[:, :], a[:, :], 0.5, None, ALU.mult), "mean")
                o(nc.vector.scalar_tensor_tensor(out=a[:, :], in0=b[:, :], scalar=0.25, in1=b[:, :],
                                               op0=ALU.mult, op1=ALU.mult), "spread")
                o(nc.vector.scalar_tensor_tensor(out=var[:, :], in0=c[:, :], scalar=1.0 / P, in1=a[:, :],
                                               op0=ALU.mult, op1=ALU.add), "var")
                o(nc.vector.tensor_scalar(ve[:, :], var[:, :], LN_EPS, None, ALU.add), "ve")
                dve.wait_ge(S("rstd"), 1)
                for i in range(NT):
                    o(nc.vector.tensor_scalar(U[:, i, :], X[:, i, :], mean[:, i:i + 1], rstd[:, i:i + 1],
                                            ALU.subtract, ALU.mult), "u")
                    if inner and i == 0:
                        o(nc.vector.tensor_tensor(a[:, :], rstd[:, :], rstd[:, :], ALU.mult), "sq")
                        o(nc.vector.tensor_tensor(b[:, :], a[:, :], var[:, :], ALU.mult), "var2")
                        o(nc.vector.tensor_scalar(c[:, :], b[:, :], LN_EPS, None, ALU.add), "ve2")
                if gain is not None and loads:
                    dve.wait_ge(S("loaded"), 16 * len(loads))
                for k in range(NC):
                    dve.wait_ge(S("turned"), k + 1)
                    dst = UT[:, k * CH:(k + 1) * CH]
                    if gain is not None:
                        o(nc.vector.tensor_scalar(dst, turned[:, k, :], gain, shift, ALU.mult,
                                                ALU.add if shift is not None else ALU.bypass), "ut")
                    else:
                        o(nc.vector.tensor_copy(dst, turned[:, k, :]), "ut")

            @block.gpsimd
            def _(pool):
                pool.wait_ge(S("ve"), 1)
                pool.tensor_tensor(rstd[:, :], ve[:, :], mhalf[:, 0:NT], ALU.pow).then_inc(S("rstd"), 1)
                if inner:
                    pool.wait_ge(S("ve2"), 1)
                    pool.tensor_tensor(rstd2[:, :], c[:, :], mhalf[:, 0:NT], ALU.pow).then_inc(S("rstd2"), 1)

            @block.scalar
            def _(act):
                if inner:
                    act.wait_ge(S("rstd2"), 1)
                    for i in range(NT):
                        act.wait_ge(S("u"), i + 1)
                        nc.scalar.activation(H[:, i, :], U[:, i, :], ACT.Copy,
                                             scale=rstd2[:, i:i + 1]).then_inc(S("h"), 1)

            @block.tensor
            def _(pe):
                for i in range(NT):
                    pe.wait_ge(S("h" if inner else "u"), i + 1)
                    mm = nc.tensor.transpose(turned[:, i // TC, (i % TC) * P:(i % TC + 1) * P], H[:, i, :],
                                             ident[:, :])
                    if i % TC == TC - 1:
                        mm.then_inc(S("turned"), 1)


def linear_attention(nc, G, W):
    H, D = 16, 8
    X, U, UT, ident, mhalf = G["X"], G["U"], G["UT"], G["ident"], G["mhalf"]
    with Stage(nc, "la") as S:
        wqk = S.sb("wqk", [P, 4, P])
        wv = S.sb("wv", [P, D, P])
        wb, wo = S.sb("wb", [P, P]), S.sb("wo", [P, P])
        cos, sin = S.sb("cos", [P, T]), S.sb("sin", [P, T])
        pick = S.sb("pick", [P, D + 1, P])
        bb, nbb = S.sb("bb", [P, 1]), S.sb("nbb", [P, 1])
        bo, scale = S.sb("bo", [P, P]), S.sb("scale", [P, P])
        layernorm(nc, G, "ln1", [
            (wqk[:, :, :], W["la_wqk"]), (wb[:, :], W["la_wb"]), (bb[:, :], W["la_bb"]),
            (cos[:, :], W["la_cos"]), (sin[:, :], W["la_sin"]), (wv[:, :, :], W["la_wv"]),
            (pick[:, :, :], W["la_pick"]), (wo[:, :], W["la_wo"]),
            (bo[:, :], W["la_bo"].to_broadcast([P, P])), (scale[:, :], W["la_scale"].to_broadcast([P, P]))], False)
        acc = [S.ps(f"acc{k}", [P, CH]) for k in range(8)]
        rot = S.sb("rot", [P, 4, CH])
        qk = S.sb("qk", [P, 2, CH])
        low = S.sb("low", [P, 2, CH])
        ex = S.sb("ex", [P, 2, CH])
        phi = S.sb("phi", [P, 2, CH])
        beta = S.sb("beta", [P, CH])
        kv = S.sb("kv", [P, 2, CH])
        st = S.sb("st", [P, D + 1, CH])
        last = S.sb("last", [P, D + 1])
        sq = S.sb("sq", [P, 2, CH])
        rden = S.sb("rden", [P, CH])
        attn = S.sb("attn", [P, CH])
        h = S.sb("h", [P, TC, P])
        hh = S.sb("hh", [P, TC, P])
        ms, rr = S.sb("ms", [P, TC]), S.sb("rr", [P, TC])
        with nc.Block() as block:
            @block.tensor
            def _(pe):
                with pe.Fori(0, NC) as c:
                    rhs = UT[:, bass.ts(c, CH)]
                    pe.wait_ge(S("y_read"), c + 1)
                    for n in range(4):
                        nc.tensor.matmul(acc[n][:, :], wqk[:, n, :], rhs, start=True, stop=True).then_inc(S("qk"), 1)
                    nc.tensor.matmul(acc[4][:, :], wb[:, :], rhs, start=True, stop=True).then_inc(S("zb"), 1)
                    for e in range(D + 1):
                        if e < D:
                            if e < 2:
                                pe.wait_ge(S("v_read"), D * c + e + 1)
                            else:
                                pe.wait_ge(S("v_read"), D * c + e + 1)
                            nc.tensor.matmul(acc[5 + e % 2][:, :], wv[:, e, :], rhs, start=True,
                                             stop=True).then_inc(S("v"), 1)
                        if e >= 1:
                            pe.wait_ge(S("sq"), (D + 1) * c + e)
                            if e == 1:
                                pe.wait_ge(S("rot"), 4 * c + 4)
                            nc.tensor.matmul(acc[0][:, :], pick[:, e - 1, :], sq[:, (e - 1) % 2, :], start=(e == 1),
                                             stop=(e == D)).then_inc(S("num"), 1)
                    pe.wait_ge(S("sq"), (D + 1) * (c + 1))
                    nc.tensor.matmul(acc[1][:, :], pick[:, D, :], sq[:, D % 2, :], start=True,
                                     stop=True).then_inc(S("num"), 1)
                    pe.wait_ge(S("attn"), c + 1)
                    for i in range(TC):
                        mm = nc.tensor.matmul(acc[7][:, i * P:(i + 1) * P], attn[:, i * P:(i + 1) * P], wo[:, :],
                                              start=True, stop=True)
                    mm.then_inc(S("y"), 1)

            @block.scalar
            def _(act):
                nc.scalar.activation(ms[:, :], mhalf[:, 0:TC], ACT.Exp).then_inc(S("table"), 1)
                with act.Fori(0, NC) as c:
                    act.wait_ge(S("low"), c + 1)
                    nc.scalar.activation(ex[:, :, :], low[:, :, :], ACT.Exp).then_inc(S("ex"), 1)
                    act.wait_ge(S("zb"), c + 1)
                    act.wait_ge(S("nbb"), 1)
                    act.wait_ge(S("beta"), c + 1)
                    nc.scalar.activation(beta[:, :], acc[4][:, :], ACT.Exp, bias=nbb[:, 0:1],
                                         scale=-1.0).then_inc(S("eb"), 1)

            @block.vector
            def _(dve):
                dve.sem_inc(S("beta"), 1)
                dve.sem_inc(S("v_read"), 2)
                dve.sem_inc(S("y_read"), 1)
                dve.wait_ge(S("table"), 1)
                o = InOrder(dve, S)
                o(nc.vector.memset(last[:, :], 0.0), "start")
                o(nc.vector.tensor_scalar(nbb[:, :], bb[:, :], -1.0, None, ALU.mult), "nbb")
                with dve.Fori(0, NC) as c:
                    o = InOrder(dve, S, c, {"rot": 4, "v_read": D, "scan": D + 1, "sq": D + 1},
                                {"beta": 1, "v_read": 2, "y_read": 1})
                    for n in range(4):
                        dve.wait_ge(S("qk"), 4 * c + n + 1)
                        o(nc.vector.tensor_tensor(rot[:, n, :], acc[n][:, :],
                                                (cos if n % 2 == 0 else sin)[:, bass.ts(c, CH)],
                                                ALU.mult), "rot")
                    o(nc.vector.tensor_tensor(qk[:, :, :], rot[:, 0:4:2, :], rot[:, 1:4:2, :],
                                            ALU.add), "rotated")
                    o(nc.vector.tensor_scalar(low[:, :, :], qk[:, :, :], 0.0, None, ALU.min), "low")
                    dve.wait_ge(S("ex"), c + 1)
                    o(nc.vector.scalar_tensor_tensor(out=phi[:, :, :], in0=qk[:, :, :], scalar=0.0, in1=ex[:, :, :],
                                                   op0=ALU.max, op1=ALU.add), "phi")
                    dve.wait_ge(S("eb"), c + 1)
                    o(nc.vector.tensor_scalar(rden[:, :], beta[:, :], 1.0, None, ALU.add), "eb1")
                    o(nc.vector.reciprocal(attn[:, :], rden[:, :]), "sig")
                    o(nc.vector.tensor_scalar(beta[:, :], attn[:, :], 0.8, 0.999, ALU.max, ALU.min), "clip")
                    for e in range(D + 1):
                        if e < D:
                            dve.wait_ge(S("v"), D * c + e + 1)
                            o(nc.vector.tensor_tensor(kv[:, e % 2, :], acc[5 + e % 2][:, :], phi[:, 1, :],
                                                    ALU.mult), "v_read")
                            src = kv[:, e % 2, :]
                        else:
                            src = phi[:, 1, :]
                        o(nc.vector.tensor_tensor_scan(st[:, e, :], beta[:, :], src, last[:, e:e + 1],
                                                     ALU.mult, ALU.add), "scan")
                        o(nc.vector.tensor_tensor(sq[:, e % 2, :], st[:, e, :], phi[:, 0, :],
                                                ALU.mult), "sq")
                        if e + 1 < D + 1:
                            if e >= 1:
                                dve.wait_ge(S("num"), (D + 1) * c + e)
                    o(nc.vector.tensor_copy(last[:, :], st[:, :, CH - 1]), "beta")
                    dve.wait_ge(S("num"), (D + 1) * (c + 1))
                    o(nc.vector.tensor_scalar(ex[:, 0, :], acc[1][:, :], 1e-6, None, ALU.add), "den")
                    o(nc.vector.reciprocal(rden[:, :], ex[:, 0, :]), "rden")
                    o(nc.vector.tensor_tensor(attn[:, :], acc[0][:, :], rden[:, :], ALU.mult), "attn")
                    dve.wait_ge(S("y"), c + 1)
                    o(nc.vector.tensor_tensor(hh[:, :, :], acc[7][:, :].rearrange("p (i f) -> p i f", f=P),
                                            U[:, bass.ts(c, TC), :], ALU.add), "y_read")
                    o(nc.vector.tensor_tensor(h[:, :, :], hh[:, :, :],
                                            bo[:, :].unsqueeze(1).to_broadcast([P, TC, P]), ALU.add), "h")
                    o(nc.vector.tensor_tensor(hh[:, :, :], h[:, :, :], h[:, :, :], ALU.mult), "hh")
                    o(nc.vector.tensor_reduce(ms[:, :], hh[:, :, :], AX.X, ALU.add), "ms")
                    o(nc.vector.tensor_scalar(rr[:, :], ms[:, :], 1.0 / P, 1e-6, ALU.mult, ALU.add), "mse")
                    dve.wait_ge(S("rr"), c + 1)
                    o(nc.vector.tensor_tensor(hh[:, :, :], h[:, :, :],
                                            ms[:, :].unsqueeze(2).to_broadcast([P, TC, P]), ALU.mult), "hr")
                    o(nc.vector.tensor_tensor(h[:, :, :], hh[:, :, :],
                                            scale[:, :].unsqueeze(1).to_broadcast([P, TC, P]),
                                            ALU.mult), "hs")
                    o(nc.vector.tensor_tensor(X[:, bass.ts(c, TC), :], X[:, bass.ts(c, TC), :], h[:, :, :],
                                            ALU.add), "x")

            @block.gpsimd
            def _(pool):
                with pool.Fori(0, NC) as c:
                    pool.wait_ge(S("mse"), c + 1)
                    pool.tensor_tensor(ms[:, :], rr[:, :], mhalf[:, 0:TC], ALU.pow).then_inc(S("rr"), 1)


def ffn(nc, G, W, name, dequantise):
    X, U, UT = G["X"], G["U"], G["UT"]
    w1, w2, b1, hb2 = G["w1"], G["w2"], G["b1"], G["hb2"]
    FB = 4
    layernorm(nc, G, name + "ln", [], True, G["ffn_gain"][:, 0:1], G["ffn_shift"][:, 0:1])
    with Stage(nc, name) as S:
        if dequantise:
            q1, q2 = S.sb("q1", [P, FB * P], I32), S.sb("q2", [P, FB, P], I32)
            s1, s2 = S.sb("s1", [P, FB * P]), S.sb("s2", [P, FB, P])
            with nc.Block() as block:
                @block.sync
                def _(sp):
                    for n, (dst, src) in enumerate([
                            (q1[:, :], W["fc1_q"]), (s1[:, :], W["fc1_scales"].to_broadcast([P, FB * P])),
                            (q2[:, :, :], W["fc2_q"].rearrange("(b p) n -> p b n", p=P)),
                            (b1[:, :], W["fc1_bias"])]):
                        sp.dma_start(dst, src).then_inc(S("quantised"), 16)
                    for b in range(FB):
                        sp.dma_start(s2[:, b, :], W["fc2_scales"][b:b + 1, :].to_broadcast([P, P])).then_inc(S("quantised"), 16)
                    sp.dma_start(hb2[:, :], W["fc2_bias"].to_broadcast([P, P])).then_inc(S("quantised"), 16)

                @block.vector
                def _(dve):
                    o = InOrder(dve, S)
                    dve.wait_ge(S("quantised"), 16 * (5 + FB))
                    o(nc.vector.scalar_tensor_tensor(out=w1[:, :], in0=q1[:, :], scalar=-128.0, in1=s1[:, :],
                                                   op0=ALU.add, op1=ALU.mult), "w")
                    o(nc.vector.scalar_tensor_tensor(out=w2[:, :, :], in0=q2[:, :, :], scalar=-128.0, in1=s2[:, :, :],
                                                   op0=ALU.add, op1=ALU.mult), "w")
                    o(nc.vector.tensor_scalar(s1[:, 0:P], hb2[:, :], 0.5, None, ALU.mult), "hb")
                    o(nc.vector.tensor_copy(hb2[:, :], s1[:, 0:P]), "w")
        hid = [S.ps(f"hid{b}", [P, CH]) for b in range(FB)]
        z = S.ps("z", [P, TC, P])
        y = S.sb("y", [P, FB, CH])
        xu = S.sb("xu", [P, TC, P])
        xub = S.sb("xub", [P, TC, P])
        with nc.Block() as block:
            @block.tensor
            def _(pe):
                with pe.Fori(0, NC) as c:
                    for b in range(FB):
                        pe.wait_ge(S("y"), FB * c + b + 1)
                        nc.tensor.matmul(hid[b][:, :], w1[:, b * P:(b + 1) * P], UT[:, bass.ts(c, CH)],
                                         start=True, stop=True).then_inc(S("hid"), 1)
                    pe.wait_ge(S("y"), FB * c + 2 * FB)
                    pe.wait_ge(S("x"), c + 1)
                    for i in range(TC):
                        for b in range(FB):
                            mm = nc.tensor.matmul(z[:, i, :], y[:, b, i * P:(i + 1) * P], w2[:, b, :],
                                                  start=(b == 0), stop=(b == FB - 1))
                    mm.then_inc(S("z"), 1)

            @block.scalar
            def _(act):
                act.sem_inc(S("y"), FB)
                nc.scalar.activation(y[:, 0, 0:1], b1[:, 0:1], ACT.Silu).then_inc(S("table"), 1)
                act.wait_ge(S("table"), 1)
                with act.Fori(0, NC) as c:
                    act.wait_ge(S("z_free"), c + 1)
                    for b in range(FB):
                        act.wait_ge(S("hid"), FB * c + b + 1)
                        nc.scalar.activation(y[:, b, :], hid[b][:, :], ACT.Silu, bias=b1[:, b:b + 1]).then_inc(S("y"), 1)

            @block.vector
            def _(dve):
                dve.sem_inc(S("x"), 1)
                dve.sem_inc(S("z_free"), 1)
                with dve.Fori(0, NC) as c:
                    o = InOrder(dve, S, c, {}, {"x": 1})
                    o(nc.vector.tensor_tensor(xu[:, :, :], X[:, bass.ts(c, TC), :], U[:, bass.ts(c, TC), :],
                                            ALU.add), "xu")
                    o(nc.vector.tensor_tensor(xub[:, :, :], xu[:, :, :], hb2[:, :].unsqueeze(1).to_broadcast([P, TC, P]),
                                            ALU.add), "xub")
                    dve.wait_ge(S("z"), c + 1)
                    dve.sem_inc(S("z_free"), 1)
                    o(nc.vector.scalar_tensor_tensor(out=X[:, bass.ts(c, TC), :], in0=z[:, :, :], scalar=0.5,
                                                   in1=xub[:, :, :], op0=ALU.mult, op1=ALU.add), "x")


def experts(nc, G, W, name):
    E, GR, K = 16, 4, 4
    NB, NE = 10, 8
    X, U, UT, ident = G["X"], G["U"], G["UT"], G["ident"]
    with Stage(nc, name) as S:
        up, down = S.sb("up", [P, NB, P]), S.sb("down", [P, NB, P])
        gate, bias = S.sb("gate", [P, E]), S.sb("bias", [P, E])
        tri, trig = S.sb("tri", [P, E, E]), S.sb("trig", [P, GR, GR])
        layernorm(nc, G, name + "ln", [
            (gate[:, :], W["moe_gate"]), (bias[:, :], W["moe_bias"].to_broadcast([P, E])),
            (tri[:, :, :], W["before16"].to_broadcast([P, E * E]).rearrange("p (a b) -> p a b", a=E)),
            (trig[:, :, :], W["before4"].to_broadcast([P, GR * GR]).rearrange("p (a b) -> p a b", a=GR)),
            (up[:, :, :], W["moe_up"]), (down[:, :, :], W["moe_down"])], False)
        cw = S.sb("cw", [P, NT, E])
        router(nc, G, name + "r", gate, bias, tri, trig, cw)
        hid = [S.ps(f"hid{b}", [P, CH]) for b in range(3)]
        crep = [S.ps(f"crep{b}", [P, CH]) for b in range(2)]
        z = S.ps("z", [P, TC, P])
        cwe = S.sb("cwe", [P, TC, E, P // 2])
        r = S.sb("r", [P, 2, CH])
        sq = S.sb("sq", [P, 2, CH])
        hT = S.sb("hT", [P, NB, CH])
        with nc.Block() as block:
            @block.tensor
            def _(pe):
                with pe.Fori(0, NC) as c:
                    pe.wait_ge(S("cwe"), c + 1)
                    for b in range(NB):
                        pe.wait_ge(S("r"), NB * c + b + 1)
                        nc.tensor.matmul(hid[b % 3][:, :], up[:, b, :], UT[:, bass.ts(c, CH)],
                                         start=True, stop=True).then_inc(S("hid"), 1)
                        if b < NE:
                            pe.wait_ge(S("weighted"), NE * c + b + 1)
                            for i in range(TC):
                                w = cwe[:, i, 2 * b:2 * b + 2, :].rearrange("p e f -> p (e f)")
                                mm = nc.tensor.transpose(crep[b % 2][:, i * P:(i + 1) * P], w, ident[:, :])
                            mm.then_inc(S("crep"), 1)
                    pe.wait_ge(S("weighted"), NE * c + NE + 2)
                    pe.wait_ge(S("shared"), 2 * c + 2)
                    pe.wait_ge(S("x"), c + 1)
                    for i in range(TC):
                        for b in range(NB):
                            mm = nc.tensor.matmul(z[:, i, :], hT[:, b, i * P:(i + 1) * P], down[:, b, :],
                                                  start=(b == 0), stop=(b == NB - 1))
                    mm.then_inc(S("z"), 1)

            @block.scalar
            def _(act):
                act.sem_inc(S("r"), 3)
                nc.scalar.activation(sq[:, 0, 0:1], bias[:, 0:1], ACT.Square).then_inc(S("table"), 1)
                act.wait_ge(S("table"), 1)
                with act.Fori(0, NC) as c:
                    act.wait_ge(S("hT_free"), c + 1)
                    for b in range(NB):
                        act.wait_ge(S("hid"), NB * c + b + 1)
                        act.wait_ge(S("squared"), NB * c + b + 1)
                        nc.scalar.activation(r[:, b % 2, :], hid[b % 3][:, :], ACT.Relu).then_inc(S("r"), 1)
                        act.wait_ge(S("r"), NB * c + b + 4)
                        if b < NE:
                            act.wait_ge(S("weighted"), NE * c + b + 1)
                            nc.scalar.activation(sq[:, b % 2, :], r[:, b % 2, :], ACT.Square).then_inc(S("squared"), 1)
                        else:
                            nc.scalar.activation(hT[:, b, :], r[:, b % 2, :], ACT.Square).then_inc(S("shared"), 1)
                            act.wait_ge(S("shared"), 2 * c + b - NE + 1)
                            act.sem_inc(S("squared"), 1)

            @block.gpsimd
            def _(pool):
                with pool.Fori(0, NC) as c:
                    pool.wait_ge(S("crep"), NE * c + 1)
                    pool.tensor_copy(cwe[:, :, :, :], cw[:, bass.ts(c, TC), :].unsqueeze(3).to_broadcast(
                        [P, TC, E, P // 2])).then_inc(S("cwe"), 1)

            @block.vector
            def _(dve):
                dve.sem_inc(S("crep"), 1)
                dve.sem_inc(S("x"), 1)
                dve.sem_inc(S("hT_free"), 1)
                dve.sem_inc(S("weighted"), 2)
                dve.sem_inc(S("squared"), 2)
                with dve.Fori(0, NC) as c:
                    o = InOrder(dve, S, c, {"weighted": NE}, {"x": 1, "weighted": 2})
                    for b in range(NE):
                        dve.wait_ge(S("squared"), NB * c + b + 3)
                        dve.wait_ge(S("crep"), NE * c + b + 2)
                        o(nc.vector.tensor_tensor(hT[:, b, :], crep[b % 2][:, :], sq[:, b % 2, :], ALU.mult), "weighted")
                    dve.wait_ge(S("z"), c + 1)
                    dve.sem_inc(S("hT_free"), 1)
                    o(nc.vector.tensor_tensor(X[:, bass.ts(c, TC), :], z[:, :, :], X[:, bass.ts(c, TC), :],
                                              ALU.add), "x")


def router(nc, G, name, gate, bias, tri, trig, cw):
    E, GR, KE = 16, 4, 4
    KG = E // GR
    with Stage(nc, name) as S:
        logits = S.ps("logits", [P, NT, E])
        score, sc = S.sb("score", [P, NT, E]), S.sb("sc", [P, NT, E])
        big, small, big2, small2, top, second, least, sums = (
            S.sb(n, [P, NT, GR]) for n in ("big", "small", "big2", "small2", "top", "second", "least", "sums"))
        pg, pge = S.sb("pg", [P, NT, GR, GR]), S.sb("pge", [P, NT, GR, GR])
        pa, pae = S.sb("pa", [P, NT, E, E]), S.sb("pae", [P, NT, E, E])
        rg, ra, kept, tot, inv = (S.sb("rg", [P, NT, GR]), S.sb("ra", [P, NT, E]), S.sb("kept", [P, NT, E]),
                                  S.sb("tot", [P, NT]), S.sb("inv", [P, NT]))
        UT = G["UT"]
        with nc.Block() as block:
            @block.tensor
            def _(pe):
                for i in range(NT):
                    mm = nc.tensor.matmul(logits[:, i, :], UT[:, i * P:(i + 1) * P], gate[:, :], start=True, stop=True)
                mm.then_inc(S("logits"), 1)

            @block.scalar
            def _(act):
                act.wait_ge(S("logits"), 1)
                nc.scalar.activation(score[:, :, :], logits[:, :, :], ACT.Sigmoid).then_inc(S("score"), 1)

            @block.vector
            def _(dve):
                o = InOrder(dve, S)
                tt = nc.vector.tensor_tensor
                dve.wait_ge(S("score"), 1)
                o(tt(sc[:, :, :], score[:, :, :], bias[:, :].unsqueeze(1).to_broadcast([P, NT, E]), ALU.add), "sc")
                v = sc[:, :, :].rearrange("p t (g k) -> p t g k", k=KG)
                o(tt(big[:, :, :], v[:, :, :, 0], v[:, :, :, 1], ALU.max), "pairs")
                o(tt(small[:, :, :], v[:, :, :, 0], v[:, :, :, 1], ALU.min), "pairs")
                o(tt(big2[:, :, :], v[:, :, :, 2], v[:, :, :, 3], ALU.max), "pairs")
                o(tt(small2[:, :, :], v[:, :, :, 2], v[:, :, :, 3], ALU.min), "pairs")
                o(tt(top[:, :, :], big[:, :, :], big2[:, :, :], ALU.max), "pairs")
                o(tt(second[:, :, :], big[:, :, :], big2[:, :, :], ALU.min), "pairs")
                o(tt(least[:, :, :], small[:, :, :], small2[:, :, :], ALU.max), "pairs")
                o(tt(big[:, :, :], second[:, :, :], least[:, :, :], ALU.max), "pairs")
                o(tt(sums[:, :, :], top[:, :, :], big[:, :, :], ALU.add), "sums")

                def rank(out, x, n, pairs, equal, before):
                    other, own = (x.unsqueeze(k).to_broadcast([P, NT, n, n]) for k in (2, 3))
                    o(tt(pairs, other, own, ALU.is_gt), "ranks")
                    o(tt(equal, other, own, ALU.is_equal), "ranks")
                    o(tt(equal, equal, before.unsqueeze(1).to_broadcast([P, NT, n, n]), ALU.mult), "ranks")
                    o(tt(pairs, pairs, equal, ALU.add), "ranks")
                    o(nc.vector.tensor_reduce(out, pairs, AX.X, ALU.add), "ranks")

                rank(rg[:, :, :], sums[:, :, :], GR, pg[:, :, :, :], pge[:, :, :, :], trig[:, :, :])
                o(nc.vector.tensor_scalar(top[:, :, :], rg[:, :, :], 2.0, None, ALU.is_lt), "groups")
                o(tt(kept[:, :, :].rearrange("p t (g k) -> p t g k", k=KG), v,
                     top[:, :, :].unsqueeze(3).to_broadcast([P, NT, GR, KG]), ALU.mult), "kept")
                rank(ra[:, :, :], kept[:, :, :], E, pa[:, :, :, :], pae[:, :, :, :], tri[:, :, :])
                o(nc.vector.scalar_tensor_tensor(out=kept[:, :, :], in0=ra[:, :, :], scalar=float(KE), in1=score[:, :, :],
                                                 op0=ALU.is_lt, op1=ALU.mult), "chosen")
                o(nc.vector.tensor_reduce(tot[:, :], kept[:, :, :], AX.X, ALU.add), "total")
                o(nc.vector.tensor_scalar(tot[:, :], tot[:, :], 1e-20, None, ALU.add), "total")
                o(nc.vector.reciprocal(inv[:, :], tot[:, :]), "inverse")
                o(nc.vector.scalar_tensor_tensor(out=cw[:, :, :], in0=kept[:, :, :], scalar=2.5,
                                                 in1=inv[:, :].unsqueeze(2).to_broadcast([P, NT, E]),
                                                 op0=ALU.mult, op1=ALU.mult), "weights")


def split3(nc, o, src, parts, left):
    o(nc.vector.tensor_copy(parts[0], src), "split")
    o(nc.vector.tensor_tensor(left, src, parts[0], ALU.subtract), "split")
    o(nc.vector.tensor_copy(parts[1], left), "split")
    o(nc.vector.tensor_tensor(parts[2], left, parts[1], ALU.subtract), "split")


def causal_attention(nc, G, W):
    NH, D = 16, 8
    X, U, UT, ident, identb = G["X"], G["U"], G["UT"], G["ident"], G["identb"]
    ORDER_Q, ORDER_K = (0, 0, 1, 1, 0, 2), (0, 1, 0, 1, 2, 0)
    SHIFT = 64
    SCALE = float(D) ** -0.5
    VW = 32
    items1 = [(i, k) for i in range(NT) for k in range(i // TC + 1)]
    items2 = [(c, k) for c in range(NC) for k in range(TC * (c + 1))]
    N1, N2 = len(items1), len(items2)
    AHEAD = 2
    B1, B2 = 3, 2
    LATE = 4
    EARLY = 28
    row_of = [nc.dram_tensor(f"ca_row{s}", (3, T), BF16).ap() for s in range(2)]
    rows_of = nc.dram_tensor("ca_rows", (NH, 2, 6 * D, T), BF16).ap()
    with Stage(nc, "ca") as S:
        wqkv = S.sb("wqkv", [P, 3 * P])
        bqkv, bproj = S.sb("bqkv", [P, 3 * P]), S.sb("bproj", [P, P])
        wproj = S.sb("wproj", [P, P])
        later, earlier = S.sb("later", [P, P], BF16), S.sb("earlier", [P, P], BF16)
        maskf = S.sb("maskf", [P, 2, P])
        sel = S.sb("sel", [P, 16])
        layernorm(nc, G, "caln", [
            (wqkv[:, :], W["ca_wqkv"]), (bqkv[:, :], W["ca_bqkv"].to_broadcast([P, 3 * P])),
            (wproj[:, :], W["ca_wproj"]), (bproj[:, :], W["ca_bproj"].to_broadcast([P, P])),
            (maskf[:, :, :], W["ca_mask"]), (sel[:, :], W["ca_sel"])], False)
        parts = S.sb("parts", [P, 2, 3, T], BF16)
        vall = S.sb("vall", [P, NT, P])
        with Stage(nc, "cap") as R:
            proj = [R.ps(f"proj{n}", [P, 3 * P]) for n in range(2)]
            turned = [R.ps(f"turned{n}", [P, TC, P]) for n in range(4)]
            xq = R.sb("xq", [P, 3, NT, NH, D])
            flat = R.sb("flat", [P, 3, T])
            left = R.sb("left", [P, T])
            with nc.Block() as block:
                @block.sync
                def _(sp):
                    for s in range(2):
                        sp.wait_ge(R("split"), 4 * (s + 1))
                        for n in range(6):
                            sp.dma_start(rows_of.rearrange("h s (n d) t -> n s h d t", d=D)[n, s],
                                         parts[:, s, (ORDER_Q, ORDER_K)[s][n], :]).then_inc(R("rows"), 16)
                    sp.wait_ge(R("rows"), 16 * 12)

                @block.tensor
                def _(pe):
                    for i in range(NT):
                        if i >= 2:
                            pe.wait_ge(R("xq"), i - 1)
                        nc.tensor.matmul(proj[i % 2][:, :], UT[:, i * P:(i + 1) * P], wqkv[:, :], start=True,
                                         stop=True).then_inc(R("proj"), 1)
                    pe.wait_ge(R("xq"), NT)
                    for n in range(12):
                        if n >= 4:
                            pe.wait_ge(R("flat"), n - 3)
                        for j in range(4):
                            mm = nc.tensor.transpose(turned[n % 4][:, j, :],
                                                     xq[:, n // 4, 4 * (n % 4) + j, :, :].rearrange("p h d -> p (h d)"),
                                                     ident[:, :])
                        mm.then_inc(R("turned"), 1)
                    for n in range(4):
                        pe.wait_ge(R("flat"), 12)
                        for j in range(TC):
                            mm = nc.tensor.transpose(turned[n][:, j, :], flat[:, 2, (TC * n + j) * P:(TC * n + j + 1) * P],
                                                     ident[:, :])
                        mm.then_inc(R("v_turned"), 1)

                @block.vector
                def _(dve):
                    o = InOrder(dve, R)
                    o(nc.vector.tensor_copy(later[:, :], maskf[:, 0, :]), "mask")
                    o(nc.vector.tensor_copy(earlier[:, :], maskf[:, 1, :]), "mask")
                    for i in range(NT):
                        dve.wait_ge(R("proj"), i + 1)
                        o(nc.vector.tensor_tensor(xq[:, :, :, i, :],
                                                  proj[i % 2][:, :].rearrange("p (s j d) -> p s j d", s=3, d=D),
                                                  bqkv[:, :].rearrange("p (s j d) -> p s j d", s=3, d=D), ALU.add), "xq")
                    for n in range(12):
                        dve.wait_ge(R("turned"), n + 1)
                        o(nc.vector.tensor_copy(
                            flat[:, n // 4, :].rearrange("r (p j) -> r j p", j=NT)[:, 4 * (n % 4):4 * (n % 4) + 4, :],
                            turned[n % 4][:, :, :]), "flat")
                    for n in range(4):
                        dve.wait_ge(R("v_turned"), n + 1)
                        o(nc.vector.tensor_copy(vall[:, TC * n:TC * (n + 1), :], turned[n][:, :, :]), "vall")
                    for s in range(2):
                        split3(nc, o, flat[:, s, :], [parts[:, s, n, :] for n in range(3)], left[:, :])

        y = S.sb("y", [P, NT, P])
        qs = [S.sb(f"qs{s}", [P, T], BF16) for s in range(2)]
        ks = [S.sb(f"ks{s}", [P, T], BF16) for s in range(2)]
        zeros = S.sb("zeros", [3, T], BF16)
        vh = [S.sb(f"vh{s}", [P, NT, VW]) for s in range(2)]
        pt = S.sb("pt", [P, 3, CH])
        most = S.sb("most", [P, NT, NC])
        negm = S.sb("negm", [P, NT])
        nmt, nml = S.sb("nmt", [NT, P]), S.sb("nml", [NT, P])
        nm3 = S.sb("nm3", [NT, 3, P], BF16)
        os_ = S.sb("os", [P, CH])
        den = S.sb("den", [P, TC])
        s1 = [S.ps(f"s1{n}", [P, CH]) for n in range(B1)]
        s2 = [S.ps(f"s2{n}", [P, CH]) for n in range(B2)]
        pv = [S.ps(f"pv{n}", [P, CH]) for n in range(2)]
        misc = S.ps("misc", [P, CH])
        nm_ps = misc[0:NT, 0:P]
        fin = misc[:, 256:256 + TC * 16].rearrange("p (i c) -> p i c", c=16)
        per1 = [[n for n in range(N1) if LATE + n * (EARLY - LATE) // N1 == k] for k in range(N2)]
        with nc.Block() as block:
            @block.sync
            def _(sp):
                def stack(h, g, s):
                    sp.dma_start(qs[s][0:6 * D, :], rows_of[h, 0, :, :]).then_inc(S(f"stack{s}"), 16)
                    sp.dma_start(ks[s][0:6 * D, :], rows_of[h, 1, :, :]).then_inc(S(f"stack{s}"), 16)
                    sp.dma_start(qs[s][SHIFT:SHIFT + 3, :], zeros[:, :]).then_inc(S(f"stack{s}"), 16)

                def shift(h, g, s):
                    sp.wait_ge(S("nm3"), h + 1)
                    sp.dma_start(row_of[s].rearrange("n (i p) -> i n p", p=P), nm3[:, :, :]).then_inc(S(f"row{s}"), 16)
                    sp.wait_ge(S(f"row{s}"), 16 * (g + 1))
                    sp.dma_start(qs[s][SHIFT:SHIFT + 3, :], row_of[s]).then_inc(S(f"shift{s}"), 16)

                def next_stack(h, g, s):
                    sp.wait_ge(S("pass2"), N2 * (h - 1))
                    sp.sem_inc(S("paced"), 1)
                    stack(h, g, s)

                sp.wait_ge(S("clean"), 7)
                for s in range(2):
                    stack(s, 0, s)
                shift(0, 0, 0)
                with sp.Fori(0, NH // 2 - 1) as g:
                    shift(2 * g + 1, g, 1)
                    next_stack(2 * g + 2, g + 1, 0)
                    shift(2 * g + 2, g + 1, 0)
                    next_stack(2 * g + 3, g + 1, 1)
                shift(NH - 1, NH // 2 - 1, 1)

            @block.gpsimd
            def _(pool):
                o = InOrder(pool, S)
                for s in range(2):
                    o(pool.memset(qs[s][:, :], 0.0), "clean")
                    o(pool.memset(ks[s][:, :], 0.0), "clean")
                    o(pool.memset(ks[s][SHIFT:SHIFT + 3, :], 1.0), "clean")
                o(pool.memset(zeros[:, :], 0.0), "clean")
                for s in range(2):
                    o(pool.memset(vh[s][:, :, D:VW], 0.0), "vclean")
                    o(pool.memset(vh[s][:, :, D:D + 1], 1.0), "vclean")
                o(pool.memset(most[:, :, :], -3e38), "vclean")

            @block.tensor
            def _(pe):
                def pass1(h, g, s, n):
                    i, k = items1[n]
                    if n == 0:
                        pe.wait_ge(S(f"stack{s}"), 16 * 3 * (g + 1))
                    pe.wait_ge(S("max"), N1 * h + n + 1)
                    width = min(CH, (i + 1) * P - k * CH)
                    last = k == i // TC
                    mm = nc.tensor.matmul(s1[n % B1][:, 0:width], qs[s][:, i * P:(i + 1) * P],
                                          ks[s][:, k * CH:k * CH + width], start=True, stop=not last)
                    if last:
                        mm = nc.tensor.matmul(s1[n % B1][:, width - P:width], identb[:, :], later[:, :],
                                              start=False, stop=True)
                    mm.then_inc(S("pass1"), 1)

                def pass2(h, g, s, n):
                    c, k = items2[n]
                    if n == 0:
                        pe.wait_ge(S(f"shift{s}"), 16 * (g + 1))
                    pe.wait_ge(S("exp"), N2 * h + n + 1)
                    lo = max(0, k - TC * c) * P
                    mm = nc.tensor.matmul(s2[n % B2][:, lo:CH], ks[s][:, k * P:(k + 1) * P],
                                          qs[s][:, c * CH + lo:(c + 1) * CH], start=True, stop=k < TC * c)
                    if k >= TC * c:
                        mm = nc.tensor.matmul(s2[n % B2][:, lo:lo + P], identb[:, :], earlier[:, :],
                                              start=False, stop=True)
                    mm.then_inc(S("pass2"), 1)

                def values(h, g, s, n):
                    c, k = items2[n]
                    if n == 0:
                        pe.wait_ge(S("vh"), h + 1)
                    if k == 0:
                        pe.wait_ge(S("os"), NC * h + c + 1)
                    pe.wait_ge(S("exp"), N2 * h + n + B2 + 1)
                    lo = max(0, k - TC * c) * P
                    grp = (k % TC) * VW if c else 0
                    nc.tensor.matmul(pv[c % 2][grp:grp + VW, lo:CH], vh[s][:, k, :], pt[:, n % 3, lo:CH],
                                     start=(k < TC if c else k == 0), stop=(k >= TC * c if c else k == TC - 1)
                                     ).then_inc(S("pv"), 1)

                def finish(h, c, more):
                    pe.wait_ge(S("os"), NC * h + c + 3)
                    if more and c == NC - 1:
                        pe.wait_ge(S("nmt_here"), h + 2)
                    pe.wait_ge(S("y"), NC * h + c + 1)
                    rows = P if c else VW
                    for i in range(TC):
                        mm = nc.tensor.matmul(fin[:, i, :], os_[0:rows, i * P:(i + 1) * P], sel[0:rows, :],
                                              start=True, stop=True)
                    mm.then_inc(S("fin"), 1)

                def turn(h, divided):
                    pe.wait_ge(S("negm"), h + 1)
                    if divided:
                        pe.wait_ge(S("y"), NC * (h - 1) + divided + 1)
                    nc.tensor.transpose(nm_ps, negm[:, :], ident[:, :]).then_inc(S("nmt"), 1)

                def head(h, g, s, more):
                    g1 = g if s == 0 else g + 1
                    for n in range(N2 + AHEAD + 1):
                        if n < N2:
                            if more:
                                for m in per1[n]:
                                    pass1(h + 1, g1, 1 - s, m)
                            pass2(h, g, s, n)
                        if n == EARLY + 3 and more:
                            turn(h + 1, sum(TC * (c + 1) * (c + 2) // 2 - 1 + AHEAD + 1 < n for c in range(NC)))
                        if AHEAD <= n < N2 + AHEAD:
                            values(h, g, s, n - AHEAD)
                        m = n - AHEAD - 1
                        if m >= 0 and items2[m][1] == TC * (items2[m][0] + 1) - 1:
                            finish(h, items2[m][0], more)

                for n in range(N1):
                    pass1(0, 0, 0, n)
                turn(0, 0)
                with pe.Fori(0, NH // 2 - 1) as g:
                    head(2 * g, g, 0, True)
                    head(2 * g + 1, g, 1, True)
                head(NH - 2, NH // 2 - 1, 0, True)
                head(NH - 1, NH // 2 - 1, 1, False)

            @block.scalar
            def _(act):
                act.sem_inc(S("exp"), B2)
                nc.scalar.activation(pt[:, 0, 0:1], ident[:, 0:1], ACT.Exp).then_inc(S("table"), 1)
                act.wait_ge(S("table"), 1)

                def sums(h, c):
                    act.wait_ge(S("pv"), N2 * h + TC * (c + 1) * (c + 2) // 2 + 3)
                    act.wait_ge(S("fin"), NC * h + c + 1)
                    rows = P if c else VW
                    nc.scalar.activation(os_[0:rows, :], pv[c % 2][0:rows, :], ACT.Copy).then_inc(S("os"), 1)

                def head(h):
                    for n in range(N2 + AHEAD):
                        m = n - AHEAD
                        if m >= 0 and items2[m][1] == TC * (items2[m][0] + 1) - 1:
                            sums(h, items2[m][0])
                        if n >= N2:
                            continue
                        c, k = items2[n]
                        act.wait_ge(S("pass2"), N2 * h + n + 1)
                        act.wait_ge(S("pv"), N2 * h + n + 1)
                        lo = max(0, k - TC * c) * P
                        nc.scalar.activation(pt[:, n % 3, lo:CH], s2[n % B2][:, lo:CH], ACT.Exp,
                                             scale=SCALE).then_inc(S("exp"), 1)
                with act.Fori(0, NH // 2) as g:
                    head(2 * g)
                    head(2 * g + 1)

            @block.vector
            def _(dve):
                dve.wait_ge(S("vclean"), 5)
                dve.sem_inc(S("max"), B1)
                dve.sem_inc(S("os"), 2)
                dve.sem_inc(S("fin"), 1)
                dve.sem_inc(S("y"), 1)
                dve.sem_inc(S("pv"), 3)
                dve.sem_inc(S("shifted"), 1)

                def maxima(h, n):
                    i, k = items1[n]
                    width = min(CH, (i + 1) * P - k * CH)
                    dve.wait_ge(S("pass1"), N1 * h + n + 1)
                    nc.vector.tensor_reduce(most[:, i, k:k + 1], s1[n % B1][:, 0:width], AX.X, ALU.max).then_inc(S("max"), 1)

                def negate(h):
                    dve.wait_ge(S("max"), N1 * (h + 1) + B1)
                    nc.vector.tensor_reduce(negm[:, :], most[:, :, :], AX.X, ALU.max, negate=True).then_inc(S("negm"), 1)
                    dve.wait_ge(S("negm"), h + 1)

                def spread(h, g, s):
                    dve.wait_ge(S("nmt"), h + 1)
                    if s is not None:
                        dve.wait_ge(S(f"row{1 - s}"), 16 * (g + 1 if s else g))
                    o = InOrder(dve, S, h, {"split": 4})
                    o(nc.vector.tensor_copy(nmt[:, :], nm_ps), "nmt_here")
                    o(nc.vector.tensor_copy(nm3[:, 0, :], nmt[:, :]), "split")
                    o(nc.vector.tensor_tensor(nml[:, :], nmt[:, :], nm3[:, 0, :], ALU.subtract), "split")
                    o(nc.vector.tensor_copy(nm3[:, 1, :], nml[:, :]), "split")
                    nc.vector.tensor_tensor(nm3[:, 2, :], nml[:, :], nm3[:, 1, :], ALU.subtract).then_inc(S("nm3"), 1)
                    dve.wait_ge(S("nm3"), h + 1)
                    dve.sem_inc(S("split"), 1)

                def take_v(h, s, first):
                    if not first:
                        dve.wait_ge(S("pv"), N2 * (h - 1) + 3)
                    nc.vector.tensor_copy(vh[s][:, :, 0:D], vall[:, :, bass.ds(h * D, D)]).then_inc(S("vh"), 1)

                def divide(h, c):
                    dve.wait_ge(S("fin"), NC * h + c + 2)
                    nc.vector.reciprocal(den[:, :], fin[:, :, D]).then_inc(S("den"), 1)
                    dve.wait_ge(S("den"), NC * h + c + 1)
                    nc.vector.tensor_tensor(y[:, TC * c:TC * (c + 1), bass.ds(h * D, D)], fin[:, :, 0:D],
                                            den[:, :].unsqueeze(2).to_broadcast([P, TC, D]), ALU.mult).then_inc(S("y"), 1)
                    dve.wait_ge(S("y"), NC * h + c + 2)

                def head(h, g, s, more):
                    for n in range(N2 + AHEAD + 2):
                        if n < N2 and more:
                            for m in per1[n]:
                                maxima(h + 1, m)
                        if n == EARLY + 1 and more:
                            negate(h + 1)
                        if n == EARLY + 4 and more:
                            spread(h + 1, g, 1 - s) if s == 0 else spread(h + 1, g + 1, 0)
                        m = n - AHEAD - 2
                        if 0 <= m < N2 and items2[m][1] == TC * (items2[m][0] + 1) - 1:
                            divide(h, items2[m][0])
                    if more:
                        take_v(h + 1, 1 - s, False)

                for n in range(N1):
                    maxima(0, n)
                negate(0)
                spread(0, 0, None)
                take_v(0, 0, True)
                head(0, 0, 0, True)
                with dve.Fori(0, NH // 2 - 1) as g:
                    head(2 * g + 1, g, 1, True)
                    head(2 * g + 2, g + 1, 0, True)
                head(NH - 1, NH // 2 - 1, 1, False)

        with Stage(nc, "cao") as R:
            turned = s1
            z = [pv[n][:, :].rearrange("p (i f) -> p i f", f=P) for n in range(2)]
            yt = R.sb("yt", [P, 2, CH])
            xb = R.sb("xb", [P, NT, P])
            with nc.Block() as block:
                @block.tensor
                def _(pe):
                    def turn(c):
                        for i in range(TC):
                            mm = nc.tensor.transpose(turned[c % 2][:, i * P:(i + 1) * P], y[:, TC * c + i, :], ident[:, :])
                        mm.then_inc(R("turned"), 1)

                    turn(0)
                    for c in range(NC):
                        if c + 1 < NC:
                            if c:
                                pe.wait_ge(R("yt"), c)
                            turn(c + 1)
                        pe.wait_ge(R("yt"), c + 1)
                        if c >= 2:
                            pe.wait_ge(R("x"), c - 1)
                        for i in range(TC):
                            mm = nc.tensor.matmul(z[c % 2][:, i, :], yt[:, c % 2, i * P:(i + 1) * P], wproj[:, :],
                                                  start=True, stop=True)
                        mm.then_inc(R("z"), 1)

                @block.scalar
                def _(act):
                    for c in range(NC):
                        act.wait_ge(R("turned"), c + 1)
                        if c >= 2:
                            act.wait_ge(R("z"), c - 1)
                        nc.scalar.activation(yt[:, c % 2, :], turned[c % 2][:, :], ACT.Copy).then_inc(R("yt"), 1)

                @block.vector
                def _(dve):
                    o = InOrder(dve, R)
                    o(nc.vector.tensor_tensor(xb[:, :, :], X[:, :, :], bproj[:, :].unsqueeze(1).to_broadcast([P, NT, P]),
                                              ALU.add), "xb")
                    for c in range(NC):
                        dve.wait_ge(R("z"), c + 1)
                        o(nc.vector.tensor_tensor(X[:, TC * c:TC * (c + 1), :], z[c % 2],
                                                  xb[:, TC * c:TC * (c + 1), :], ALU.add), "x")


def delta_rule(nc, G, W):
    H, D = 4, 32
    C = P
    HALF = C // 2
    LEVELS = 6
    X, U, UT, ident, mhalf = G["X"], G["U"], G["UT"], G["ident"], G["mhalf"]
    with Stage(nc, "dr") as S:
        ww, wr = S.sb("ww", [P, P]), S.sb("wr", [P, P])
        dcol, drow, lalpha = S.sb("dcol", [P, 1]), S.sb("drow", [P, H]), S.sb("lalpha", [P, 1])
        dist, place, tail = S.sb("dist", [P, C]), S.sb("place", [P, C]), S.sb("tail", [P, H])
        steps = S.sb("steps", [P, LEVELS + 1, C])
        low0 = S.sb("low0", [P, C])
        hmask, blk = S.sb("hmask", [P, H]), S.sb("blk", [P, P])
        layernorm(nc, G, "drln", [
            (ww[:, :], W["dr_ww"]), (wr[:, :], W["dr_wr"]), (dcol[:, :], W["dr_dcol"]),
            (drow[:, :], W["dr_drow"].to_broadcast([P, H])), (lalpha[:, :], W["dr_lalpha"]),
            (dist[:, :], W["dr_dist"]), (place[:, :], W["dr_place"]), (tail[:, :], W["dr_tail"]),
            (steps[:, :, :], W["dr_steps"]), (low0[:, :], W["dr_low0"]),
            (hmask[:, :], W["dr_hmask"]), (blk[:, :], W["dr_blk"])], False)
        rkT = S.sb("rkT", [P, T + 1])
        pack = S.sb("pack", [P, NT, 3, P])
        v = S.sb("v", [P, NT, P])
        upper = S.sb("upper", [P, LEVELS + 1, H, C])
        lower = S.sb("lower", [P, H, C])
        gC = S.sb("gC", [P, 1])
        alpha = S.sb("alpha", [P, 1])
        with Stage(nc, "drp") as R:
            sq, rk = R.sb("sq", [P, NT, H, D]), R.sb("rk", [P, NT, H, D])
            ss, rn = R.sb("ss", [P, NT * H]), R.sb("rn", [P, NT * H])
            gcol, grow = R.sb("gcol", [P, 1]), R.sb("grow", [P, H])
            gp, gt, dec = R.sb("gp", [P, C]), R.sb("gt", [P, H]), R.sb("dec", [P, H, C])
            chunk = R.sb("chunk", [P, 1])
            ps = [R.ps(f"ps{n}", [P, TC, P]) for n in range(6)]
            with nc.Block() as block:
                @block.scalar
                def _(act):
                    nc.scalar.activation(gcol[:, :], dcol[:, :], ACT.Sigmoid).then_inc(R("gamma"), 1)
                    nc.scalar.activation(grow[:, :], drow[:, :], ACT.Sigmoid).then_inc(R("gamma"), 1)
                    nc.scalar.activation(alpha[:, :], lalpha[:, :], ACT.Exp).then_inc(R("alpha"), 1)
                    for c in range(NC):
                        act.wait_ge(R("v_ps"), c + 1)
                        nc.scalar.activation(v[:, TC * c:TC * (c + 1), :], ps[4 + c % 2][:, :, :], ACT.Copy).then_inc(R("v"), 1)

                @block.gpsimd
                def _(pool):
                    o = InOrder(pool, R)
                    o(pool.memset(chunk[:, :], float(HALF)), "const")
                    pool.wait_ge(R("ss"), 2)
                    o(pool.tensor_tensor(rn[:, :], ss[:, :], mhalf[:, 0:NT * H], ALU.pow), "rn")
                    pool.wait_ge(R("gamma"), 2)
                    o(pool.tensor_tensor(gp[:, :], gcol[:, :].to_broadcast([P, C]), place[:, :], ALU.pow), "gp")
                    o(pool.tensor_tensor(gt[:, :], grow[:, :], tail[:, :], ALU.pow), "gt")
                    o(pool.tensor_tensor(gC[:, :], gcol[:, :], chunk[:, :], ALU.pow), "gC")
                    for h in range(H):
                        o(pool.tensor_tensor(dec[:, h, :], grow[:, h:h + 1].to_broadcast([P, C]), dist[:, :], ALU.pow), "dec")

                @block.tensor
                def _(pe):
                    for c in range(NC):
                        if c >= 2:
                            pe.wait_ge(R("v"), c - 1)
                        for i in range(TC):
                            t = TC * c + i
                            mm = nc.tensor.matmul(ps[4 + c % 2][:, i, :], UT[:, t * P:(t + 1) * P], ww[:, :], start=True, stop=True)
                        mm.then_inc(R("v_ps"), 1)
                    pe.wait_ge(R("rk"), 1)
                    for c in range(NC):
                        for i in range(TC):
                            mm = nc.tensor.transpose(ps[c][:, i, :], rk[:, TC * c + i, :, :].rearrange("p h d -> p (h d)"),
                                                     ident[:, :])
                        mm.then_inc(R("rk_turned"), 1)
                    for c in range(NC):
                        pe.wait_ge(R("rkT"), c + 2)
                        for i in range(TC):
                            t = TC * c + i
                            mm = nc.tensor.transpose(ps[c][:, i, :], rkT[:, t * P:(t + 1) * P], ident[:, :])
                        mm.then_inc(R("wk_turned"), 1)

                @block.vector
                def _(dve):
                    o = InOrder(dve, R)
                    uh = U[:, :, :].rearrange("p t (h d) -> p t h d", h=H)
                    o(nc.vector.memset(rkT[:, 0:1], 0.0), "rkT")
                    o(nc.vector.tensor_tensor(sq[:, :, :, :], uh, uh, ALU.mult), "sq")
                    o(nc.vector.tensor_reduce(ss[:, :].rearrange("p (t h) -> p t h", h=H), sq[:, :, :, :], AX.X, ALU.add), "ss")
                    o(nc.vector.tensor_scalar(ss[:, :], ss[:, :], 1e-24, None, ALU.max), "ss")
                    dve.wait_ge(R("rn"), 1)
                    o(nc.vector.tensor_tensor(rk[:, :, :, :], uh, rn[:, :].rearrange("p (t h) -> p t h", h=H)
                                              .unsqueeze(3).to_broadcast([P, NT, H, D]), ALU.mult), "rk")
                    for c in range(NC):
                        dve.wait_ge(R("rk_turned"), c + 1)
                        o(nc.vector.tensor_copy(rkT[:, 1 + c * CH:1 + (c + 1) * CH],
                                                ps[c][:, :, :].rearrange("p i f -> p (i f)")), "rkT")
                    dve.wait_ge(R("gp"), 1)
                    o(nc.vector.tensor_tensor(pack[:, :, 2, :], rkT[:, 1:T + 1].rearrange("p (t i) -> p t i", i=C),
                                              gp[:, :].unsqueeze(1).to_broadcast([P, NT, C]), ALU.mult), "rkg")
                    dve.wait_ge(R("gt"), 1)
                    for c in range(NC):
                        dve.wait_ge(R("wk_turned"), c + 1)
                        o(nc.vector.tensor_copy(pack[:, TC * c:TC * (c + 1), 0, :], ps[c][:, :, :]), "wk")
                    for h in range(H):
                        o(nc.vector.tensor_scalar(pack[:, :, 1, h * D:(h + 1) * D], pack[:, :, 0, h * D:(h + 1) * D],
                                                  gt[:, h:h + 1], None, ALU.mult), "wkg")
                    dve.wait_ge(R("dec"), H)
                    for s in range(LEVELS + 1):
                        o(nc.vector.tensor_tensor(upper[:, s, :, :], dec[:, :, :],
                                                  steps[:, s, :].unsqueeze(1).to_broadcast([P, H, C]), ALU.mult), "upper")
                    o(nc.vector.tensor_tensor(lower[:, :, :], dec[:, :, :],
                                              low0[:, :].unsqueeze(1).to_broadcast([P, H, C]), ALU.mult), "lower")

        out = S.sb("out", [P, NT, P])
        with Stage(nc, "drr") as R:
            wkm = [R.sb(f"wkm{t}", [P, H, C]) for t in range(2)]
            mu = [R.sb(f"mu{t}", [P, LEVELS - 1, H, C]) for t in range(2)]
            x0, xt0 = R.sb("x0", [P, H, C]), R.sb("xt0", [P, H, C])
            intra = [R.sb(f"intra{t}", [P, H, C]) for t in range(2)]
            A = [R.sb(f"A{t}", [P, H, C]) for t in range(2)]
            AT = [R.sb(f"AT{t}", [P, H, C]) for t in range(2)]
            ma = [R.sb(f"ma{t}", [P, H, C]) for t in range(2)]
            pk = [R.sb(f"pk{t}", [P, 3, P]) for t in range(2)]
            nwk = [R.sb(f"nwk{t}", [P, C]) for t in range(2)]
            av = [R.sb(f"av{t}", [P, P]) for t in range(2)]
            vn = [R.sb(f"vn{t}", [P, P]) for t in range(2)]
            state, ds = R.sb("state", [P, P]), R.sb("ds", [P, P])
            gram = R.ps("gram", [P, H, 256])
            pma = [R.ps(f"pma{t}", [P, H, C]) for t in range(2)]
            pa = [R.ps(f"pa{t}", [P, H, C]) for t in range(2)]
            pat = [R.ps(f"pat{t}", [P, H, C]) for t in range(2)]
            G_WIDTH = C + 1
            with nc.Block() as block:
                @block.gpsimd
                def _(pool):
                    pool.sem_inc(R("gram"), 2)
                    with pool.Fori(0, NT // 2) as g:
                        for t in range(2):
                            pool.wait_ge(R("gram"), 2 * g + t + 1)
                            pool.tensor_tensor(wkm[t][:, :, :],
                                               rkT[:, bass.ds(2 * g * C + t * C, C)].unsqueeze(1).to_broadcast([P, H, C]),
                                               hmask[:, :].unsqueeze(2).to_broadcast([P, H, C]), ALU.mult).then_inc(R("wkm"), 1)

                @block.tensor
                def _(pe):
                    with pe.Fori(0, NT // 2) as g:
                        for t in range(2):
                            pe.wait_ge(R("wkm"), 2 * g + t + 1)
                            pe.wait_ge(R("gram_read"), 2 * g + t + 1)
                            if t == 0:
                                pe.wait_ge(R("state"), 4 * g + 1)
                            for h in range(H):
                                mm = nc.tensor.matmul(gram[:, h, 0:G_WIDTH], wkm[t][:, h, :],
                                                      rkT[:, bass.ds(2 * g * C + t * C, G_WIDTH)], start=True, stop=True)
                            mm.then_inc(R("gram"), 1)
                        for s in range(1, LEVELS):
                            for t in range(2):
                                pe.wait_ge(R("AT"), 2 * LEVELS * g + 2 * (s - 1) + t + 1)
                                if s == 1:
                                    pe.wait_ge(R("out"), 2 * g + t + 1)
                                for h in range(H):
                                    mm = nc.tensor.matmul(pma[t][:, h, :], mu[t][:, s - 1, h, :], A[t][:, h, :],
                                                          start=True, stop=True)
                                mm.then_inc(R("pma"), 1)
                            for t in range(2):
                                pe.wait_ge(R("ma"), 2 * (LEVELS - 1) * g + 2 * (s - 1) + t + 1)
                                if s < LEVELS - 1:
                                    for h in range(H):
                                        mm = nc.tensor.matmul(pa[t][:, h, :], AT[t][:, h, :], ma[t][:, h, :],
                                                              start=True, stop=True)
                                    mm.then_inc(R("pa"), 1)
                                for h in range(H):
                                    mm = nc.tensor.matmul(pat[t][:, h, :], ma[t][:, h, :], AT[t][:, h, :],
                                                          start=True, stop=True)
                                mm.then_inc(R("pat"), 1)
                        for t in range(2):
                            pe.wait_ge(R("AT"), 2 * LEVELS * g + 2 * (LEVELS - 1) + t + 1)
                            pe.wait_ge(R("pk"), 2 * g + t + 1)
                            for h in range(H):
                                mm = nc.tensor.matmul(pma[t][h * D:(h + 1) * D, 0, :], pk[t][:, 0, h * D:(h + 1) * D],
                                                      AT[t][:, h, :], start=True, stop=True)
                            mm.then_inc(R("wk_ps"), 1)
                            for h in range(H):
                                mm = nc.tensor.matmul(pa[t][:, 0, h * D:(h + 1) * D], AT[t][:, h, :],
                                                      v[:, bass.ds(2 * g + t, 1), h * D:(h + 1) * D],
                                                      start=True, stop=True)
                            mm.then_inc(R("av_ps"), 1)
                        for t in range(2):
                            pe.wait_ge(R("nwk"), 2 * g + t + 1)
                            for q in range(2):
                                lo, hi = q * HALF, (q + 1) * HALF
                                pe.wait_ge(R("state"), 4 * g + 2 * t + q + 1)
                                nc.tensor.matmul(pat[t][lo:hi, 1, :], nwk[t][:, lo:hi], state[:, :], start=True,
                                                 stop=True).then_inc(R("ws_ps"), 1)
                                nc.tensor.matmul(pma[t][lo:hi, 0, :], pk[t][:, 2, lo:hi], state[:, :], start=True, stop=False)
                                pe.wait_ge(R("vn"), 4 * g + 2 * t + q + 1)
                                nc.tensor.matmul(gram[:, 2 * q, 0:P], pk[t][lo:hi, 1, :], vn[t][lo:hi, :], start=True,
                                                 stop=True).then_inc(R("ds_ps"), 1)
                            for h in range(H):
                                mm = nc.tensor.matmul(pma[t][:, 0, h * D:(h + 1) * D], intra[t][:, h, :],
                                                      vn[t][:, h * D:(h + 1) * D], start=False, stop=h == H - 1)
                            mm.then_inc(R("out_ps"), 1)

                @block.scalar
                def _(act):
                    with act.Fori(0, NT // 2) as g:
                        for t in range(2):
                            act.wait_ge(R("out_ps"), 2 * g + t + 1)
                            nc.scalar.activation(pk[t][:, :, :], pack[:, bass.ds(2 * g + t, 1), :, :], ACT.Copy).then_inc(R("pk"), 1)
                        for s in range(1, LEVELS):
                            for t in range(2):
                                act.wait_ge(R("pma"), 2 * (LEVELS - 1) * g + 2 * (s - 1) + t + 1)
                                nc.scalar.activation(ma[t][:, :, :], pma[t][:, :, :], ACT.Copy).then_inc(R("ma"), 1)
                        for t in range(2):
                            act.wait_ge(R("wk_ps"), 2 * g + t + 1)
                            nc.scalar.activation(nwk[t][:, :], pma[t][:, 0, :], ACT.Copy, scale=-1.0).then_inc(R("nwk"), 1)
                        for t in range(2):
                            act.wait_ge(R("out_ps"), 2 * g + t + 3)
                            nc.scalar.activation(out[:, bass.ds(2 * g + t, 1), :], pma[t][:, 0:1, :], ACT.Copy).then_inc(R("out"), 1)

                @block.vector
                def _(dve):
                    dve.sem_inc(R("gram_read"), 1)
                    dve.sem_inc(R("out_ps"), 2)
                    dve.sem_inc(R("out"), 2)
                    nc.vector.memset(state[:, :], 0.0).then_inc(R("state"), 1)
                    with dve.Fori(0, NT // 2) as g:
                        o = InOrder(dve, R, g, {"mu": 2, "intra": 2, "gram_read": 2, "x0": 2, "A": 2 * (LEVELS - 1),
                                                "AT": 2 * LEVELS, "av": 2, "vn": 4, "ds": 4, "state": 4},
                                    {"gram_read": 1, "state": 1})
                        for t in range(2):
                            dve.wait_ge(R("out_ps"), 2 * g + t + 1)
                            dve.wait_ge(R("gram"), 2 * g + t + 3)
                            wk = gram[:, :, 0:C]
                            for s in range(1, LEVELS):
                                ins = nc.vector.tensor_tensor(mu[t][:, s - 1, :, :], wk, upper[:, s, :, :], ALU.mult)
                            o(ins, "mu")
                            o(nc.vector.tensor_tensor(intra[t][:, :, :], gram[:, :, 1:G_WIDTH], upper[:, LEVELS, :, :],
                                                      ALU.mult), "intra")
                            o(nc.vector.tensor_tensor(x0[:, :, :], wk, lower[:, :, :], ALU.mult), "x0")
                            o(nc.vector.tensor_tensor(xt0[:, :, :], wk, upper[:, 0, :, :], ALU.mult), "gram_read")
                            one = ident[:, :].unsqueeze(1).to_broadcast([P, H, C])
                            o(nc.vector.tensor_tensor(A[t][:, :, :], one, x0[:, :, :], ALU.subtract), "A")
                            o(nc.vector.tensor_tensor(AT[t][:, :, :], one, xt0[:, :, :], ALU.subtract), "AT")
                        for s in range(1, LEVELS):
                            for t in range(2):
                                if s < LEVELS - 1:
                                    dve.wait_ge(R("pa"), 2 * (LEVELS - 2) * g + 2 * (s - 1) + t + 1)
                                    o(nc.vector.tensor_tensor(A[t][:, :, :], A[t][:, :, :], pa[t][:, :, :], ALU.subtract), "A")
                                dve.wait_ge(R("pat"), 2 * (LEVELS - 1) * g + 2 * (s - 1) + t + 1)
                                o(nc.vector.tensor_tensor(AT[t][:, :, :], AT[t][:, :, :], pat[t][:, :, :], ALU.subtract), "AT")
                        for t in range(2):
                            dve.wait_ge(R("av_ps"), 2 * g + t + 1)
                            o(nc.vector.tensor_copy(av[t][:, :], pa[t][:, 0, :]), "av")
                        for t in range(2):
                            for q in range(2):
                                lo, hi = q * HALF, (q + 1) * HALF
                                dve.wait_ge(R("ws_ps"), 4 * g + 2 * t + q + 1)
                                o(nc.vector.tensor_tensor(vn[t][lo:hi, :], pat[t][lo:hi, 1, :], av[t][lo:hi, :], ALU.add), "vn")
                                dve.wait_ge(R("ds_ps"), 4 * g + 2 * t + q + 1)
                                o(nc.vector.tensor_tensor(ds[:, :], gram[:, 2 * q, 0:P], blk[:, :], ALU.mult), "ds")
                                o(nc.vector.scalar_tensor_tensor(out=state[:, :], in0=state[:, :], scalar=gC[:, 0:1],
                                                                 in1=ds[:, :], op0=ALU.mult, op1=ALU.add), "state")

        with Stage(nc, "dro") as R:
            turned = [R.ps(f"turned{n}", [P, CH]) for n in range(2)]
            z = [R.ps(f"z{n}", [P, TC, P]) for n in range(2)]
            ot = R.sb("ot", [P, 2, CH])
            xu = R.sb("xu", [P, NT, P])
            with nc.Block() as block:
                @block.tensor
                def _(pe):
                    def turn(c):
                        for i in range(TC):
                            mm = nc.tensor.transpose(turned[c % 2][:, i * P:(i + 1) * P], out[:, TC * c + i, :], ident[:, :])
                        mm.then_inc(R("turned"), 1)

                    turn(0)
                    for c in range(NC):
                        if c + 1 < NC:
                            if c:
                                pe.wait_ge(R("ot"), c)
                            turn(c + 1)
                        pe.wait_ge(R("ot"), c + 1)
                        if c >= 2:
                            pe.wait_ge(R("x"), c - 1)
                        for i in range(TC):
                            mm = nc.tensor.matmul(z[c % 2][:, i, :], ot[:, c % 2, i * P:(i + 1) * P], wr[:, :],
                                                  start=True, stop=True)
                        mm.then_inc(R("z"), 1)

                @block.scalar
                def _(act):
                    for c in range(NC):
                        act.wait_ge(R("turned"), c + 1)
                        if c >= 2:
                            act.wait_ge(R("z"), c - 1)
                        nc.scalar.activation(ot[:, c % 2, :], turned[c % 2][:, :], ACT.Copy,
                                             scale=alpha[:, 0:1]).then_inc(R("ot"), 1)

                @block.vector
                def _(dve):
                    o = InOrder(dve, R)
                    o(nc.vector.tensor_tensor(xu[:, :, :], X[:, :, :], U[:, :, :], ALU.add), "xu")
                    for c in range(NC):
                        dve.wait_ge(R("z"), c + 1)
                        o(nc.vector.tensor_tensor(X[:, TC * c:TC * (c + 1), :], z[c % 2][:, :, :],
                                                  xu[:, TC * c:TC * (c + 1), :], ALU.add), "x")


def bilinear_attention(nc, G, W):
    NH, D = 16, 64
    PAIRS = NH // 2
    UQ = 2
    NU = NT // UQ
    NG = NT // 2
    SCALE = D ** -0.5
    X, UT, ident, v = G["X"], G["UT"], G["ident"], G["U"]
    STQ = ((0, 1), (2, 0))
    STK = ((0, 0), (1, 1), (0, 2))
    PASSES = ((0, 0), (0, 1), (1, 2))
    with Stage(nc, "ba") as S:
        gain = S.sb("gain", [P, 1])
        cos, sin = S.sb("cos", [P, T]), S.sb("sin", [P, T])
        wo = S.sb("wo", [P, NH, P])
        wp = S.sb("wp", [P, 6, P])
        layernorm(nc, G, "baln", [
            (gain[:, :], W["ba_gain"]), (cos[:, :], W["ba_cos"]), (sin[:, :], W["ba_sin"]),
            (wo[:, :, :], W["ba_wo"]), (wp[:, :, :], W["ba_w"][0])], True, gain=gain[:, 0:1])
        rot = S.sb("rot", [P, 2, CH])
        qf, kf = S.sb("qf", [P, 2, CH]), S.sb("kf", [P, 2, CH])
        left = S.sb("left", [P, 2, CH])
        parts = S.sb("parts", [P, 2, 3, T], BF16)
        sq = S.sb("sq", [P, 2, 2, T], BF16)
        sk = S.sb("sk", [P, 2, 3, T], BF16)
        pb = [S.sb(f"pb{n}", [P, UQ, T]) for n in range(2)]
        pt = S.sb("pt", [P, 4, CH])
        osb = S.sb("osb", [P, UQ * P])
        most, nm = S.sb("most", [P, 2]), S.sb("nm", [P, 2])
        scale = S.sb("scale", [P, 1])
        rs = S.sb("rs", [P, 2, UQ, 2])
        rsum, rinv = S.sb("rsum", [P, UQ]), S.sb("rinv", [P, UQ])
        sc = S.ps("sc", [P, 4, CH])
        tr = [S.ps(f"tr{n}", [P, CH]) for n in range(2)]
        ops = S.ps("ops", [P, CH])
        yps = S.ps("yps", [P, CH])
        PROJ = 4
        with nc.Block() as block:
            @block.sync
            def _(sp):
                def stacks():
                    for hh in range(2):
                        rows = slice(hh * D, (hh + 1) * D)
                        for n in range(2):
                            for half in range(2):
                                sp.dma_start(sq[half * D:(half + 1) * D, hh, n, :],
                                             parts[rows, 0, STQ[n][half], :]).then_inc(S("stack"), 16)
                        for n in range(3):
                            for half in range(2):
                                sp.dma_start(sk[half * D:(half + 1) * D, hh, n, :],
                                             parts[rows, 1, STK[n][half], :]).then_inc(S("stack"), 16)

                with sp.Fori(0, PAIRS - 1) as p:
                    sp.wait_ge(S("projected"), p + 1)
                    sp.sem_inc(S("paced"), 1)
                    sp.dma_start(wp[:, :, :], W["ba_w"][p + 1]).then_inc(S("weights"), 16)
                    sp.wait_ge(S("split"), p + 1)
                    stacks()
                sp.wait_ge(S("split"), PAIRS)
                stacks()

            @block.tensor
            def _(pe):
                def projections(p):
                    for c in range(NC):
                        rhs = UT[:, c * CH:(c + 1) * CH]
                        for n in range(PROJ):
                            pe.wait_ge(S("rotated"), PROJ * NC * p + PROJ * c + n + 1)
                            nc.tensor.matmul(sc[:, n, :], wp[:, n, :], rhs, start=True, stop=True).then_inc(S("proj"), 1)
                        pe.wait_ge(S("v"), NC * p + c + 1)
                        bank = (ops, yps)[c % 2]
                        for i in range(TC):
                            t = TC * c + i
                            mm = nc.tensor.matmul(bank[:, i * P:(i + 1) * P], UT[:, t * P:(t + 1) * P], wp[:, 4, :],
                                                  start=True, stop=True)
                        mm.then_inc(S("v_ps"), 1)
                        pe.wait_ge(S("kf"), NC * p + c + 1)
                        pe.wait_ge(S("kl"), NC * p + c + 1)
                        mm = nc.tensor.matmul(tr[c % 2][:, :], wp[:, 5, :], kf[:, c % 2, :], start=True, stop=True)
                        mm.then_inc(S("kt"), 1)

                def scores(un, hh, u, t, half):
                    for c in (2 * half, 2 * half + 1):
                        if c % 2 == 0:
                            pe.wait_ge(S("exp"), 4 * un + 2 * t + half + 1)
                        for n, (a, b) in enumerate(PASSES):
                            mm = nc.tensor.matmul(sc[:, c, :], sq[:, hh, a, bass.ds(u * UQ * P + t * P, P)],
                                                  sk[:, hh, b, c * CH:(c + 1) * CH], start=n == 0, stop=n == 2)
                        if c % 2:
                            mm.then_inc(S("scores"), 1)

                def turn(un, par, g):
                    if g == 0:
                        pe.wait_ge(S("exp"), 4 * un + 6)
                    pe.wait_ge(S("pt_act" if g % 2 == 0 else "pt_dve"), 4 * un + g // 2 + 1)
                    for k in range(2):
                        for t in range(UQ):
                            mm = nc.tensor.transpose(tr[g % 2][:, (2 * k + t) * P:(2 * k + t + 1) * P],
                                                     pb[par][:, t, (2 * g + k) * P:(2 * g + k + 1) * P], ident[:, :])
                    mm.then_inc(S("turned"), 1)

                def values(un, hh, g):
                    if g == 0:
                        pe.wait_ge(S("osb"), un + 1)
                    pe.wait_ge(S("pt_act" if g % 2 == 0 else "pt_dve"), 4 * un + g // 2 + 2)
                    for k in range(2):
                        mm = nc.tensor.matmul(ops[k * D:(k + 1) * D, 0:UQ * P], v[:, 2 * g + k, hh * D:(hh + 1) * D],
                                              pt[:, g % 4, k * UQ * P:(k + 1) * UQ * P], start=g == 0, stop=g == NG - 1)
                    mm.then_inc(S("values"), 1)

                def output(un, head):
                    pe.wait_ge(S("osb"), un + 2)
                    pe.wait_ge(S("x"), UQ * un + 2)
                    for t in range(UQ):
                        mm = nc.tensor.matmul(yps[:, t * P:(t + 1) * P], osb[:, t * P:(t + 1) * P],
                                              wo[:, bass.ds(head, 1), :], start=True, stop=True)
                    mm.then_inc(S("y"), 1)

                def step(now, before, last):
                    for t in range(UQ):
                        a = NG // 2 * t
                        if now:
                            scores(*now, t, 0)
                        if before:
                            un, hh, par = before
                            turn(un, par, a)
                            turn(un, par, a + 1)
                        if now:
                            scores(*now, t, 1)
                        if last and t == 0:
                            output(*last)
                        if before:
                            values(un, hh, a)
                            turn(un, par, a + 2)
                            values(un, hh, a + 1)
                            turn(un, par, a + 3)
                            values(un, hh, a + 2)
                            values(un, hh, a + 3)

                with pe.Fori(0, PAIRS) as p:
                    pe.wait_ge(S("weights"), 16 * p + 16)
                    projections(p)
                    pe.drain().then_inc(S("projected"), 1)
                    pe.wait_ge(S("stack"), 16 * 20 * (p + 1))
                    for hh in range(2):
                        base, head = 2 * NU * p + NU * hh, 2 * p + hh
                        step((base, hh, 0), (base - 1, 0, 1) if hh else None, (base - 2, head - 1) if hh else None)
                        step((base + 1, hh, 1), (base, hh, 0), (base - 1, head - 1) if hh else None)
                        with pe.Fori(0, NU // 2 - 1) as w:
                            step((base + 2 * w + 2, hh, 2 * w + 2), (base + 2 * w + 1, hh, 1), (base + 2 * w, head))
                            step((base + 2 * w + 3, hh, 2 * w + 3), (base + 2 * w + 2, hh, 0), (base + 2 * w + 1, head))
                    step(None, (base + NU - 1, 1, 1), (base + NU - 2, head))
                    output(base + NU - 1, head)

            @block.scalar
            def _(act):
                nc.scalar.activation(scale[:, :], gain[:, :], ACT.Exp).then_inc(S("table"), 1)
                act.sem_inc(S("exp"), 2)
                act.sem_inc(S("pt_act"), 1)

                def projections(p):
                    for c in range(NC):
                        act.wait_ge(S("v_ps"), NC * p + c + 1)
                        nc.scalar.activation(v[:, TC * c:TC * (c + 1), :],
                                             (ops, yps)[c % 2][:, :].rearrange("p (i f) -> p i f", f=P),
                                             ACT.Copy).then_inc(S("v"), 1)
                        cols = slice(c * CH, (c + 1) * CH)
                        act.wait_ge(S("qf"), NC * p + c + 1)
                        nc.scalar.activation(parts[:, 0, 0, cols], qf[:, c % 2, :], ACT.Copy).then_inc(S("qh"), 1)
                        act.wait_ge(S("kt"), NC * p + c + 1)
                        nc.scalar.activation(parts[:, 1, 0, cols], tr[c % 2][:, :], ACT.Copy).then_inc(S("kh"), 1)
                        act.wait_ge(S("qleft"), NC * p + c + 1)
                        nc.scalar.activation(parts[:, 0, 1, cols], left[:, 0, :], ACT.Copy).then_inc(S("qm"), 1)
                        act.wait_ge(S("kleft"), NC * p + c + 1)
                        nc.scalar.activation(parts[:, 1, 1, cols], left[:, 1, :], ACT.Copy).then_inc(S("km"), 1)

                def exponentials(un, par, t):
                    act.wait_ge(S("nm"), UQ * un + t + 1)
                    if t == 0:
                        act.wait_ge(S("turned"), NG * un + 1)
                    for half in range(2):
                        nc.scalar.activation(pb[par][:, t, half * 1024:(half + 1) * 1024],
                                             sc[:, 2 * half:2 * half + 2, :].rearrange("p a b -> p (a b)"), ACT.Exp,
                                             bias=nm[:, t:t + 1], scale=SCALE,
                                             accum_out=rs[:, par, t, half:half + 1]).then_inc(S("exp"), 1)

                def copies(un, g):
                    act.wait_ge(S("turned"), NG * un + g + 10)
                    act.wait_ge(S("values"), NG * un + g + 1)
                    nc.scalar.activation(pt[:, g % 4, :], tr[g % 2][:, :], ACT.Copy).then_inc(S("pt_act"), 1)

                def step(now, before):
                    for t in range(UQ):
                        if before is not None:
                            copies(before, NG // 2 * t)
                            copies(before, NG // 2 * t + 2)
                        if now:
                            exponentials(*now, t)
                    if before is not None:
                        act.wait_ge(S("values"), NG * before + NG + 4)
                        act.wait_ge(S("y"), before + 1)
                        nc.scalar.activation(osb[:, :], ops[:, 0:UQ * P], ACT.Copy).then_inc(S("osb"), 1)

                with act.Fori(0, PAIRS) as p:
                    projections(p)
                    for hh in range(2):
                        base = 2 * NU * p + NU * hh
                        step((base, 0), base - 1 if hh else None)
                        step((base + 1, 1), base)
                        with act.Fori(0, NU // 2 - 1) as w:
                            step((base + 2 * w + 2, 0), base + 2 * w + 1)
                            step((base + 2 * w + 3, 1), base + 2 * w + 2)
                    step(None, base + NU - 1)

            @block.vector
            def _(dve):
                dve.sem_inc(S("rotated"), PROJ)
                dve.sem_inc(S("v"), 2)
                dve.sem_inc(S("kl"), 2)
                dve.sem_inc(S("turned"), NG + 1)
                dve.sem_inc(S("values"), 4)
                dve.sem_inc(S("pt_dve"), 1)
                dve.sem_inc(S("osb"), 1)
                dve.sem_inc(S("y"), 1)
                dve.sem_inc(S("x"), 2)
                dve.sem_inc(S("weights"), 16)

                def projections(p):
                    o = InOrder(dve, S, p, {n: NC for n in ("qf", "kf", "qleft", "kleft", "ql", "kl")}
                                | {"rotated": PROJ * NC}, {"rotated": PROJ, "kl": 2})
                    for c in range(NC + 1):
                        if c < NC:
                            cols = slice(c * CH, (c + 1) * CH)
                            for n in range(PROJ):
                                dve.wait_ge(S("proj"), PROJ * NC * p + PROJ * c + n + 1)
                                o(nc.vector.tensor_tensor(rot[:, n % 2, :], sc[:, n, :], (cos, sin)[n % 2][:, cols],
                                                          ALU.mult), "rotated")
                                if n % 2:
                                    o(nc.vector.tensor_tensor((qf, kf)[n // 2][:, c % 2, :], rot[:, 0, :], rot[:, 1, :],
                                                              ALU.add), ("qf", "kf")[n // 2])
                        if c:
                            m = c - 1
                            cols = slice(m * CH, (m + 1) * CH)
                            for n, (src, a) in enumerate(((qf[:, m % 2, :], "qh"), (tr[m % 2][:, :], "kh"))):
                                dve.wait_ge(S(a), NC * p + m + 1)
                                o(nc.vector.tensor_tensor(left[:, n, :], src, parts[:, n, 0, cols], ALU.subtract),
                                  ("qleft", "kleft")[n])
                            for n, b in enumerate(("qm", "km")):
                                dve.wait_ge(S(b), NC * p + m + 1)
                                o(nc.vector.tensor_tensor(parts[:, n, 2, cols], left[:, n, :], parts[:, n, 1, cols],
                                                          ALU.subtract), ("ql", "kl")[n])
                    dve.sem_inc(S("split"), 1)

                def maximum(un, t, half):
                    dve.wait_ge(S("scores"), 4 * un + 2 * t + half + 1)
                    nc.vector.tensor_reduce(most[:, half:half + 1], sc[:, 2 * half:2 * half + 2, :], AX.XY,
                                            ALU.max).then_inc(S("most"), 1)

                def bias(un, t):
                    dve.wait_ge(S("most"), 4 * un + 2 * t + 2)
                    nc.vector.scalar_tensor_tensor(out=nm[:, t:t + 1], in0=most[:, 0:1], scalar=most[:, 1:2],
                                                   in1=scale[:, :], op0=ALU.max, op1=ALU.mult).then_inc(S("nm"), 1)
                    dve.wait_ge(S("nm"), UQ * un + t + 1)
                    dve.sem_inc(S("paced_dve"), 1)

                def copies(un, g):
                    dve.wait_ge(S("turned"), NG * un + g + 10)
                    dve.wait_ge(S("values"), NG * un + g + 1)
                    nc.vector.tensor_copy(pt[:, g % 4, :], tr[g % 2][:, :]).then_inc(S("pt_dve"), 1)

                def inverse(un, par):
                    dve.wait_ge(S("exp"), 4 * un + 6)
                    o = InOrder(dve, S, un)
                    o(nc.vector.tensor_tensor(rsum[:, :], rs[:, par, :, 0], rs[:, par, :, 1], ALU.add), "rsum")
                    o(nc.vector.reciprocal(rinv[:, :], rsum[:, :]), "rinv")
                    dve.sem_inc(S("paced_dve"), 1)

                def add(un, u):
                    dve.wait_ge(S("y"), un + 2)
                    for t in range(UQ):
                        tile = X[:, bass.ds(UQ * u + t, 1), :]
                        nc.vector.scalar_tensor_tensor(out=tile, in0=yps[:, t * P:(t + 1) * P].unsqueeze(1),
                                                       scalar=rinv[:, t:t + 1], in1=tile, op0=ALU.mult,
                                                       op1=ALU.add).then_inc(S("x"), 1)
                    dve.wait_ge(S("x"), UQ * un + UQ + 2)
                    dve.sem_inc(S("paced_dve"), 1)

                def step(now, before, last):
                    for t in range(UQ):
                        a = NG // 2 * t
                        if now is not None:
                            maximum(now, t, 0)
                        if before:
                            copies(before[0], a + 1)
                        if now is not None:
                            maximum(now, t, 1)
                            bias(now, t)
                        if before:
                            copies(before[0], a + 3)
                    if last:
                        add(*last)
                    if before:
                        inverse(*before)

                dve.wait_ge(S("table"), 1)
                nc.vector.memset(scale[:, :], -SCALE).then_inc(S("const"), 1)
                dve.wait_ge(S("const"), 1)
                with dve.Fori(0, PAIRS) as p:
                    projections(p)
                    for hh in range(2):
                        base = 2 * NU * p + NU * hh
                        step(base, (base - 1, 1) if hh else None, (base - 2, NU - 2) if hh else None)
                        step(base + 1, (base, 0), (base - 1, NU - 1) if hh else None)
                        with dve.Fori(0, NU // 2 - 1) as w:
                            step(base + 2 * w + 2, (base + 2 * w + 1, 1), (base + 2 * w, 2 * w))
                            step(base + 2 * w + 3, (base + 2 * w + 2, 0), (base + 2 * w + 1, 2 * w + 1))
                    step(None, (base + NU - 1, 1), (base + NU - 2, NU - 2))
                    add(base + NU - 1, NU - 1)


def program(nc, W, out, first, last):
    with ExitStack() as stack:
        def sb(name, shape, dt=F32):
            return stack.enter_context(nc.sbuf_tensor(name, shape, dt))

        G = {"X": sb("X", [P, NT, P]), "U": sb("U", [P, NT, P]), "UT": sb("UT", [P, T]),
             "ident": sb("ident", [P, P]), "identb": sb("identb", [P, P], BF16), "mhalf": sb("mhalf", [P, NT * 4]),
             "w1": sb("w1", [P, 4 * P]), "w2": sb("w2", [P, 4, P]), "b1": sb("b1", [P, 4]), "hb2": sb("hb2", [P, P]),
             "ffn_gain": sb("ffn_gain", [P, 1]), "ffn_shift": sb("ffn_shift", [P, 1])}
        x_view = W["x"].rearrange("(i p) f -> p i f", p=P)
        out_view = out.rearrange("(i p) f -> p i f", p=P)
        with Stage(nc, "start") as S:
            with nc.Block() as block:
                @block.sync
                def _(sp):
                    sp.dma_start(G["X"][:, :, :], x_view).then_inc(S("here"), 16)
                    sp.dma_start(G["ident"][:, :], W["ident"]).then_inc(S("ident"), 16)
                    sp.dma_start(G["ffn_gain"][:, :], W["ffn_gain"]).then_inc(S("here"), 16)
                    sp.dma_start(G["ffn_shift"][:, :], W["ffn_shift"]).then_inc(S("here"), 16)
                    sp.wait_ge(S("here"), 48)

                @block.gpsimd
                def _(pool):
                    pool.memset(G["mhalf"][:, :], -0.5).then_inc(S("half"), 1)

                @block.vector
                def _(dve):
                    dve.wait_ge(S("ident"), 16)
                    nc.vector.tensor_copy(G["identb"][:, :], G["ident"][:, :]).then_inc(S("identb"), 1)
        stages = [
            lambda: linear_attention(nc, G, W),
            lambda: ffn(nc, G, W, "f1", True),
            lambda: delta_rule(nc, G, W),
            lambda: ffn(nc, G, W, "f2", first == 4),
            lambda: causal_attention(nc, G, W),
            lambda: experts(nc, G, W, "m1"),
            lambda: bilinear_attention(nc, G, W),
            lambda: experts(nc, G, W, "m2"),
        ]
        for stage in stages[first - 1:last]:
            stage()
        with Stage(nc, "end") as S:
            with nc.Block() as block:
                @block.sync
                def _(sp):
                    sp.dma_start(out_view, G["X"][:, :, :]).then_inc(S("stored"), 16)
                    sp.wait_ge(S("stored"), 16)


FIRST, LAST = 1, 8


def _rotation(np, n_dim, halves):
    inv = (np.float32(1.0) / np.float32(10000.0) ** (np.arange(0, n_dim, 2, dtype=np.float32) / np.float32(n_dim))).astype(np.float32)
    freqs = np.arange(T, dtype=np.float32)[:, None] * inv[None, :]
    emb = np.concatenate([freqs, freqs], axis=-1)
    sign = np.where(np.arange(n_dim) < n_dim // 2, -1.0, 1.0) if halves else np.where(np.arange(n_dim) % 2 == 0, -1.0, 1.0)
    reps = P // n_dim
    cos = np.tile(np.cos(emb).T, (reps, 1)).astype(np.float32)
    sin = np.tile((np.sin(emb) * sign).T, (reps, 1)).astype(np.float32)
    return cos, sin


def _lay_out(np, a):
    W = {}

    def put(name, x):
        W[name] = np.ascontiguousarray(x)

    put("x", a["L0_attn_a_x"].reshape(T, P))
    put("ident", np.eye(P, dtype=np.float32))
    feature = np.arange(P)
    half_swap = (feature // 8) * 8 + (feature % 8 + 4) % 8
    put("la_wqk", np.stack([a["L0_attn_a_Wq"].T, a["L0_attn_a_Wq"][half_swap].T,
                            a["L0_attn_a_Wk"].T, a["L0_attn_a_Wk"][half_swap].T], axis=1))
    put("la_wv", np.stack([a["L0_attn_a_Wv"][(feature // 8) * 8 + e].T for e in range(8)], axis=1))
    put("la_wb", a["L0_attn_a_Wb"][feature // 8].T)
    put("la_bb", a["L0_attn_a_bb"][feature // 8].reshape(P, 1))
    put("la_wo", a["L0_attn_a_Wo"].T)
    put("la_bo", a["L0_attn_a_bo"].reshape(1, P))
    put("la_scale", a["L0_attn_a_scale"].reshape(1, P))
    cos, sin = _rotation(np, 8, True)
    put("la_cos", cos)
    put("la_sin", sin)
    same_head = (feature[:, None] // 8 == feature[None, :] // 8)
    pick = [same_head & (feature[None, :] % 8 == e) for e in range(8)] + [same_head]
    put("la_pick", np.stack(pick, axis=1).astype(np.float32))
    put("ffn_gain", a["L0_ffn_ln_gamma"].reshape(P, 1))
    put("ffn_shift", a["L0_ffn_ln_beta"].reshape(P, 1))
    put("fc1_q", a["L0_ffn_fc1_q"])
    put("fc1_scales", a["L0_ffn_fc1_scales"].reshape(1, -1))
    put("fc1_bias", a["L0_ffn_fc1_bias"].reshape(4, P).T)
    put("fc2_q", a["L0_ffn_fc2_q"])
    put("fc2_scales", a["L0_ffn_fc2_scales"])
    put("fc2_bias", a["L0_ffn_fc2_bias"].reshape(1, P))
    put("dr_ww", a["L0_attn_b_Ww"].T)
    put("dr_wr", a["L0_attn_b_Wr"].T)
    put("dr_dcol", np.repeat(a["L0_attn_b_decay"], 32).reshape(P, 1))
    put("dr_drow", a["L0_attn_b_decay"].reshape(1, 4))
    put("dr_lalpha", np.repeat(a["L0_attn_b_log_alpha"], 32).reshape(P, 1))
    row, col = np.arange(P)[:, None], np.arange(P)[None, :]
    put("dr_dist", np.abs(row - col).astype(np.float32))
    put("dr_place", (col % 64 + 0 * row).astype(np.float32))
    put("dr_tail", (63 - row % 64 + np.zeros((1, 4))).astype(np.float32))
    halves = [(row // (2 * b) == col // (2 * b)) & (row // b != col // b) for b in (1, 2, 4, 8, 16, 32)]
    put("dr_steps", np.stack([m & (col > row) for m in halves] + [(col > row) & (row // 64 == col // 64)], axis=1).astype(np.float32))
    put("dr_low0", (halves[0] & (row > col)).astype(np.float32))
    put("dr_hmask", (row // 32 == np.arange(4)[None, :]).astype(np.float32))
    put("dr_blk", (row // 32 == col // 32).astype(np.float32))
    put("ca_wqkv", a["L1_attn_a_Wqkv"])
    put("ca_bqkv", a["L1_attn_a_bqkv"].reshape(1, 3 * P))
    put("ca_wproj", a["L1_attn_a_Wproj"])
    put("ca_bproj", a["L1_attn_a_bproj"].reshape(1, P))
    row, col = np.arange(P)[:, None], np.arange(P)[None, :]
    put("ca_mask", np.stack([np.where(col > row, -1e30, 0.0), np.where(row > col, -1e30, 0.0)], axis=1).astype(np.float32))
    put("ca_sel", (np.arange(P)[:, None] % 32 == np.arange(16)[None, :]).astype(np.float32))
    put("ba_gain", a["L1_attn_b_gamma"].reshape(P, 1))
    cos, sin = _rotation(np, 64, False)
    put("ba_cos", cos)
    put("ba_sin", sin)
    wq, wk, wv = a["L1_attn_b_Wq"], a["L1_attn_b_Wkv"][:, :1024], a["L1_attn_b_Wkv"][:, 1024:]
    inner = np.arange(1024)
    neighbour = inner ^ 1
    pairs = np.zeros((8, P, 6, P), np.float32)
    for n, w in enumerate((wq, wq[:, neighbour], wk, wk[:, neighbour], wv)):
        pairs[:, :, n, :] = w.reshape(P, 8, P).transpose(1, 0, 2)
    for h in range(16):
        at = 64 * (h % 2)
        pairs[h // 2, at:at + 64, 5, at:at + 64] = a["L1_attn_b_W_bilinear"][h]
    put("ba_w", pairs)
    put("ba_wo", np.tile(a["L1_attn_b_Wo"].reshape(16, 64, P), (1, 2, 1)).transpose(1, 0, 2))
    put("moe_gate", a["L1_ffn_gate_w"].T)
    put("moe_bias", a["L1_ffn_bias_e"].reshape(1, 16))
    ups = np.concatenate([a["L1_ffn_up_w"].reshape(16 * 64, P), a["L1_ffn_shared_up"]], axis=0)
    put("moe_up", ups.T.reshape(P, 10, P))
    downs = np.concatenate([a["L1_ffn_down_w"].transpose(0, 2, 1).reshape(16 * 64, P), a["L1_ffn_shared_down"].T], axis=0)
    put("moe_down", downs.reshape(10, P, P).transpose(1, 0, 2))
    for n in (4, 16):
        put(f"before{n}", np.tril(np.ones((n, n), np.float32), -1).reshape(1, n * n))
    return W


def kernel(**inputs):
    import numpy as _np
    import concourse.bacc as _bacc
    from concourse.bass_utils import run_bass_kernel_spmd as _run

    laid = _lay_out(_np, {k: _np.asarray(v) for k, v in inputs.items()})
    nc = _bacc.Bacc("TRN2", target_bir_lowering=False, num_devices=1)
    arrays, W = {}, {}
    for name, a in laid.items():
        arrays[f"in_{name}"] = a
        W[name] = nc.dram_tensor(f"in_{name}", a.shape, mybir.dt.from_np(a.dtype), kind="ExternalInput").ap()
    out = nc.dram_tensor("out_x", (T, P), F32, kind="ExternalOutput").ap()
    program(nc, W, out, FIRST, LAST)
    got = _run(nc, [arrays], core_ids=[0])
    return got.results[0]["out_x"].reshape(1, T, P)
```

```python
from contextlib import ExitStack

import concourse.bass as bass
from concourse import mybir

ALU = mybir.AluOpType
ACT = mybir.ActivationFunctionType
AX = mybir.AxisListType
F32 = mybir.dt.float32
BF16 = mybir.dt.bfloat16
I32 = mybir.dt.int32

P = 128
T = 2048
NT = T // P
CH = 512
NC = T // CH
TC = CH // P
LN_EPS = 1e-5


class Stage:

    def __init__(self, nc, name):
        self.nc, self.name, self.sems, self.stack = nc, name, {}, ExitStack()

    def __enter__(self):
        return self

    def __exit__(self, *e):
        self.stack.close()
        self.nc.clear_and_free_semaphores(list(self.sems.values()))
        self.nc.all_engine_barrier()

    def sb(self, name, shape, dt=F32):
        return self.stack.enter_context(self.nc.sbuf_tensor(f"{self.name}_{name}", shape, dt))

    def ps(self, name, shape, dt=F32):
        return self.stack.enter_context(self.nc.psum_tensor(f"{self.name}_{name}", shape, dt))

    def __call__(self, name):
        if name not in self.sems:
            self.sems[name] = self.nc.alloc_semaphore(f"{self.name}_{name}")
        return self.sems[name]


class InOrder:

    def __init__(self, eng, S, c=0, per={}, start={}):
        self.eng, self.S, self.c, self.per, self.start, self.seen = eng, S, c, per, start, {}

    def __call__(self, instruction, name):
        self.seen[name] = self.seen.get(name, 0) + 1
        instruction.then_inc(self.S(name), 1)
        self.eng.wait_ge(self.S(name), self.c * self.per.get(name, 1) + self.start.get(name, 0) + self.seen[name])


def layernorm(nc, G, name, loads, inner, gain=None, shift=None, sums=None):
    X, U, UT, ident, mhalf = G["X"], G["U"], G["UT"], G["ident"], G["mhalf"]
    with Stage(nc, name) as S:
        stats = S.sb("stats", [P, NT, 6])
        mean, var, rstd = S.sb("mean", [P, NT]), S.sb("var", [P, NT]), S.sb("rstd", [P, NT])
        a, b, c, ve = (S.sb(n, [P, NT]) for n in ("a", "b", "c", "ve"))
        rstd2 = S.sb("rstd2", [P, NT])
        H = S.sb("H", [P, NT, P]) if inner else U
        turned = S.ps("turned", [P, NC, CH])
        with nc.Block() as block:
            @block.sync
            def _(sp):
                for dst, src in loads:
                    sp.dma_start(dst, src).then_inc(S("loaded"), 16)
                if loads:
                    sp.wait_ge(S("loaded"), 16 * len(loads))

            @block.vector
            def _(dve):
                o = InOrder(dve, S)
                for i in range(NT):
                    o(nc.vector.bn_stats(stats[:, i, :], X[:, i, :]), "stats")
                o(nc.vector.tensor_tensor(a[:, :], stats[:, :, 1], stats[:, :, 4], ALU.add), "halves")
                o(nc.vector.tensor_tensor(b[:, :], stats[:, :, 1], stats[:, :, 4], ALU.subtract), "halves")
                o(nc.vector.tensor_tensor(c[:, :], stats[:, :, 2], stats[:, :, 5], ALU.add), "halves")
                o(nc.vector.tensor_scalar(mean[:, :], a[:, :], 0.5, None, ALU.mult), "mean")
                o(nc.vector.scalar_tensor_tensor(out=a[:, :], in0=b[:, :], scalar=0.25, in1=b[:, :],
                                               op0=ALU.mult, op1=ALU.mult), "spread")
                o(nc.vector.scalar_tensor_tensor(out=var[:, :], in0=c[:, :], scalar=1.0 / P, in1=a[:, :],
                                               op0=ALU.mult, op1=ALU.add), "var")
                o(nc.vector.tensor_scalar(ve[:, :], var[:, :], LN_EPS, None, ALU.add), "ve")
                dve.wait_ge(S("rstd"), 1)
                for i in range(NT):
                    o(nc.vector.tensor_scalar(U[:, i, :], X[:, i, :], mean[:, i:i + 1], rstd[:, i:i + 1],
                                            ALU.subtract, ALU.mult), "u")
                    if inner and i == 0:
                        o(nc.vector.tensor_tensor(a[:, :], rstd[:, :], rstd[:, :], ALU.mult), "sq")
                        o(nc.vector.tensor_tensor(b[:, :], a[:, :], var[:, :], ALU.mult), "var2")
                        o(nc.vector.tensor_scalar(c[:, :], b[:, :], LN_EPS, None, ALU.add), "ve2")
                if gain is not None and loads:
                    dve.wait_ge(S("loaded"), 16 * len(loads))
                for k in range(NC):
                    dve.wait_ge(S("turned"), k + 1)
                    dst = UT[:, k * CH:(k + 1) * CH]
                    if gain is not None:
                        o(nc.vector.tensor_scalar(dst, turned[:, k, :], gain, shift, ALU.mult,
                                                ALU.add if shift is not None else ALU.bypass), "ut")
                    else:
                        o(nc.vector.tensor_copy(dst, turned[:, k, :]), "ut")

            @block.gpsimd
            def _(pool):
                pool.wait_ge(S("ve"), 1)
                pool.tensor_tensor(rstd[:, :], ve[:, :], mhalf[:, 0:NT], ALU.pow).then_inc(S("rstd"), 1)
                if inner:
                    pool.wait_ge(S("ve2"), 1)
                    pool.tensor_tensor(rstd2[:, :], c[:, :], mhalf[:, 0:NT], ALU.pow).then_inc(S("rstd2"), 1)

            @block.scalar
            def _(act):
                if inner:
                    act.wait_ge(S("rstd2"), 1)
                    for i in range(NT):
                        act.wait_ge(S("u"), i + 1)
                        nc.scalar.activation(H[:, i, :], U[:, i, :], ACT.Copy,
                                             scale=rstd2[:, i:i + 1]).then_inc(S("h"), 1)

            @block.tensor
            def _(pe):
                for i in range(NT):
                    pe.wait_ge(S("h" if inner else "u"), i + 1)
                    mm = nc.tensor.transpose(turned[:, i // TC, (i % TC) * P:(i % TC + 1) * P], H[:, i, :],
                                             ident[:, :])
                    if i % TC == TC - 1:
                        mm.then_inc(S("turned"), 1)


def linear_attention(nc, G, W):
    H, D = 16, 8
    X, U, UT, ident, mhalf = G["X"], G["U"], G["UT"], G["ident"], G["mhalf"]
    with Stage(nc, "la") as S:
        wqk = S.sb("wqk", [P, 4, P])
        wv = S.sb("wv", [P, D, P])
        wb, wo = S.sb("wb", [P, P]), S.sb("wo", [P, P])
        cos, sin = S.sb("cos", [P, T]), S.sb("sin", [P, T])
        pick = S.sb("pick", [P, D + 1, P])
        bb = S.sb("bb", [P, 1])
        bo, scale = S.sb("bo", [P, P]), S.sb("scale", [P, P])
        layernorm(nc, G, "ln1", [
            (wqk[:, :, :], W["la_wqk"]), (wb[:, :], W["la_wb"]), (bb[:, :], W["la_bb"]),
            (cos[:, :], W["la_cos"]), (sin[:, :], W["la_sin"]), (wv[:, :, :], W["la_wv"]),
            (pick[:, :, :], W["la_pick"]), (wo[:, :], W["la_wo"]),
            (bo[:, :], W["la_bo"].to_broadcast([P, P])), (scale[:, :], W["la_scale"].to_broadcast([P, P]))], False)
        acc = [S.ps(f"acc{k}", [P, CH]) for k in range(8)]
        rot = S.sb("rot", [P, 4, CH])
        qk = S.sb("qk", [P, 2, CH])
        low = S.sb("low", [P, 2, CH])
        ex = S.sb("ex", [P, 2, CH])
        phi = S.sb("phi", [P, 2, CH])
        beta = S.sb("beta", [P, T])
        kv = S.sb("kv", [P, 2, CH])
        st = S.sb("st", [P, D + 1, CH])
        last = S.sb("last", [P, D + 1])
        sq = S.sb("sq", [P, 2, CH])
        rden = S.sb("rden", [P, CH])
        attn = S.sb("attn", [P, CH])
        h = S.sb("h", [P, TC, P])
        hh = S.sb("hh", [P, TC, P])
        ms, rr = S.sb("ms", [P, TC]), S.sb("rr", [P, TC])
        with nc.Block() as block:
            @block.tensor
            def _(pe):
                for c in range(NC):
                    nc.tensor.matmul(acc[c][:, :], wb[:, :], UT[:, c * CH:(c + 1) * CH], start=True,
                                     stop=True).then_inc(S("zb"), 1)
                pe.wait_ge(S("sigmoid"), NC)
                with pe.Fori(0, NC) as c:
                    rhs = UT[:, bass.ts(c, CH)]
                    pe.wait_ge(S("y_read"), c + 1)
                    for n in range(4):
                        nc.tensor.matmul(acc[n][:, :], wqk[:, n, :], rhs, start=True, stop=True).then_inc(S("qk"), 1)
                    for e in range(D + 1):
                        if e < D:
                            pe.wait_ge(S("v_read"), D * c + e + 1)
                            nc.tensor.matmul(acc[5 + e % 2][:, :], wv[:, e, :], rhs, start=True,
                                             stop=True).then_inc(S("v"), 1)
                        if e >= 1:
                            pe.wait_ge(S("sq"), (D + 1) * c + e)
                            if e == 1:
                                pe.wait_ge(S("rot"), 4 * c + 4)
                            nc.tensor.matmul(acc[0][:, :], pick[:, e - 1, :], sq[:, (e - 1) % 2, :], start=(e == 1),
                                             stop=(e == D)).then_inc(S("num"), 1)
                    pe.wait_ge(S("sq"), (D + 1) * (c + 1))
                    nc.tensor.matmul(acc[1][:, :], pick[:, D, :], sq[:, D % 2, :], start=True,
                                     stop=True).then_inc(S("num"), 1)
                    pe.wait_ge(S("attn"), c + 1)
                    for i in range(TC):
                        mm = nc.tensor.matmul(acc[7][:, i * P:(i + 1) * P], attn[:, i * P:(i + 1) * P], wo[:, :],
                                              start=True, stop=True)
                    mm.then_inc(S("y"), 1)

            @block.scalar
            def _(act):
                for c in range(NC):
                    act.wait_ge(S("zb"), c + 1)
                    nc.scalar.activation(beta[:, c * CH:(c + 1) * CH], acc[c][:, :], ACT.Sigmoid,
                                         bias=bb[:, 0:1]).then_inc(S("sigmoid"), 1)
                nc.scalar.activation(ms[:, :], mhalf[:, 0:TC], ACT.Exp).then_inc(S("table"), 1)
                with act.Fori(0, NC) as c:
                    act.wait_ge(S("low"), c + 1)
                    nc.scalar.activation(ex[:, :, :], low[:, :, :], ACT.Exp).then_inc(S("ex"), 1)

            @block.vector
            def _(dve):
                dve.sem_inc(S("v_read"), 2)
                dve.sem_inc(S("y_read"), 1)
                dve.wait_ge(S("table"), 1)
                o = InOrder(dve, S)
                o(nc.vector.memset(last[:, :], 0.0), "start")
                dve.wait_ge(S("sigmoid"), NC)
                o(nc.vector.tensor_scalar(beta[:, :], beta[:, :], 0.8, 0.999, ALU.max, ALU.min), "clip")
                with dve.Fori(0, NC) as c:
                    o = InOrder(dve, S, c, {"rot": 4, "v_read": D, "scan": D + 1, "sq": D + 1},
                                {"v_read": 2, "y_read": 1})
                    for n in range(4):
                        dve.wait_ge(S("qk"), 4 * c + n + 1)
                        o(nc.vector.tensor_tensor(rot[:, n, :], acc[n][:, :],
                                                (cos if n % 2 == 0 else sin)[:, bass.ts(c, CH)],
                                                ALU.mult), "rot")
                    o(nc.vector.tensor_tensor(qk[:, :, :], rot[:, 0:4:2, :], rot[:, 1:4:2, :],
                                            ALU.add), "rotated")
                    o(nc.vector.tensor_scalar(low[:, :, :], qk[:, :, :], 0.0, None, ALU.min), "low")
                    dve.wait_ge(S("ex"), c + 1)
                    o(nc.vector.scalar_tensor_tensor(out=phi[:, :, :], in0=qk[:, :, :], scalar=0.0, in1=ex[:, :, :],
                                                   op0=ALU.max, op1=ALU.add), "phi")
                    for e in range(D + 1):
                        if e < D:
                            dve.wait_ge(S("v"), D * c + e + 1)
                            o(nc.vector.tensor_tensor(kv[:, e % 2, :], acc[5 + e % 2][:, :], phi[:, 1, :],
                                                    ALU.mult), "v_read")
                            src = kv[:, e % 2, :]
                        else:
                            src = phi[:, 1, :]
                        o(nc.vector.tensor_tensor_scan(st[:, e, :], beta[:, bass.ts(c, CH)], src, last[:, e:e + 1],
                                                     ALU.mult, ALU.add), "scan")
                        o(nc.vector.tensor_tensor(sq[:, e % 2, :], st[:, e, :], phi[:, 0, :],
                                                ALU.mult), "sq")
                        if e + 1 < D + 1:
                            if e >= 1:
                                dve.wait_ge(S("num"), (D + 1) * c + e)
                    o(nc.vector.tensor_copy(last[:, :], st[:, :, CH - 1]), "last")
                    dve.wait_ge(S("num"), (D + 1) * (c + 1))
                    o(nc.vector.tensor_scalar(ex[:, 0, :], acc[1][:, :], 1e-6, None, ALU.add), "den")
                    o(nc.vector.reciprocal(rden[:, :], ex[:, 0, :]), "rden")
                    o(nc.vector.tensor_tensor(attn[:, :], acc[0][:, :], rden[:, :], ALU.mult), "attn")
                    dve.wait_ge(S("y"), c + 1)
                    o(nc.vector.tensor_tensor(hh[:, :, :], acc[7][:, :].rearrange("p (i f) -> p i f", f=P),
                                            U[:, bass.ts(c, TC), :], ALU.add), "y_read")
                    o(nc.vector.tensor_tensor(h[:, :, :], hh[:, :, :],
                                            bo[:, :].unsqueeze(1).to_broadcast([P, TC, P]), ALU.add), "h")
                    o(nc.vector.tensor_tensor(hh[:, :, :], h[:, :, :], h[:, :, :], ALU.mult), "hh")
                    o(nc.vector.tensor_reduce(ms[:, :], hh[:, :, :], AX.X, ALU.add), "ms")
                    o(nc.vector.tensor_scalar(rr[:, :], ms[:, :], 1.0 / P, 1e-6, ALU.mult, ALU.add), "mse")
                    dve.wait_ge(S("rr"), c + 1)
                    o(nc.vector.tensor_tensor(hh[:, :, :], h[:, :, :],
                                            ms[:, :].unsqueeze(2).to_broadcast([P, TC, P]), ALU.mult), "hr")
                    o(nc.vector.tensor_tensor(h[:, :, :], hh[:, :, :],
                                            scale[:, :].unsqueeze(1).to_broadcast([P, TC, P]),
                                            ALU.mult), "hs")
                    o(nc.vector.tensor_tensor(X[:, bass.ts(c, TC), :], X[:, bass.ts(c, TC), :], h[:, :, :],
                                            ALU.add), "x")

            @block.gpsimd
            def _(pool):
                with pool.Fori(0, NC) as c:
                    pool.wait_ge(S("mse"), c + 1)
                    pool.tensor_tensor(ms[:, :], rr[:, :], mhalf[:, 0:TC], ALU.pow).then_inc(S("rr"), 1)


def ffn(nc, G, W, name, dequantise):
    X, U, UT = G["X"], G["U"], G["UT"]
    w1, w2, b1, hb2 = G["w1"], G["w2"], G["b1"], G["hb2"]
    FB = 4
    layernorm(nc, G, name + "ln", [], True, G["ffn_gain"][:, 0:1], G["ffn_shift"][:, 0:1])
    with Stage(nc, name) as S:
        if dequantise:
            q1, q2 = S.sb("q1", [P, FB * P], I32), S.sb("q2", [P, FB, P], I32)
            s1, s2 = S.sb("s1", [P, FB * P]), S.sb("s2", [P, FB, P])
            with nc.Block() as block:
                @block.sync
                def _(sp):
                    for n, (dst, src) in enumerate([
                            (q1[:, :], W["fc1_q"]), (s1[:, :], W["fc1_scales"].to_broadcast([P, FB * P])),
                            (q2[:, :, :], W["fc2_q"].rearrange("(b p) n -> p b n", p=P)),
                            (b1[:, :], W["fc1_bias"])]):
                        sp.dma_start(dst, src).then_inc(S("quantised"), 16)
                    for b in range(FB):
                        sp.dma_start(s2[:, b, :], W["fc2_scales"][b:b + 1, :].to_broadcast([P, P])).then_inc(S("quantised"), 16)
                    sp.dma_start(hb2[:, :], W["fc2_bias"].to_broadcast([P, P])).then_inc(S("quantised"), 16)

                @block.vector
                def _(dve):
                    o = InOrder(dve, S)
                    dve.wait_ge(S("quantised"), 16 * (5 + FB))
                    o(nc.vector.scalar_tensor_tensor(out=w1[:, :], in0=q1[:, :], scalar=-128.0, in1=s1[:, :],
                                                   op0=ALU.add, op1=ALU.mult), "w")
                    o(nc.vector.scalar_tensor_tensor(out=w2[:, :, :], in0=q2[:, :, :], scalar=-128.0, in1=s2[:, :, :],
                                                   op0=ALU.add, op1=ALU.mult), "w")
                    o(nc.vector.tensor_scalar(s1[:, 0:P], hb2[:, :], 0.5, None, ALU.mult), "hb")
                    o(nc.vector.tensor_copy(hb2[:, :], s1[:, 0:P]), "w")
        hid = [S.ps(f"hid{b}", [P, CH]) for b in range(FB)]
        z = S.ps("z", [P, TC, P])
        y = S.sb("y", [P, FB, CH])
        xu = S.sb("xu", [P, TC, P])
        xub = S.sb("xub", [P, TC, P])
        with nc.Block() as block:
            @block.tensor
            def _(pe):
                with pe.Fori(0, NC) as c:
                    for b in range(FB):
                        pe.wait_ge(S("y"), FB * c + b + 1)
                        nc.tensor.matmul(hid[b][:, :], w1[:, b * P:(b + 1) * P], UT[:, bass.ts(c, CH)],
                                         start=True, stop=True).then_inc(S("hid"), 1)
                    pe.wait_ge(S("y"), FB * c + 2 * FB)
                    pe.wait_ge(S("x"), c + 1)
                    for i in range(TC):
                        for b in range(FB):
                            mm = nc.tensor.matmul(z[:, i, :], y[:, b, i * P:(i + 1) * P], w2[:, b, :],
                                                  start=(b == 0), stop=(b == FB - 1))
                    mm.then_inc(S("z"), 1)

            @block.scalar
            def _(act):
                act.sem_inc(S("y"), FB)
                nc.scalar.activation(y[:, 0, 0:1], b1[:, 0:1], ACT.Silu).then_inc(S("table"), 1)
                act.wait_ge(S("table"), 1)
                with act.Fori(0, NC) as c:
                    act.wait_ge(S("z_free"), c + 1)
                    for b in range(FB):
                        act.wait_ge(S("hid"), FB * c + b + 1)
                        nc.scalar.activation(y[:, b, :], hid[b][:, :], ACT.Silu, bias=b1[:, b:b + 1]).then_inc(S("y"), 1)

            @block.vector
            def _(dve):
                dve.sem_inc(S("x"), 1)
                dve.sem_inc(S("z_free"), 1)
                with dve.Fori(0, NC) as c:
                    o = InOrder(dve, S, c, {}, {"x": 1})
                    o(nc.vector.tensor_tensor(xu[:, :, :], X[:, bass.ts(c, TC), :], U[:, bass.ts(c, TC), :],
                                            ALU.add), "xu")
                    o(nc.vector.tensor_tensor(xub[:, :, :], xu[:, :, :], hb2[:, :].unsqueeze(1).to_broadcast([P, TC, P]),
                                            ALU.add), "xub")
                    dve.wait_ge(S("z"), c + 1)
                    dve.sem_inc(S("z_free"), 1)
                    o(nc.vector.scalar_tensor_tensor(out=X[:, bass.ts(c, TC), :], in0=z[:, :, :], scalar=0.5,
                                                   in1=xub[:, :, :], op0=ALU.mult, op1=ALU.add), "x")


def experts(nc, G, W, name):
    E, GR, K = 16, 4, 4
    NB, NE = 10, 8
    X, U, UT, ident = G["X"], G["U"], G["UT"], G["ident"]
    with Stage(nc, name) as S:
        up, down = S.sb("up", [P, NB, P]), S.sb("down", [P, NB, P])
        gate, bias = S.sb("gate", [P, E]), S.sb("bias", [P, E])
        tri, trig = S.sb("tri", [P, E, E]), S.sb("trig", [P, GR, GR])
        layernorm(nc, G, name + "ln", [
            (gate[:, :], W["moe_gate"]), (bias[:, :], W["moe_bias"].to_broadcast([P, E])),
            (tri[:, :, :], W["before16"].to_broadcast([P, E * E]).rearrange("p (a b) -> p a b", a=E)),
            (trig[:, :, :], W["before4"].to_broadcast([P, GR * GR]).rearrange("p (a b) -> p a b", a=GR)),
            (up[:, :, :], W["moe_up"]), (down[:, :, :], W["moe_down"])], False)
        cw = S.sb("cw", [P, NT, E])
        router(nc, G, name + "r", gate, bias, tri, trig, cw)
        hid = [S.ps(f"hid{b}", [P, CH]) for b in range(3)]
        crep = [S.ps(f"crep{b}", [P, CH]) for b in range(2)]
        z = [S.ps(f"z{n}", [P, TC, P]) for n in range(2)]
        cwe = [S.sb(f"cwe{n}", [P, TC, E, P // 2]) for n in range(2)]
        r = S.sb("r", [P, 2, CH])
        sq = S.sb("sq", [P, 2, CH])
        hT = [S.sb(f"hT{n}", [P, NB, CH]) for n in range(2)]
        spread = [cw[:, TC * c:TC * (c + 1), :].unsqueeze(3).to_broadcast([P, TC, E, P // 2]) for c in range(NC)]
        with nc.Block() as block:
            @block.tensor
            def _(pe):
                def down_part(c, n):
                    if n == 0:
                        pe.wait_ge(S("weighted"), NE * c + NE)
                        pe.wait_ge(S("shared"), 2 * c + 2)
                        if c >= 2:
                            pe.wait_ge(S("x"), c - 1)
                    for m in range(TC * n, TC * (n + 1)):
                        i, b = m // NB, m % NB
                        mm = nc.tensor.matmul(z[c % 2][:, i, :], hT[c % 2][:, b, i * P:(i + 1) * P], down[:, b, :],
                                              start=(b == 0), stop=(b == NB - 1))
                    if n == NB - 1:
                        mm.then_inc(S("z"), 1)

                for c in range(NC + 1):
                    for b in range(NB):
                        if c < NC:
                            if NB * c + b >= 3:
                                pe.wait_ge(S("r"), NB * c + b - 2)
                            nc.tensor.matmul(hid[(NB * c + b) % 3][:, :], up[:, b, :], UT[:, c * CH:(c + 1) * CH],
                                             start=True, stop=True).then_inc(S("hid"), 1)
                            if b < NE:
                                if b == 0:
                                    pe.wait_ge(S("cwe_first" if c == 0 else "cwe"), max(c, 1))
                                if NE * c + b >= 2:
                                    pe.wait_ge(S("weighted"), NE * c + b - 1)
                                for i in range(TC):
                                    w = cwe[c % 2][:, i, 2 * b:2 * b + 2, :].rearrange("p e f -> p (e f)")
                                    mm = nc.tensor.transpose(crep[b % 2][:, i * P:(i + 1) * P], w, ident[:, :])
                                mm.then_inc(S("crep"), 1)
                        if c:
                            down_part(c - 1, b)

            @block.scalar
            def _(act):
                nc.scalar.activation(cwe[0][:, :, :, :], spread[0], ACT.Copy).then_inc(S("cwe_first"), 1)
                for c in range(NC):
                    for b in range(NB):
                        k = NB * c + b
                        act.wait_ge(S("hid"), k + 1)
                        if k >= 2:
                            act.wait_ge(S("squared"), k - 1)
                        nc.scalar.activation(r[:, b % 2, :], hid[k % 3][:, :], ACT.Relu).then_inc(S("r"), 1)
                        act.wait_ge(S("r"), k + 1)
                        if b < NE:
                            if NE * c + b >= 2:
                                act.wait_ge(S("weighted"), NE * c + b - 1)
                            nc.scalar.activation(sq[:, b % 2, :], r[:, b % 2, :], ACT.Square).then_inc(S("squared"), 1)
                        else:
                            if c >= 2:
                                act.wait_ge(S("z"), c - 1)
                            nc.scalar.activation(hT[c % 2][:, b, :], r[:, b % 2, :], ACT.Square).then_inc(S("shared"), 1)
                            act.wait_ge(S("shared"), 2 * c + b - NE + 1)
                            act.sem_inc(S("squared"), 1)

            @block.gpsimd
            def _(pool):
                for c in range(1, NC):
                    if c >= 2:
                        pool.wait_ge(S("crep"), NE * (c - 1))
                    pool.tensor_copy(cwe[c % 2][:, :, :, :], spread[c]).then_inc(S("cwe"), 1)

            @block.vector
            def _(dve):
                o = InOrder(dve, S)
                for c in range(NC + 1):
                    if c < NC:
                        for b in range(NE):
                            if b == 0 and c >= 2:
                                dve.wait_ge(S("z"), c - 1)
                            dve.wait_ge(S("squared"), NB * c + b + 1)
                            dve.wait_ge(S("crep"), NE * c + b + 1)
                            o(nc.vector.tensor_tensor(hT[c % 2][:, b, :], crep[b % 2][:, :], sq[:, b % 2, :],
                                                      ALU.mult), "weighted")
                    if c:
                        tiles = slice(TC * (c - 1), TC * c)
                        dve.wait_ge(S("z"), c)
                        o(nc.vector.tensor_tensor(X[:, tiles, :], z[(c - 1) % 2][:, :, :], X[:, tiles, :], ALU.add), "x")


def router(nc, G, name, gate, bias, tri, trig, cw):
    E, GR, KE = 16, 4, 4
    KG = E // GR
    with Stage(nc, name) as S:
        logits = S.ps("logits", [P, NT, E])
        score, sc = S.sb("score", [P, NT, E]), S.sb("sc", [P, NT, E])
        big, small, big2, small2, top, second, least, sums = (
            S.sb(n, [P, NT, GR]) for n in ("big", "small", "big2", "small2", "top", "second", "least", "sums"))
        pg, pge = S.sb("pg", [P, NT, GR, GR]), S.sb("pge", [P, NT, GR, GR])
        pa, pae = S.sb("pa", [P, NT, E, E]), S.sb("pae", [P, NT, E, E])
        rg, ra, kept, tot, inv = (S.sb("rg", [P, NT, GR]), S.sb("ra", [P, NT, E]), S.sb("kept", [P, NT, E]),
                                  S.sb("tot", [P, NT]), S.sb("inv", [P, NT]))
        UT = G["UT"]
        with nc.Block() as block:
            @block.tensor
            def _(pe):
                for i in range(NT):
                    mm = nc.tensor.matmul(logits[:, i, :], UT[:, i * P:(i + 1) * P], gate[:, :], start=True, stop=True)
                mm.then_inc(S("logits"), 1)

            @block.scalar
            def _(act):
                act.wait_ge(S("logits"), 1)
                nc.scalar.activation(score[:, :, :], logits[:, :, :], ACT.Sigmoid).then_inc(S("score"), 1)

            @block.vector
            def _(dve):
                o = InOrder(dve, S)
                tt = nc.vector.tensor_tensor
                dve.wait_ge(S("score"), 1)
                o(tt(sc[:, :, :], score[:, :, :], bias[:, :].unsqueeze(1).to_broadcast([P, NT, E]), ALU.add), "sc")
                v = sc[:, :, :].rearrange("p t (g k) -> p t g k", k=KG)
                o(tt(big[:, :, :], v[:, :, :, 0], v[:, :, :, 1], ALU.max), "pairs")
                o(tt(small[:, :, :], v[:, :, :, 0], v[:, :, :, 1], ALU.min), "pairs")
                o(tt(big2[:, :, :], v[:, :, :, 2], v[:, :, :, 3], ALU.max), "pairs")
                o(tt(small2[:, :, :], v[:, :, :, 2], v[:, :, :, 3], ALU.min), "pairs")
                o(tt(top[:, :, :], big[:, :, :], big2[:, :, :], ALU.max), "pairs")
                o(tt(second[:, :, :], big[:, :, :], big2[:, :, :], ALU.min), "pairs")
                o(tt(least[:, :, :], small[:, :, :], small2[:, :, :], ALU.max), "pairs")
                o(tt(big[:, :, :], second[:, :, :], least[:, :, :], ALU.max), "pairs")
                o(tt(sums[:, :, :], top[:, :, :], big[:, :, :], ALU.add), "sums")

                def rank(out, x, n, pairs, equal, before):
                    other, own = (x.unsqueeze(k).to_broadcast([P, NT, n, n]) for k in (2, 3))
                    o(tt(pairs, other, own, ALU.is_gt), "ranks")
                    o(tt(equal, other, own, ALU.is_equal), "ranks")
                    o(tt(equal, equal, before.unsqueeze(1).to_broadcast([P, NT, n, n]), ALU.mult), "ranks")
                    o(tt(pairs, pairs, equal, ALU.add), "ranks")
                    o(nc.vector.tensor_reduce(out, pairs, AX.X, ALU.add), "ranks")

                rank(rg[:, :, :], sums[:, :, :], GR, pg[:, :, :, :], pge[:, :, :, :], trig[:, :, :])
                o(nc.vector.tensor_scalar(top[:, :, :], rg[:, :, :], 2.0, None, ALU.is_lt), "groups")
                o(tt(kept[:, :, :].rearrange("p t (g k) -> p t g k", k=KG), v,
                     top[:, :, :].unsqueeze(3).to_broadcast([P, NT, GR, KG]), ALU.mult), "kept")
                rank(ra[:, :, :], kept[:, :, :], E, pa[:, :, :, :], pae[:, :, :, :], tri[:, :, :])
                o(nc.vector.scalar_tensor_tensor(out=kept[:, :, :], in0=ra[:, :, :], scalar=float(KE), in1=score[:, :, :],
                                                 op0=ALU.is_lt, op1=ALU.mult), "chosen")
                o(nc.vector.tensor_reduce(tot[:, :], kept[:, :, :], AX.X, ALU.add), "total")
                o(nc.vector.tensor_scalar(tot[:, :], tot[:, :], 1e-20, None, ALU.add), "total")
                o(nc.vector.reciprocal(inv[:, :], tot[:, :]), "inverse")
                o(nc.vector.scalar_tensor_tensor(out=cw[:, :, :], in0=kept[:, :, :], scalar=2.5,
                                                 in1=inv[:, :].unsqueeze(2).to_broadcast([P, NT, E]),
                                                 op0=ALU.mult, op1=ALU.mult), "weights")


def split3(nc, o, src, parts, left):
    o(nc.vector.tensor_copy(parts[0], src), "split")
    o(nc.vector.tensor_tensor(left, src, parts[0], ALU.subtract), "split")
    o(nc.vector.tensor_copy(parts[1], left), "split")
    o(nc.vector.tensor_tensor(parts[2], left, parts[1], ALU.subtract), "split")


def causal_attention(nc, G, W):
    NH, D = 16, 8
    X, U, UT, ident, identb = G["X"], G["U"], G["UT"], G["ident"], G["identb"]
    ORDER_Q, ORDER_K = (0, 0, 1, 1, 0, 2), (0, 1, 0, 1, 2, 0)
    SHIFT = 64
    SCALE = float(D) ** -0.5
    VW = 32
    items1 = [(i, k) for i in range(NT) for k in range(i // TC + 1)]
    items2 = [(c, k) for c in range(NC) for k in range(TC * (c + 1))]
    N1, N2 = len(items1), len(items2)
    AHEAD = 2
    SLOTS = 2 * TC
    B1, B2 = 3, 2
    LATE = 3
    EARLY = 28
    row_of = [nc.dram_tensor(f"ca_row{s}", (3, T), BF16).ap() for s in range(2)]
    rows_of = nc.dram_tensor("ca_rows", (NH, 2, 6 * D, T), BF16).ap()
    with Stage(nc, "ca") as S:
        wqkv = S.sb("wqkv", [P, 3 * P])
        bqkv, bproj = S.sb("bqkv", [P, 3 * P]), S.sb("bproj", [P, P])
        wproj = S.sb("wproj", [P, P])
        later, earlier = S.sb("later", [P, P], BF16), S.sb("earlier", [P, P], BF16)
        maskf = S.sb("maskf", [P, 2, P])
        sel = S.sb("sel", [P, 16])
        layernorm(nc, G, "caln", [
            (wqkv[:, :], W["ca_wqkv"]), (bqkv[:, :], W["ca_bqkv"].to_broadcast([P, 3 * P])),
            (wproj[:, :], W["ca_wproj"]), (bproj[:, :], W["ca_bproj"].to_broadcast([P, P])),
            (maskf[:, :, :], W["ca_mask"]), (sel[:, :], W["ca_sel"])], False)
        parts = S.sb("parts", [P, 2, 3, T], BF16)
        vall = S.sb("vall", [P, NT, P])
        qs = [S.sb(f"qs{s}", [P, T], BF16) for s in range(2)]
        ks = [S.sb(f"ks{s}", [P, T], BF16) for s in range(2)]
        zeros = S.sb("zeros", [3, T], BF16)
        vh = [S.sb(f"vh{s}", [P, NT, VW]) for s in range(2)]
        most = S.sb("most", [P, NT, NC])
        with Stage(nc, "cap") as R:
            proj = [R.ps(f"proj{n}", [P, 3 * P]) for n in range(2)]
            turned = [R.ps(f"turned{n}", [P, TC, P]) for n in range(4)]
            xq = R.sb("xq", [P, 3, NT, NH, D])
            flat = R.sb("flat", [P, 3, T])
            left = R.sb("left", [P, T])
            with nc.Block() as block:
                @block.sync
                def _(sp):
                    for s in range(2):
                        sp.wait_ge(R("split"), 4 * (s + 1))
                        for n in range(6):
                            sp.dma_start(rows_of.rearrange("h s (n d) t -> n s h d t", d=D)[n, s],
                                         parts[:, s, (ORDER_Q, ORDER_K)[s][n], :]).then_inc(R("rows"), 16)
                    sp.wait_ge(R("rows"), 16 * 12)

                @block.gpsimd
                def _(pool):
                    o = InOrder(pool, S)
                    for s in range(2):
                        o(pool.memset(qs[s][:, :], 0.0), "clean")
                        o(pool.memset(ks[s][:, :], 0.0), "clean")
                        o(pool.memset(ks[s][SHIFT:SHIFT + 3, :], 1.0), "clean")
                    o(pool.memset(zeros[:, :], 0.0), "clean")
                    for s in range(2):
                        o(pool.memset(vh[s][:, :, D:VW], 0.0), "vclean")
                        o(pool.memset(vh[s][:, :, D:D + 1], 1.0), "vclean")
                    o(pool.memset(most[:, :, :], -3e38), "vclean")

                @block.tensor
                def _(pe):
                    for i in range(NT):
                        if i >= 2:
                            pe.wait_ge(R("xq"), i - 1)
                        nc.tensor.matmul(proj[i % 2][:, :], UT[:, i * P:(i + 1) * P], wqkv[:, :], start=True,
                                         stop=True).then_inc(R("proj"), 1)
                    pe.wait_ge(R("xq"), NT)
                    for n in range(12):
                        if n >= 4:
                            pe.wait_ge(R("flat"), n - 3)
                        for j in range(4):
                            mm = nc.tensor.transpose(turned[n % 4][:, j, :],
                                                     xq[:, n // 4, 4 * (n % 4) + j, :, :].rearrange("p h d -> p (h d)"),
                                                     ident[:, :])
                        mm.then_inc(R("turned"), 1)
                    for n in range(4):
                        pe.wait_ge(R("flat"), 12)
                        for j in range(TC):
                            mm = nc.tensor.transpose(turned[n][:, j, :], flat[:, 2, (TC * n + j) * P:(TC * n + j + 1) * P],
                                                     ident[:, :])
                        mm.then_inc(R("v_turned"), 1)

                @block.vector
                def _(dve):
                    o = InOrder(dve, R)
                    o(nc.vector.tensor_copy(later[:, :], maskf[:, 0, :]), "mask")
                    o(nc.vector.tensor_copy(earlier[:, :], maskf[:, 1, :]), "mask")
                    for i in range(NT):
                        dve.wait_ge(R("proj"), i + 1)
                        o(nc.vector.tensor_tensor(xq[:, :, :, i, :],
                                                  proj[i % 2][:, :].rearrange("p (s j d) -> p s j d", s=3, d=D),
                                                  bqkv[:, :].rearrange("p (s j d) -> p s j d", s=3, d=D), ALU.add), "xq")
                    for n in range(12):
                        dve.wait_ge(R("turned"), n + 1)
                        o(nc.vector.tensor_copy(
                            flat[:, n // 4, :].rearrange("r (p j) -> r j p", j=NT)[:, 4 * (n % 4):4 * (n % 4) + 4, :],
                            turned[n % 4][:, :, :]), "flat")
                        if n in (3, 7):
                            s = n // 4
                            split3(nc, o, flat[:, s, :], [parts[:, s, m, :] for m in range(3)], left[:, :])
                    for n in range(4):
                        dve.wait_ge(R("v_turned"), n + 1)
                        o(nc.vector.tensor_copy(vall[:, TC * n:TC * (n + 1), :], turned[n][:, :, :]), "vall")

        y = S.sb("y", [P, NT, P])
        pt = S.sb("pt", [P, SLOTS, CH])
        negm = S.sb("negm", [P, NT])
        nmt, nml = S.sb("nmt", [NT, P]), S.sb("nml", [NT, P])
        nm3 = S.sb("nm3", [NT, 3, P], BF16)
        os_ = S.sb("os", [P, CH])
        den = S.sb("den", [P, TC])
        s1 = [S.ps(f"s1{n}", [P, CH]) for n in range(B1)]
        s2 = [S.ps(f"s2{n}", [P, CH]) for n in range(B2)]
        pv = [S.ps(f"pv{n}", [P, CH]) for n in range(2)]
        misc = S.ps("misc", [P, CH])
        nm_ps = misc[0:NT, 0:P]
        fin = misc[:, 256:256 + TC * 16].rearrange("p (i c) -> p i c", c=16)
        per1 = [[n for n in range(N1) if LATE + n * (EARLY - LATE) // N1 == k] for k in range(N2)]
        with nc.Block() as block:
            @block.sync
            def _(sp):
                def stack(h, g, s):
                    sp.dma_start(qs[s][0:6 * D, :], rows_of[h, 0, :, :]).then_inc(S(f"stack{s}"), 16)
                    sp.dma_start(ks[s][0:6 * D, :], rows_of[h, 1, :, :]).then_inc(S(f"stack{s}"), 16)
                    sp.dma_start(qs[s][SHIFT:SHIFT + 3, :], zeros[:, :]).then_inc(S(f"stack{s}"), 16)

                def shift(h, g, s):
                    sp.wait_ge(S("nm3"), h + 1)
                    sp.dma_start(row_of[s].rearrange("n (i p) -> i n p", p=P), nm3[:, :, :]).then_inc(S(f"row{s}"), 16)
                    sp.wait_ge(S(f"row{s}"), 16 * (g + 1))
                    sp.dma_start(qs[s][SHIFT:SHIFT + 3, :], row_of[s]).then_inc(S(f"shift{s}"), 16)

                def next_stack(h, g, s):
                    sp.wait_ge(S("pass2"), N2 * (h - 1))
                    sp.sem_inc(S("paced"), 1)
                    stack(h, g, s)

                sp.wait_ge(S("clean"), 7)
                for s in range(2):
                    stack(s, 0, s)
                shift(0, 0, 0)
                with sp.Fori(0, NH // 2 - 1) as g:
                    shift(2 * g + 1, g, 1)
                    next_stack(2 * g + 2, g + 1, 0)
                    shift(2 * g + 2, g + 1, 0)
                    next_stack(2 * g + 3, g + 1, 1)
                shift(NH - 1, NH // 2 - 1, 1)

            @block.gpsimd
            def _(pool):
                with pool.Fori(0, NH) as h:
                    for k in range(1, TC):
                        pool.wait_ge(S("pv"), N2 * h + k + 1)
                        pool.sem_inc(S("paced_pool"), 1)
                        pool.memset(pt[:, k, 0:k * P], 0.0).then_inc(S("blank"), 1)

            @block.tensor
            def _(pe):
                def pass1(h, g, s, n):
                    i, k = items1[n]
                    if n == 0:
                        pe.wait_ge(S(f"stack{s}"), 16 * 3 * (g + 1))
                    pe.wait_ge(S("max"), N1 * h + n + 1)
                    width = min(CH, (i + 1) * P - k * CH)
                    last = k == i // TC
                    mm = nc.tensor.matmul(s1[n % B1][:, 0:width], qs[s][:, i * P:(i + 1) * P],
                                          ks[s][:, k * CH:k * CH + width], start=True, stop=not last)
                    if last:
                        mm = nc.tensor.matmul(s1[n % B1][:, width - P:width], identb[:, :], later[:, :],
                                              start=False, stop=True)
                    mm.then_inc(S("pass1"), 1)

                def pass2(h, g, s, n):
                    c, k = items2[n]
                    if n == 0:
                        pe.wait_ge(S(f"shift{s}"), 16 * (g + 1))
                    pe.wait_ge(S("exp"), N2 * h + n + 1)
                    lo = max(0, k - TC * c) * P
                    mm = nc.tensor.matmul(s2[n % B2][:, lo:CH], ks[s][:, k * P:(k + 1) * P],
                                          qs[s][:, c * CH + lo:(c + 1) * CH], start=True, stop=k < TC * c)
                    if k >= TC * c:
                        mm = nc.tensor.matmul(s2[n % B2][:, lo:lo + P], identb[:, :], earlier[:, :],
                                              start=False, stop=True)
                    mm.then_inc(S("pass2"), 1)

                def values(h, g, s, n):
                    c, k = items2[n]
                    if n == 0:
                        pe.wait_ge(S("vh"), h + 1)
                    if k == 0:
                        pe.wait_ge(S("os"), NC * h + c + 1)
                    pe.wait_ge(S("exp"), N2 * h + n + B2 + 1)
                    if c == 0 and k == 0:
                        pe.wait_ge(S("blank"), (TC - 1) * (h + 1))
                    lo = max(0, k - TC * c) * P if c else 0
                    grp = (k % TC) * VW
                    nc.tensor.matmul(pv[c % 2][grp:grp + VW, lo:CH], vh[s][:, k, :], pt[:, n % SLOTS, lo:CH],
                                     start=k < TC, stop=k >= TC * c).then_inc(S("pv"), 1)

                def finish(h, c, more):
                    pe.wait_ge(S("os"), NC * h + c + 3)
                    if more and c == NC - 1:
                        pe.wait_ge(S("nmt_here"), h + 2)
                    pe.wait_ge(S("y"), NC * h + c + 1)
                    for i in range(TC):
                        mm = nc.tensor.matmul(fin[:, i, :], os_[:, i * P:(i + 1) * P], sel[:, :],
                                              start=True, stop=True)
                    mm.then_inc(S("fin"), 1)

                def turn(h, divided):
                    pe.wait_ge(S("negm"), h + 1)
                    if divided:
                        pe.wait_ge(S("y"), NC * (h - 1) + divided + 1)
                    nc.tensor.transpose(nm_ps, negm[:, :], ident[:, :]).then_inc(S("nmt"), 1)

                def head(h, g, s, more):
                    g1 = g if s == 0 else g + 1
                    for n in range(N2 + AHEAD + 1):
                        if n < N2:
                            if more:
                                for m in per1[n]:
                                    pass1(h + 1, g1, 1 - s, m)
                            pass2(h, g, s, n)
                        if n == EARLY + 3 and more:
                            turn(h + 1, sum(TC * (c + 1) * (c + 2) // 2 - 1 + AHEAD + 1 < n for c in range(NC)))
                        if n >= AHEAD and (n - AHEAD) % TC == TC - 1:
                            for m in range(n - AHEAD - TC + 1, n - AHEAD + 1):
                                values(h, g, s, m)
                        m = n - AHEAD - 1
                        if m >= 0 and items2[m][1] == TC * (items2[m][0] + 1) - 1:
                            finish(h, items2[m][0], more)

                for n in range(N1):
                    pass1(0, 0, 0, n)
                turn(0, 0)
                with pe.Fori(0, NH // 2 - 1) as g:
                    head(2 * g, g, 0, True)
                    head(2 * g + 1, g, 1, True)
                head(NH - 2, NH // 2 - 1, 0, True)
                head(NH - 1, NH // 2 - 1, 1, False)

            @block.scalar
            def _(act):
                act.sem_inc(S("exp"), B2)
                nc.scalar.activation(pt[:, 0, 0:1], ident[:, 0:1], ACT.Exp).then_inc(S("table"), 1)
                act.wait_ge(S("table"), 1)

                def sums(h, c):
                    act.wait_ge(S("pv"), N2 * h + TC * (c + 1) * (c + 2) // 2 + SLOTS)
                    act.wait_ge(S("fin"), NC * h + c + 1)
                    nc.scalar.activation(os_[:, :], pv[c % 2][:, :], ACT.Copy).then_inc(S("os"), 1)

                def head(h):
                    for n in range(N2 + AHEAD):
                        m = n - AHEAD
                        if m >= 0 and items2[m][1] == TC * (items2[m][0] + 1) - 1:
                            sums(h, items2[m][0])
                        if n >= N2:
                            continue
                        c, k = items2[n]
                        act.wait_ge(S("pass2"), N2 * h + n + 1)
                        act.wait_ge(S("pv"), N2 * h + n + 1)
                        lo = max(0, k - TC * c) * P
                        nc.scalar.activation(pt[:, n % SLOTS, lo:CH], s2[n % B2][:, lo:CH], ACT.Exp,
                                             scale=SCALE).then_inc(S("exp"), 1)
                with act.Fori(0, NH // 2) as g:
                    head(2 * g)
                    head(2 * g + 1)

            @block.vector
            def _(dve):
                dve.wait_ge(S("vclean"), 5)
                dve.sem_inc(S("max"), B1)
                dve.sem_inc(S("os"), 2)
                dve.sem_inc(S("fin"), 1)
                dve.sem_inc(S("y"), 1)
                dve.sem_inc(S("pv"), SLOTS)

                def maxima(h, n):
                    i, k = items1[n]
                    width = min(CH, (i + 1) * P - k * CH)
                    dve.wait_ge(S("pass1"), N1 * h + n + 1)
                    nc.vector.tensor_reduce(most[:, i, k:k + 1], s1[n % B1][:, 0:width], AX.X, ALU.max).then_inc(S("max"), 1)

                def negate(h):
                    dve.wait_ge(S("max"), N1 * (h + 1) + B1)
                    nc.vector.tensor_reduce(negm[:, :], most[:, :, :], AX.X, ALU.max, negate=True).then_inc(S("negm"), 1)
                    dve.wait_ge(S("negm"), h + 1)

                def spread(h, g, s):
                    dve.wait_ge(S("nmt"), h + 1)
                    if s is not None:
                        dve.wait_ge(S(f"row{1 - s}"), 16 * (g + 1 if s else g))
                    o = InOrder(dve, S, h, {"split": 4})
                    o(nc.vector.tensor_copy(nmt[:, :], nm_ps), "nmt_here")
                    o(nc.vector.tensor_copy(nm3[:, 0, :], nmt[:, :]), "split")
                    o(nc.vector.tensor_tensor(nml[:, :], nmt[:, :], nm3[:, 0, :], ALU.subtract), "split")
                    o(nc.vector.tensor_copy(nm3[:, 1, :], nml[:, :]), "split")
                    nc.vector.tensor_tensor(nm3[:, 2, :], nml[:, :], nm3[:, 1, :], ALU.subtract).then_inc(S("nm3"), 1)
                    dve.wait_ge(S("nm3"), h + 1)
                    dve.sem_inc(S("split"), 1)

                def take_v(h, s, first):
                    if not first:
                        dve.wait_ge(S("pv"), N2 * (h - 1) + SLOTS)
                    nc.vector.tensor_copy(vh[s][:, :, 0:D], vall[:, :, bass.ds(h * D, D)]).then_inc(S("vh"), 1)

                def divide(h, c):
                    dve.wait_ge(S("fin"), NC * h + c + 2)
                    nc.vector.reciprocal(den[:, :], fin[:, :, D]).then_inc(S("den"), 1)
                    dve.wait_ge(S("den"), NC * h + c + 1)
                    nc.vector.tensor_tensor(y[:, TC * c:TC * (c + 1), bass.ds(h * D, D)], fin[:, :, 0:D],
                                            den[:, :].unsqueeze(2).to_broadcast([P, TC, D]), ALU.mult).then_inc(S("y"), 1)
                    dve.wait_ge(S("y"), NC * h + c + 2)

                def head(h, g, s, more):
                    for n in range(N2 + AHEAD + 2):
                        if n < N2 and more:
                            for m in per1[n]:
                                maxima(h + 1, m)
                        if n == EARLY + 1 and more:
                            negate(h + 1)
                        if n == EARLY + 4 and more:
                            spread(h + 1, g, 1 - s) if s == 0 else spread(h + 1, g + 1, 0)
                        m = n - AHEAD - 2
                        if 0 <= m < N2 and items2[m][1] == TC * (items2[m][0] + 1) - 1:
                            divide(h, items2[m][0])
                    if more:
                        take_v(h + 1, 1 - s, False)

                for n in range(N1):
                    maxima(0, n)
                negate(0)
                spread(0, 0, None)
                take_v(0, 0, True)
                head(0, 0, 0, True)
                with dve.Fori(0, NH // 2 - 1) as g:
                    head(2 * g + 1, g, 1, True)
                    head(2 * g + 2, g + 1, 0, True)
                head(NH - 1, NH // 2 - 1, 1, False)

        with Stage(nc, "cao") as R:
            turned = s1
            z = [pv[n][:, :].rearrange("p (i f) -> p i f", f=P) for n in range(2)]
            yt = R.sb("yt", [P, 2, CH])
            xb = R.sb("xb", [P, NT, P])
            with nc.Block() as block:
                @block.tensor
                def _(pe):
                    def turn(c):
                        for i in range(TC):
                            mm = nc.tensor.transpose(turned[c % 2][:, i * P:(i + 1) * P], y[:, TC * c + i, :], ident[:, :])
                        mm.then_inc(R("turned"), 1)

                    turn(0)
                    for c in range(NC):
                        if c + 1 < NC:
                            if c:
                                pe.wait_ge(R("yt"), c)
                            turn(c + 1)
                        pe.wait_ge(R("yt"), c + 1)
                        if c >= 2:
                            pe.wait_ge(R("x"), c - 1)
                        for i in range(TC):
                            mm = nc.tensor.matmul(z[c % 2][:, i, :], yt[:, c % 2, i * P:(i + 1) * P], wproj[:, :],
                                                  start=True, stop=True)
                        mm.then_inc(R("z"), 1)

                @block.scalar
                def _(act):
                    for c in range(NC):
                        act.wait_ge(R("turned"), c + 1)
                        if c >= 2:
                            act.wait_ge(R("z"), c - 1)
                        nc.scalar.activation(yt[:, c % 2, :], turned[c % 2][:, :], ACT.Copy).then_inc(R("yt"), 1)

                @block.vector
                def _(dve):
                    o = InOrder(dve, R)
                    o(nc.vector.tensor_tensor(xb[:, :, :], X[:, :, :], bproj[:, :].unsqueeze(1).to_broadcast([P, NT, P]),
                                              ALU.add), "xb")
                    for c in range(NC):
                        dve.wait_ge(R("z"), c + 1)
                        o(nc.vector.tensor_tensor(X[:, TC * c:TC * (c + 1), :], z[c % 2],
                                                  xb[:, TC * c:TC * (c + 1), :], ALU.add), "x")


def delta_rule(nc, G, W):
    H, D = 4, 32
    C = P
    HALF = C // 2
    LEVELS = 6
    X, U, UT, ident, mhalf = G["X"], G["U"], G["UT"], G["ident"], G["mhalf"]
    with Stage(nc, "dr") as S:
        ww, wr = S.sb("ww", [P, P]), S.sb("wr", [P, P])
        dcol, drow, lalpha = S.sb("dcol", [P, 1]), S.sb("drow", [P, H]), S.sb("lalpha", [P, 1])
        dist, place, tail = S.sb("dist", [P, C]), S.sb("place", [P, C]), S.sb("tail", [P, H])
        halves = S.sb("halves", [P, LEVELS, C])
        above = S.sb("above", [P, 2, C])
        hmask, blk = S.sb("hmask", [P, H]), S.sb("blk", [P, P])
        layernorm(nc, G, "drln", [
            (ww[:, :], W["dr_ww"]), (wr[:, :], W["dr_wr"]), (dcol[:, :], W["dr_dcol"]),
            (drow[:, :], W["dr_drow"].to_broadcast([P, H])), (lalpha[:, :], W["dr_lalpha"]),
            (dist[:, :], W["dr_dist"]), (place[:, :], W["dr_place"]), (tail[:, :], W["dr_tail"]),
            (halves[:, :, :], W["dr_halves"]), (above[:, :, :], W["dr_above"]),
            (hmask[:, :], W["dr_hmask"]), (blk[:, :], W["dr_blk"])], False)
        rkT = S.sb("rkT", [P, T + 1])
        pack = S.sb("pack", [P, NT, 3, P])
        v = S.sb("v", [P, NT, P])
        upper = S.sb("upper", [P, 2, H, C])
        lower = S.sb("lower", [P, H, C])
        gC = S.sb("gC", [P, 1])
        gdiag = S.sb("gdiag", [P, P])
        alpha = S.sb("alpha", [P, 1])
        with Stage(nc, "drp") as R:
            sq, rk = R.sb("sq", [P, NT, H, D]), R.sb("rk", [P, NT, H, D])
            ss, rn = R.sb("ss", [P, NT * H]), R.sb("rn", [P, NT * H])
            gcol, grow = R.sb("gcol", [P, 1]), R.sb("grow", [P, H])
            gp, gt, dec = R.sb("gp", [P, C]), R.sb("gt", [P, H]), R.sb("dec", [P, H, C])
            ps = [R.ps(f"ps{n}", [P, TC, P]) for n in range(6)]
            with nc.Block() as block:
                @block.scalar
                def _(act):
                    nc.scalar.activation(gcol[:, :], dcol[:, :], ACT.Sigmoid).then_inc(R("gamma"), 1)
                    nc.scalar.activation(grow[:, :], drow[:, :], ACT.Sigmoid).then_inc(R("gamma"), 1)
                    act.wait_ge(R("gamma"), 2)
                    nc.scalar.activation(gcol[:, :], gcol[:, :], ACT.Ln).then_inc(R("log"), 1)
                    nc.scalar.activation(grow[:, :], grow[:, :], ACT.Ln).then_inc(R("log"), 1)
                    act.wait_ge(R("log"), 2)
                    nc.scalar.activation(gp[:, :], place[:, :], ACT.Exp, scale=gcol[:, 0:1]).then_inc(R("gp"), 1)
                    for h in range(H):
                        nc.scalar.activation(gt[:, h:h + 1], tail[:, h:h + 1], ACT.Exp, scale=grow[:, h:h + 1]).then_inc(R("gt"), 1)
                        nc.scalar.activation(dec[:, h, :], dist[:, :], ACT.Exp, scale=grow[:, h:h + 1]).then_inc(R("dec"), 1)
                    nc.scalar.activation(gC[:, :], gcol[:, :], ACT.Exp, scale=float(HALF)).then_inc(R("gC"), 1)
                    nc.scalar.activation(alpha[:, :], lalpha[:, :], ACT.Exp).then_inc(R("alpha"), 1)
                    for c in range(NC):
                        act.wait_ge(R("v_ps"), c + 1)
                        nc.scalar.activation(v[:, TC * c:TC * (c + 1), :], ps[4 + c % 2][:, :, :], ACT.Copy).then_inc(R("v"), 1)

                @block.gpsimd
                def _(pool):
                    pool.wait_ge(R("ss"), 2)
                    pool.tensor_tensor(rn[:, :], ss[:, :], mhalf[:, 0:NT * H], ALU.pow).then_inc(R("rn"), 1)

                @block.tensor
                def _(pe):
                    for c in range(NC):
                        if c >= 2:
                            pe.wait_ge(R("v"), c - 1)
                        for i in range(TC):
                            t = TC * c + i
                            mm = nc.tensor.matmul(ps[4 + c % 2][:, i, :], UT[:, t * P:(t + 1) * P], ww[:, :], start=True, stop=True)
                        mm.then_inc(R("v_ps"), 1)
                    pe.wait_ge(R("rk"), 1)
                    for c in range(NC):
                        for i in range(TC):
                            mm = nc.tensor.transpose(ps[c][:, i, :], rk[:, TC * c + i, :, :].rearrange("p h d -> p (h d)"),
                                                     ident[:, :])
                        mm.then_inc(R("rk_turned"), 1)
                    for c in range(NC):
                        pe.wait_ge(R("rkT"), c + 2)
                        for i in range(TC):
                            t = TC * c + i
                            mm = nc.tensor.transpose(ps[c][:, i, :], rkT[:, t * P:(t + 1) * P], ident[:, :])
                        mm.then_inc(R("wk_turned"), 1)

                @block.vector
                def _(dve):
                    o = InOrder(dve, R)
                    uh = U[:, :, :].rearrange("p t (h d) -> p t h d", h=H)
                    o(nc.vector.memset(rkT[:, 0:1], 0.0), "rkT")
                    o(nc.vector.tensor_tensor(sq[:, :, :, :], uh, uh, ALU.mult), "sq")
                    o(nc.vector.tensor_reduce(ss[:, :].rearrange("p (t h) -> p t h", h=H), sq[:, :, :, :], AX.X, ALU.add), "ss")
                    o(nc.vector.tensor_scalar(ss[:, :], ss[:, :], 1e-24, None, ALU.max), "ss")
                    dve.wait_ge(R("rn"), 1)
                    o(nc.vector.tensor_tensor(rk[:, :, :, :], uh, rn[:, :].rearrange("p (t h) -> p t h", h=H)
                                              .unsqueeze(3).to_broadcast([P, NT, H, D]), ALU.mult), "rk")
                    for c in range(NC):
                        dve.wait_ge(R("rk_turned"), c + 1)
                        o(nc.vector.tensor_copy(rkT[:, 1 + c * CH:1 + (c + 1) * CH],
                                                ps[c][:, :, :].rearrange("p i f -> p (i f)")), "rkT")
                    dve.wait_ge(R("gp"), 1)
                    o(nc.vector.tensor_tensor(pack[:, :, 2, :], rkT[:, 1:T + 1].rearrange("p (t i) -> p t i", i=C),
                                              gp[:, :].unsqueeze(1).to_broadcast([P, NT, C]), ALU.mult), "rkg")
                    dve.wait_ge(R("gt"), H)
                    for c in range(NC):
                        dve.wait_ge(R("wk_turned"), c + 1)
                        o(nc.vector.tensor_copy(pack[:, TC * c:TC * (c + 1), 0, :], ps[c][:, :, :]), "wk")
                    for h in range(H):
                        o(nc.vector.tensor_scalar(pack[:, :, 1, h * D:(h + 1) * D], pack[:, :, 0, h * D:(h + 1) * D],
                                                  gt[:, h:h + 1], None, ALU.mult), "wkg")
                    dve.wait_ge(R("gC"), 1)
                    o(nc.vector.tensor_scalar(gdiag[:, :], ident[:, :], gC[:, 0:1], None, ALU.mult), "gdiag")
                    dve.wait_ge(R("dec"), H)
                    for s in range(2):
                        o(nc.vector.tensor_tensor(upper[:, s, :, :], dec[:, :, :],
                                                  above[:, s, :].unsqueeze(1).to_broadcast([P, H, C]), ALU.mult), "upper")
                    o(nc.vector.tensor_tensor(lower[:, :, :], dec[:, :, :],
                                              halves[:, 0, :].unsqueeze(1).to_broadcast([P, H, C]), ALU.mult), "lower")

        out = S.sb("out", [P, NT, P])
        with Stage(nc, "drr") as R:
            wkm = [R.sb(f"wkm{t}", [P, H, C]) for t in range(2)]
            mt = [R.sb(f"mt{t}", [P, H, C]) for t in range(2)]
            x0 = [R.sb(f"x0{t}", [P, H, C]) for t in range(2)]
            xt0 = [R.sb(f"xt0{t}", [P, H, C]) for t in range(2)]
            intra = [R.sb(f"intra{t}", [P, H, C]) for t in range(2)]
            A = [R.sb(f"A{t}", [P, H, C]) for t in range(2)]
            AT = [R.sb(f"AT{t}", [P, H, C]) for t in range(2)]
            ma = [R.sb(f"ma{t}", [P, H, C]) for t in range(2)]
            pk = [R.sb(f"pk{t}", [P, 3, P]) for t in range(2)]
            nwk = [R.sb(f"nwk{t}", [P, C]) for t in range(2)]
            av = [R.sb(f"av{t}", [P, P]) for t in range(2)]
            vn = [R.sb(f"vn{t}", [P, P]) for t in range(2)]
            state = R.sb("state", [P, P])
            gram = R.ps("gram", [P, H, 256])
            pma = [R.ps(f"pma{t}", [P, H, C]) for t in range(2)]
            pa = [R.ps(f"pa{t}", [P, H, C]) for t in range(2)]
            pat = [R.ps(f"pat{t}", [P, H, C]) for t in range(2)]
            G_WIDTH = C + 1
            with nc.Block() as block:
                @block.gpsimd
                def _(pool):
                    pool.sem_inc(R("gram"), 2)
                    with pool.Fori(0, NT // 2) as g:
                        for t in range(2):
                            pool.wait_ge(R("gram"), 2 * g + t + 1)
                            pool.tensor_tensor(wkm[t][:, :, :],
                                               rkT[:, bass.ds(2 * g * C + t * C, C)].unsqueeze(1).to_broadcast([P, H, C]),
                                               hmask[:, :].unsqueeze(2).to_broadcast([P, H, C]), ALU.mult).then_inc(R("wkm"), 1)

                @block.tensor
                def _(pe):
                    with pe.Fori(0, NT // 2) as g:
                        for t in range(2):
                            pe.wait_ge(R("wkm"), 2 * g + t + 1)
                            pe.wait_ge(R("gram_read"), 2 * g + t + 1)
                            if t == 0:
                                pe.wait_ge(R("state"), 4 * g + 1)
                            for h in range(H):
                                mm = nc.tensor.matmul(gram[:, h, 0:G_WIDTH], wkm[t][:, h, :],
                                                      rkT[:, bass.ds(2 * g * C + t * C, G_WIDTH)], start=True, stop=True)
                            mm.then_inc(R("gram"), 1)
                        for s in range(1, LEVELS):
                            for t in range(2):
                                pe.wait_ge(R("AT"), 2 * LEVELS * g + 2 * (s - 1) + t + 1)
                                if s == 1:
                                    pe.wait_ge(R("A"), 2 * (LEVELS - 1) * g + t + 1)
                                    pe.wait_ge(R("mt"), 2 * g + t + 1)
                                    pe.wait_ge(R("out"), 2 * g + t + 1)
                                for h in range(H):
                                    mm = nc.tensor.matmul(pma[t][:, h, :], mt[t][:, h, :], A[t][:, h, :],
                                                          start=True, stop=True)
                                mm.then_inc(R("pma"), 1)
                            for t in range(2):
                                pe.wait_ge(R("ma"), 2 * (LEVELS - 1) * g + 2 * (s - 1) + t + 1)
                                if s < LEVELS - 1:
                                    for h in range(H):
                                        mm = nc.tensor.matmul(pa[t][:, h, :], AT[t][:, h, :], ma[t][:, h, :],
                                                              start=True, stop=True)
                                    mm.then_inc(R("pa"), 1)
                                for h in range(H):
                                    mm = nc.tensor.matmul(pat[t][:, h, :], ma[t][:, h, :], AT[t][:, h, :],
                                                          start=True, stop=True)
                                mm.then_inc(R("pat"), 1)
                        for t in range(2):
                            pe.wait_ge(R("AT"), 2 * LEVELS * g + 2 * (LEVELS - 1) + t + 1)
                            pe.wait_ge(R("pk"), 2 * g + t + 1)
                            for h in range(H):
                                mm = nc.tensor.matmul(pma[t][h * D:(h + 1) * D, 0, :], pk[t][:, 0, h * D:(h + 1) * D],
                                                      AT[t][:, h, :], start=True, stop=True)
                            mm.then_inc(R("wk_ps"), 1)
                            for h in range(H):
                                mm = nc.tensor.matmul(pa[t][:, 0, h * D:(h + 1) * D], AT[t][:, h, :],
                                                      v[:, bass.ds(2 * g + t, 1), h * D:(h + 1) * D],
                                                      start=True, stop=True)
                            mm.then_inc(R("av_ps"), 1)
                        for t in range(2):
                            pe.wait_ge(R("nwk"), 2 * g + t + 1)
                            for q in range(2):
                                lo, hi = q * HALF, (q + 1) * HALF
                                pe.wait_ge(R("state"), 4 * g + 2 * t + q + 1)
                                nc.tensor.matmul(pat[t][lo:hi, 1, :], nwk[t][:, lo:hi], state[:, :], start=True,
                                                 stop=True).then_inc(R("ws_ps"), 1)
                                nc.tensor.matmul(pma[t][lo:hi, 0, :], pk[t][:, 2, lo:hi], state[:, :], start=True, stop=False)
                                nc.tensor.matmul(gram[:, 2 * q, 0:P], gdiag[:, :], state[:, :], start=True, stop=False)
                                pe.wait_ge(R("vn"), 4 * g + 2 * t + q + 1)
                                nc.tensor.matmul(gram[:, 2 * q, 0:P], pk[t][lo:hi, 1, :], vn[t][lo:hi, :], start=False,
                                                 stop=True).then_inc(R("ds_ps"), 1)
                            for h in range(H):
                                mm = nc.tensor.matmul(pma[t][:, 0, h * D:(h + 1) * D], intra[t][:, h, :],
                                                      vn[t][:, h * D:(h + 1) * D], start=False, stop=h == H - 1)
                            mm.then_inc(R("out_ps"), 1)

                @block.scalar
                def _(act):
                    with act.Fori(0, NT // 2) as g:
                        for t in range(2):
                            act.wait_ge(R("out_ps"), 2 * g + t + 1)
                            nc.scalar.activation(pk[t][:, :, :], pack[:, bass.ds(2 * g + t, 1), :, :], ACT.Copy).then_inc(R("pk"), 1)
                        for t in range(2):
                            act.wait_ge(R("wk_ps"), 2 * g + t + 1)
                            nc.scalar.activation(nwk[t][:, :], pma[t][:, 0, :], ACT.Copy, scale=-1.0).then_inc(R("nwk"), 1)
                        for t in range(2):
                            act.wait_ge(R("out_ps"), 2 * g + t + 3)
                            nc.scalar.activation(out[:, bass.ds(2 * g + t, 1), :], pma[t][:, 0:1, :], ACT.Copy).then_inc(R("out"), 1)

                @block.vector
                def _(dve):
                    dve.sem_inc(R("gram_read"), 1)
                    dve.sem_inc(R("out_ps"), 2)
                    dve.sem_inc(R("out"), 2)
                    nc.vector.memset(state[:, :], 0.0).then_inc(R("state"), 1)
                    with dve.Fori(0, NT // 2) as g:
                        o = InOrder(dve, R, g, {"ma": 2 * (LEVELS - 1), "A": 2 * (LEVELS - 1),
                                                "AT": 2 * LEVELS, "av": 2, "vn": 4, "state": 4},
                                    {"A": 2, "AT": 2, "state": 1})
                        for t in range(2):
                            dve.wait_ge(R("out_ps"), 2 * g + t + 1)
                            dve.wait_ge(R("gram"), 2 * g + t + 3)
                            wk = gram[:, :, 0:C]
                            nc.vector.tensor_tensor(x0[t][:, :, :], wk, lower[:, :, :], ALU.mult).then_inc(R("x0"), 1)
                            nc.vector.tensor_tensor(xt0[t][:, :, :], wk, upper[:, 0, :, :], ALU.mult).then_inc(R("xt0"), 1)
                            nc.vector.tensor_tensor(mt[t][:, :, :], wk, upper[:, 1, :, :], ALU.mult).then_inc(R("mt"), 1)
                            nc.vector.tensor_tensor(intra[t][:, :, :], gram[:, :, 1:G_WIDTH], upper[:, 1, :, :],
                                                    ALU.mult).then_inc(R("gram_read"), 1)
                            one = ident[:, :].unsqueeze(1).to_broadcast([P, H, C])
                            dve.wait_ge(R("x0"), 2 * g + t + 1)
                            nc.vector.tensor_tensor(A[t][:, :, :], one, x0[t][:, :, :], ALU.subtract).then_inc(R("A"), 1)
                            dve.wait_ge(R("xt0"), 2 * g + t + 1)
                            nc.vector.tensor_tensor(AT[t][:, :, :], one, xt0[t][:, :, :], ALU.subtract).then_inc(R("AT"), 1)
                        dve.wait_ge(R("gram_read"), 2 * g + 3)
                        dve.wait_ge(R("mt"), 2 * g + 2)
                        for s in range(1, LEVELS):
                            for t in range(2):
                                dve.wait_ge(R("pma"), 2 * (LEVELS - 1) * g + 2 * (s - 1) + t + 1)
                                o(nc.vector.tensor_tensor(ma[t][:, :, :], pma[t][:, :, :],
                                                          halves[:, s, :].unsqueeze(1).to_broadcast([P, H, C]),
                                                          ALU.mult), "ma")
                            for t in range(2):
                                if s < LEVELS - 1:
                                    dve.wait_ge(R("pa"), 2 * (LEVELS - 2) * g + 2 * (s - 1) + t + 1)
                                    o(nc.vector.tensor_tensor(A[t][:, :, :], A[t][:, :, :], pa[t][:, :, :], ALU.subtract), "A")
                                dve.wait_ge(R("pat"), 2 * (LEVELS - 1) * g + 2 * (s - 1) + t + 1)
                                o(nc.vector.tensor_tensor(AT[t][:, :, :], AT[t][:, :, :], pat[t][:, :, :], ALU.subtract), "AT")
                        for t in range(2):
                            dve.wait_ge(R("av_ps"), 2 * g + t + 1)
                            o(nc.vector.tensor_copy(av[t][:, :], pa[t][:, 0, :]), "av")
                        for t in range(2):
                            for q in range(2):
                                lo, hi = q * HALF, (q + 1) * HALF
                                dve.wait_ge(R("ws_ps"), 4 * g + 2 * t + q + 1)
                                o(nc.vector.tensor_tensor(vn[t][lo:hi, :], pat[t][lo:hi, 1, :], av[t][lo:hi, :], ALU.add), "vn")
                                dve.wait_ge(R("ds_ps"), 4 * g + 2 * t + q + 1)
                                o(nc.vector.tensor_tensor(state[:, :], gram[:, 2 * q, 0:P], blk[:, :], ALU.mult), "state")

        with Stage(nc, "dro") as R:
            turned = [R.ps(f"turned{n}", [P, CH]) for n in range(2)]
            z = [R.ps(f"z{n}", [P, TC, P]) for n in range(2)]
            ot = R.sb("ot", [P, 2, CH])
            xu = R.sb("xu", [P, NT, P])
            with nc.Block() as block:
                @block.tensor
                def _(pe):
                    def turn(c):
                        for i in range(TC):
                            mm = nc.tensor.transpose(turned[c % 2][:, i * P:(i + 1) * P], out[:, TC * c + i, :], ident[:, :])
                        mm.then_inc(R("turned"), 1)

                    turn(0)
                    for c in range(NC):
                        if c + 1 < NC:
                            if c:
                                pe.wait_ge(R("ot"), c)
                            turn(c + 1)
                        pe.wait_ge(R("ot"), c + 1)
                        if c >= 2:
                            pe.wait_ge(R("x"), c - 1)
                        for i in range(TC):
                            mm = nc.tensor.matmul(z[c % 2][:, i, :], ot[:, c % 2, i * P:(i + 1) * P], wr[:, :],
                                                  start=True, stop=True)
                        mm.then_inc(R("z"), 1)

                @block.scalar
                def _(act):
                    for c in range(NC):
                        act.wait_ge(R("turned"), c + 1)
                        if c >= 2:
                            act.wait_ge(R("z"), c - 1)
                        nc.scalar.activation(ot[:, c % 2, :], turned[c % 2][:, :], ACT.Copy,
                                             scale=alpha[:, 0:1]).then_inc(R("ot"), 1)

                @block.vector
                def _(dve):
                    o = InOrder(dve, R)
                    o(nc.vector.tensor_tensor(xu[:, :, :], X[:, :, :], U[:, :, :], ALU.add), "xu")
                    for c in range(NC):
                        dve.wait_ge(R("z"), c + 1)
                        o(nc.vector.tensor_tensor(X[:, TC * c:TC * (c + 1), :], z[c % 2][:, :, :],
                                                  xu[:, TC * c:TC * (c + 1), :], ALU.add), "x")


def bilinear_attention(nc, G, W):
    NH, D = 16, 64
    PAIRS = NH // 2
    UQ = 2
    NU = NT // UQ
    NG = NT // 2
    SCALE = D ** -0.5
    X, U, UT, ident = G["X"], G["U"], G["UT"], G["ident"]
    STQ = ((0, 1), (2, 0))
    STK = ((0, 0), (1, 1), (0, 2))
    PASSES = ((0, 0), (0, 1), (1, 2))
    LOADS = 2 * (len(STQ) + len(STK)) + 1
    parts_of = nc.dram_tensor("ba_parts", (PAIRS, P, 2, 3, T), BF16).ap()
    v_of = nc.dram_tensor("ba_v", (PAIRS, 2, P, NT, D), F32).ap()
    with Stage(nc, "ba") as S:
        gain = S.sb("gain", [P, 1])
        wo = S.sb("wo", [P, NH, P])
        with Stage(nc, "bap") as R:
            cos, sin = R.sb("cos", [P, T]), R.sb("sin", [P, T])
            wp = [R.sb(f"wp{n}", [P, 6, P]) for n in range(2)]
            layernorm(nc, G, "baln", [
                (gain[:, :], W["ba_gain"]), (cos[:, :], W["ba_cos"]), (sin[:, :], W["ba_sin"]),
                (wo[:, :, :], W["ba_wo"]), (wp[0][:, :, :], W["ba_w"][0]), (wp[1][:, :, :], W["ba_w"][1])],
                True, gain=gain[:, 0:1])
            split_heads(nc, R, G, W, PAIRS, cos, sin, wp, parts_of, v_of)
        v = U[:, :, :].rearrange("p (h t) (a d) -> p h (t a) d", h=2, d=D)
        sq = S.sb("sq", [P, 2, 2, T], BF16)
        sk = S.sb("sk", [P, 2, 3, T], BF16)
        pb = [S.sb(f"pb{n}", [P, UQ, T]) for n in range(2)]
        pt = S.sb("pt", [P, 4, CH])
        osb = S.sb("osb", [P, UQ * P])
        most, nm = S.sb("most", [P, 2]), S.sb("nm", [P, 2])
        scale = S.sb("scale", [P, 1])
        rs = S.sb("rs", [P, 2, UQ, 2])
        rsum, rinv = S.sb("rsum", [P, UQ]), S.sb("rinv", [P, UQ])
        sc = S.ps("sc", [P, 4, CH])
        tr = [S.ps(f"tr{n}", [P, CH]) for n in range(2)]
        ops = S.ps("ops", [P, CH])
        yps = S.ps("yps", [P, CH])
        with nc.Block() as block:
            @block.sync
            def _(sp):
                def load(p, hh):
                    rows = slice(hh * D, (hh + 1) * D)
                    for s, (stack, order) in enumerate(((sq, STQ), (sk, STK))):
                        for n in range(len(order)):
                            for half in range(2):
                                sp.dma_start(stack[half * D:(half + 1) * D, hh, n, :],
                                             parts_of[p, rows, s, order[n][half], :]).then_inc(S(f"head{hh}"), 16)
                    sp.dma_start(v[:, hh, :, :], v_of[p, hh]).then_inc(S(f"head{hh}"), 16)

                for hh in range(2):
                    load(0, hh)
                with sp.Fori(0, PAIRS - 1) as p:
                    for hh in range(2):
                        sp.wait_ge(S("values"), NG * NU * (2 * p + hh + 1) + 4)
                        sp.sem_inc(S("paced"), 1)
                        load(p + 1, hh)

            @block.tensor
            def _(pe):
                def scores(un, hh, u, t, half):
                    for c in (2 * half, 2 * half + 1):
                        if c % 2 == 0:
                            pe.wait_ge(S("exp"), 4 * un + 2 * t + half + 1)
                        for n, (a, b) in enumerate(PASSES):
                            mm = nc.tensor.matmul(sc[:, c, :], sq[:, hh, a, bass.ds(u * UQ * P + t * P, P)],
                                                  sk[:, hh, b, c * CH:(c + 1) * CH], start=n == 0, stop=n == 2)
                        if c % 2:
                            mm.then_inc(S("scores"), 1)

                def turn(un, par, g):
                    if g == 0:
                        pe.wait_ge(S("exp"), 4 * un + 6)
                    pe.wait_ge(S("pt_act" if g % 2 == 0 else "pt_dve"), 4 * un + g // 2 + 1)
                    for k in range(2):
                        for t in range(UQ):
                            mm = nc.tensor.transpose(tr[g % 2][:, (2 * k + t) * P:(2 * k + t + 1) * P],
                                                     pb[par][:, t, (2 * g + k) * P:(2 * g + k + 1) * P], ident[:, :])
                    mm.then_inc(S("turned"), 1)

                def values(un, hh, g):
                    if g == 0:
                        pe.wait_ge(S("osb"), un + 1)
                    pe.wait_ge(S("pt_act" if g % 2 == 0 else "pt_dve"), 4 * un + g // 2 + 2)
                    for k in range(2):
                        mm = nc.tensor.matmul(ops[k * D:(k + 1) * D, 0:UQ * P], v[:, hh, 2 * g + k, :],
                                              pt[:, g % 4, k * UQ * P:(k + 1) * UQ * P], start=g == 0, stop=g == NG - 1)
                    mm.then_inc(S("values"), 1)

                def output(un, head):
                    pe.wait_ge(S("osb"), un + 2)
                    pe.wait_ge(S("x"), UQ * un + 2)
                    for t in range(UQ):
                        mm = nc.tensor.matmul(yps[:, t * P:(t + 1) * P], osb[:, t * P:(t + 1) * P],
                                              wo[:, bass.ds(head, 1), :], start=True, stop=True)
                    mm.then_inc(S("y"), 1)

                def step(now, before, last):
                    for t in range(UQ):
                        a = NG // 2 * t
                        if now:
                            scores(*now, t, 0)
                            scores(*now, t, 1)
                        if t == 0 and last:
                            values(last[0], last[1], NG - 1)
                        if before:
                            un, hh, par = before
                            turn(un, par, a)
                            turn(un, par, a + 1)
                            if t:
                                values(un, hh, a - 1)
                        if t and last:
                            output(last[0], last[2])
                        if before:
                            values(un, hh, a)
                            turn(un, par, a + 2)
                            values(un, hh, a + 1)
                            turn(un, par, a + 3)
                            values(un, hh, a + 2)

                def inside(base, hh, head):
                    with pe.Fori(0, NU // 2 - 1) as w:
                        step((base + 2 * w + 2, hh, 2 * w + 2), (base + 2 * w + 1, hh, 1), (base + 2 * w, hh, head))
                        step((base + 2 * w + 3, hh, 2 * w + 3), (base + 2 * w + 2, hh, 0), (base + 2 * w + 1, hh, head))

                def start(base, hh, head):
                    step((base, hh, 0), (base - 1, 1 - hh, 1), (base - 2, 1 - hh, head - 1))
                    step((base + 1, hh, 1), (base, hh, 0), (base - 1, 1 - hh, head - 1))

                def pair(p, more):
                    base, head = 2 * NU * p, 2 * p
                    inside(base, 0, head)
                    pe.wait_ge(S("head1"), 16 * LOADS * (p + 1))
                    start(base + NU, 1, head + 1)
                    inside(base + NU, 1, head + 1)
                    if more:
                        pe.wait_ge(S("head0"), 16 * LOADS * (p + 2))
                        start(base + 2 * NU, 0, head + 2)

                pe.wait_ge(S("head0"), 16 * LOADS)
                step((0, 0, 0), None, None)
                step((1, 0, 1), (0, 0, 0), None)
                with pe.Fori(0, PAIRS - 1) as p:
                    pair(p, True)
                pair(PAIRS - 1, False)
                step(None, (NH * NU - 1, 1, 1), (NH * NU - 2, 1, NH - 1))
                values(NH * NU - 1, 1, NG - 1)
                output(NH * NU - 1, NH - 1)

            @block.scalar
            def _(act):
                act.sem_inc(S("exp"), 2)
                act.sem_inc(S("pt_act"), 1)

                def exponentials(un, par, t, half):
                    if half == 0:
                        act.wait_ge(S("nm"), UQ * un + t + 1)
                        if t == 0:
                            act.wait_ge(S("turned"), NG * un + 1)
                    nc.scalar.activation(pb[par][:, t, half * 1024:(half + 1) * 1024],
                                         sc[:, 2 * half:2 * half + 2, :].rearrange("p a b -> p (a b)"), ACT.Exp,
                                         bias=nm[:, t:t + 1], scale=SCALE,
                                         accum_out=rs[:, par, t, half:half + 1]).then_inc(S("exp"), 1)

                def copies(un, g):
                    act.wait_ge(S("turned"), NG * un + g + 10)
                    act.wait_ge(S("values"), NG * un + g + 1)
                    nc.scalar.activation(pt[:, g % 4, :], tr[g % 2][:, :], ACT.Copy).then_inc(S("pt_act"), 1)

                def sums(un):
                    act.wait_ge(S("values"), NG * un + NG + 4)
                    act.wait_ge(S("y"), un + 1)
                    nc.scalar.activation(osb[:, :], ops[:, 0:UQ * P], ACT.Copy).then_inc(S("osb"), 1)

                def step(now, before, last):
                    for t in range(UQ):
                        if t == 0 and last is not None:
                            sums(last)
                        if before is not None:
                            copies(before, NG // 2 * t)
                        if now:
                            exponentials(*now, t, 0)
                        if before is not None:
                            copies(before, NG // 2 * t + 2)
                        if now:
                            exponentials(*now, t, 1)

                def inside(base):
                    with act.Fori(0, NU // 2 - 1) as w:
                        step((base + 2 * w + 2, 0), base + 2 * w + 1, base + 2 * w)
                        step((base + 2 * w + 3, 1), base + 2 * w + 2, base + 2 * w + 1)

                def start(base):
                    step((base, 0), base - 1, base - 2)
                    step((base + 1, 1), base, base - 1)

                def pair(p, more):
                    base = 2 * NU * p
                    inside(base)
                    start(base + NU)
                    inside(base + NU)
                    if more:
                        start(base + 2 * NU)

                step((0, 0), None, None)
                step((1, 1), 0, None)
                with act.Fori(0, PAIRS - 1) as p:
                    pair(p, True)
                pair(PAIRS - 1, False)
                step(None, NH * NU - 1, NH * NU - 2)
                sums(NH * NU - 1)

            @block.vector
            def _(dve):
                dve.sem_inc(S("turned"), NG + 1)
                dve.sem_inc(S("values"), 4)
                dve.sem_inc(S("pt_dve"), 1)
                dve.sem_inc(S("osb"), 1)
                dve.sem_inc(S("y"), 1)
                dve.sem_inc(S("x"), 2)

                def maximum(un, t, half):
                    dve.wait_ge(S("scores"), 4 * un + 2 * t + half + 1)
                    nc.vector.tensor_reduce(most[:, half:half + 1], sc[:, 2 * half:2 * half + 2, :], AX.XY,
                                            ALU.max).then_inc(S("most"), 1)

                def bias(un, t):
                    dve.wait_ge(S("most"), 4 * un + 2 * t + 2)
                    nc.vector.scalar_tensor_tensor(out=nm[:, t:t + 1], in0=most[:, 0:1], scalar=most[:, 1:2],
                                                   in1=scale[:, :], op0=ALU.max, op1=ALU.mult).then_inc(S("nm"), 1)
                    dve.wait_ge(S("nm"), UQ * un + t + 1)
                    dve.sem_inc(S("paced_dve"), 1)

                def copies(un, g):
                    dve.wait_ge(S("turned"), NG * un + g + 10)
                    dve.wait_ge(S("values"), NG * un + g + 1)
                    nc.vector.tensor_copy(pt[:, g % 4, :], tr[g % 2][:, :]).then_inc(S("pt_dve"), 1)

                def inverse(un, par):
                    dve.wait_ge(S("exp"), 4 * un + 6)
                    o = InOrder(dve, S, un)
                    o(nc.vector.tensor_tensor(rsum[:, :], rs[:, par, :, 0], rs[:, par, :, 1], ALU.add), "rsum")
                    o(nc.vector.reciprocal(rinv[:, :], rsum[:, :]), "rinv")
                    dve.sem_inc(S("paced_dve"), 1)

                def add(un, u):
                    dve.wait_ge(S("y"), un + 2)
                    for t in range(UQ):
                        tile = X[:, bass.ds(UQ * u + t, 1), :]
                        nc.vector.scalar_tensor_tensor(out=tile, in0=yps[:, t * P:(t + 1) * P].unsqueeze(1),
                                                       scalar=rinv[:, t:t + 1], in1=tile, op0=ALU.mult,
                                                       op1=ALU.add).then_inc(S("x"), 1)
                    dve.wait_ge(S("x"), UQ * un + UQ + 2)
                    dve.sem_inc(S("paced_dve"), 1)

                def step(now, before, last):
                    for t in range(UQ):
                        a = NG // 2 * t
                        if now is not None:
                            maximum(now, t, 0)
                            maximum(now, t, 1)
                            bias(now, t)
                        if before:
                            copies(before[0], a + 1)
                            copies(before[0], a + 3)
                    if last:
                        add(*last)
                    if before:
                        inverse(*before)

                def inside(base):
                    with dve.Fori(0, NU // 2 - 1) as w:
                        step(base + 2 * w + 2, (base + 2 * w + 1, 1), (base + 2 * w, 2 * w))
                        step(base + 2 * w + 3, (base + 2 * w + 2, 0), (base + 2 * w + 1, 2 * w + 1))

                def start(base):
                    step(base, (base - 1, 1), (base - 2, NU - 2))
                    step(base + 1, (base, 0), (base - 1, NU - 1))

                def pair(p, more):
                    base = 2 * NU * p
                    inside(base)
                    start(base + NU)
                    inside(base + NU)
                    if more:
                        start(base + 2 * NU)

                nc.vector.memset(scale[:, :], -SCALE).then_inc(S("const"), 1)
                dve.wait_ge(S("const"), 1)
                step(0, None, None)
                step(1, (0, 0), None)
                with dve.Fori(0, PAIRS - 1) as p:
                    pair(p, True)
                pair(PAIRS - 1, False)
                step(None, (NH * NU - 1, 1), (NH * NU - 2, NU - 2))
                add(NH * NU - 1, NU - 1)


def split_heads(nc, S, G, W, PAIRS, cos, sin, wp, parts_of, v_of):
    UT, D = G["UT"], P // 2
    SLOTS = 4
    LAST = 2 * NC
    rot = S.sb("rot", [P, 4, CH])
    qk = S.sb("qk", [P, 2, 2, CH])
    left = S.sb("left", [P, 2, 2, CH])
    parts = S.sb("parts", [P, SLOTS, 2, 3, CH], BF16)
    v = S.sb("v", [P, SLOTS, 2, TC, D])
    proj = S.ps("proj", [P, 4, CH])
    kt = [S.ps(f"kt{n}", [P, CH]) for n in range(2)]
    v_ps = [S.ps(f"vps{n}", [P, CH]) for n in range(2)]
    with nc.Block() as block:
        @block.sync
        def _(sp):
            def round_(g, more):
                for j in range(LAST):
                    k, s, c = LAST * g + j, j // NC, j % NC
                    sp.wait_ge(S("v"), k + 3)
                    sp.sem_inc(S("paced"), 1)
                    sp.dma_start(v_of[2 * g + s, :, :, TC * c:TC * (c + 1), :].rearrange("h p t d -> p h t d"),
                                 v[:, j % SLOTS, :, :, :]).then_inc(S(f"out{j % SLOTS}"), 16)
                    sp.wait_ge(S("low"), 2 * k + 6)
                    sp.sem_inc(S("paced"), 1)
                    sp.dma_start(parts_of[2 * g + s, :, :, :, c * CH:(c + 1) * CH],
                                 parts[:, j % SLOTS, :, :, :]).then_inc(S(f"out{j % SLOTS}"), 16)
                    if more and c == NC - 1:
                        sp.wait_ge(S("kt"), k + 1)
                        sp.sem_inc(S("paced"), 1)
                        sp.dma_start(wp[s][:, :, :], W["ba_w"][2 * g + s + 2]).then_inc(S(f"weights{s}"), 16)

            with sp.Fori(0, PAIRS // 2 - 1) as g:
                round_(g, True)
            round_(PAIRS // 2 - 1, False)
            for m in range(SLOTS):
                sp.wait_ge(S(f"out{m}"), 32 * (NC * PAIRS // SLOTS + 1))

        @block.tensor
        def _(pe):
            with pe.Fori(0, PAIRS // 2) as g:
                for j in range(LAST + 1):
                    k, s, c = LAST * g + j, j // NC, j % NC
                    if j < LAST:
                        if c == 0:
                            pe.wait_ge(S(f"weights{s}"), 16 * (g + 1))
                        for n in range(4):
                            pe.wait_ge(S("rotated"), 4 * k + n + 1)
                            nc.tensor.matmul(proj[:, n, :], wp[s][:, n, :], UT[:, c * CH:(c + 1) * CH], start=True,
                                             stop=True).then_inc(S("proj"), 1)
                        pe.wait_ge(S("v"), k + 1)
                        for i in range(TC):
                            t = TC * c + i
                            mm = nc.tensor.matmul(v_ps[j % 2][:, i * P:(i + 1) * P], UT[:, t * P:(t + 1) * P],
                                                  wp[s][:, 4, :], start=True, stop=True)
                        mm.then_inc(S("v_ps"), 1)
                    if j:
                        pe.wait_ge(S("qk"), k)
                        pe.wait_ge(S("kleft"), k)
                        nc.tensor.matmul(kt[(j - 1) % 2][:, :], wp[(j - 1) // NC][:, 5, :], qk[:, (j - 1) % 2, 1, :],
                                         start=True, stop=True).then_inc(S("kt"), 1)

        @block.scalar
        def _(act):
            act.sem_inc(S("v"), 2)
            copy = nc.scalar.activation
            with act.Fori(0, PAIRS // 2) as g:
                for j in range(LAST + 1):
                    k = LAST * g + j
                    if j < LAST:
                        act.wait_ge(S("v_ps"), k + 1)
                        act.wait_ge(S(f"out{j % SLOTS}"), 32 * (LAST // SLOTS * g + j // SLOTS + 1))
                        copy(v[:, j % SLOTS, :, :, :],
                             v_ps[j % 2][:, :].rearrange("p (t h d) -> p h t d", h=2, d=D), ACT.Copy).then_inc(S("v"), 1)
                    if j:
                        act.wait_ge(S("kt"), k)
                        copy(parts[:, (j - 1) % SLOTS, 1, 0, :], kt[(j - 1) % 2][:, :], ACT.Copy).then_inc(S("kh"), 1)
                    if j < LAST:
                        act.wait_ge(S("qk"), k + 1)
                        copy(parts[:, j % SLOTS, 0, 0, :], qk[:, j % 2, 0, :], ACT.Copy).then_inc(S("qh"), 1)
                    if j:
                        for n, name in enumerate(("qleft", "kleft")):
                            act.wait_ge(S(name), k + 2 * n)
                            copy(parts[:, (j - 1) % SLOTS, n, 1, :], left[:, (j - 1) % 2, n, :],
                                 ACT.Copy).then_inc(S("middle"), 1)

        @block.gpsimd
        def _(pool):
            with pool.Fori(0, PAIRS // 2) as g:
                for j in range(LAST):
                    for n in range(2):
                        pool.wait_ge(S("middle"), 2 * (LAST * g + j) + n + 1)
                        pool.tensor_tensor(parts[:, j % SLOTS, n, 2, :], left[:, j % 2, n, :],
                                           parts[:, j % SLOTS, n, 1, :], ALU.subtract).then_inc(S("low"), 1)

        @block.vector
        def _(dve):
            dve.sem_inc(S("rotated"), 4)
            dve.sem_inc(S("kleft"), 2)
            dve.sem_inc(S("low"), 4)
            for m in range(SLOTS):
                dve.sem_inc(S(f"out{m}"), 32)
            for s in range(2):
                dve.sem_inc(S(f"weights{s}"), 16)
            with dve.Fori(0, PAIRS // 2) as g:
                for j in range(LAST + 1):
                    k, c = LAST * g + j, j % NC
                    if j < LAST:
                        for n in range(4):
                            dve.wait_ge(S("proj"), 4 * k + n + 1)
                            nc.vector.tensor_tensor(rot[:, n, :], proj[:, n, :], (cos, sin)[n % 2][:, c * CH:(c + 1) * CH],
                                                    ALU.mult).then_inc(S("rotated"), 1)
                        dve.wait_ge(S("rotated"), 4 * k + 8)
                        nc.vector.tensor_tensor(qk[:, j % 2, :, :], rot[:, 0:4:2, :], rot[:, 1:4:2, :],
                                                ALU.add).then_inc(S("qk"), 1)
                        dve.wait_ge(S("qk"), k + 1)
                    if j:
                        m, par = (j - 1) % SLOTS, (j - 1) % 2
                        dve.wait_ge(S("qh"), k)
                        dve.wait_ge(S("low"), 2 * k)
                        nc.vector.tensor_tensor(left[:, par, 0, :], qk[:, par, 0, :], parts[:, m, 0, 0, :],
                                                ALU.subtract).then_inc(S("qleft"), 1)
                        dve.wait_ge(S("kh"), k)
                        nc.vector.tensor_tensor(left[:, par, 1, :], kt[par][:, :], parts[:, m, 1, 0, :],
                                                ALU.subtract).then_inc(S("kleft"), 1)
                        dve.wait_ge(S("qleft"), k)


def program(nc, W, out, first, last):
    with ExitStack() as stack:
        def sb(name, shape, dt=F32):
            return stack.enter_context(nc.sbuf_tensor(name, shape, dt))

        G = {"X": sb("X", [P, NT, P]), "U": sb("U", [P, NT, P]), "UT": sb("UT", [P, T]),
             "ident": sb("ident", [P, P]), "identb": sb("identb", [P, P], BF16), "mhalf": sb("mhalf", [P, NT * 4]),
             "w1": sb("w1", [P, 4 * P]), "w2": sb("w2", [P, 4, P]), "b1": sb("b1", [P, 4]), "hb2": sb("hb2", [P, P]),
             "ffn_gain": sb("ffn_gain", [P, 1]), "ffn_shift": sb("ffn_shift", [P, 1])}
        x_view = W["x"].rearrange("(i p) f -> p i f", p=P)
        out_view = out.rearrange("(i p) f -> p i f", p=P)
        with Stage(nc, "start") as S:
            with nc.Block() as block:
                @block.sync
                def _(sp):
                    sp.dma_start(G["X"][:, :, :], x_view).then_inc(S("here"), 16)
                    sp.dma_start(G["ident"][:, :], W["ident"]).then_inc(S("ident"), 16)
                    sp.dma_start(G["ffn_gain"][:, :], W["ffn_gain"]).then_inc(S("here"), 16)
                    sp.dma_start(G["ffn_shift"][:, :], W["ffn_shift"]).then_inc(S("here"), 16)
                    sp.wait_ge(S("here"), 48)

                @block.gpsimd
                def _(pool):
                    pool.memset(G["mhalf"][:, :], -0.5).then_inc(S("half"), 1)

                @block.vector
                def _(dve):
                    dve.wait_ge(S("ident"), 16)
                    nc.vector.tensor_copy(G["identb"][:, :], G["ident"][:, :]).then_inc(S("identb"), 1)
        stages = [
            lambda: linear_attention(nc, G, W),
            lambda: ffn(nc, G, W, "f1", True),
            lambda: delta_rule(nc, G, W),
            lambda: ffn(nc, G, W, "f2", first == 4),
            lambda: causal_attention(nc, G, W),
            lambda: experts(nc, G, W, "m1"),
            lambda: bilinear_attention(nc, G, W),
            lambda: experts(nc, G, W, "m2"),
        ]
        for stage in stages[first - 1:last]:
            stage()
        with Stage(nc, "end") as S:
            with nc.Block() as block:
                @block.sync
                def _(sp):
                    sp.dma_start(out_view, G["X"][:, :, :]).then_inc(S("stored"), 16)
                    sp.wait_ge(S("stored"), 16)


FIRST, LAST = 1, 8


def _rotation(np, n_dim, halves):
    inv = (np.float32(1.0) / np.float32(10000.0) ** (np.arange(0, n_dim, 2, dtype=np.float32) / np.float32(n_dim))).astype(np.float32)
    freqs = np.arange(T, dtype=np.float32)[:, None] * inv[None, :]
    emb = np.concatenate([freqs, freqs], axis=-1)
    sign = np.where(np.arange(n_dim) < n_dim // 2, -1.0, 1.0) if halves else np.where(np.arange(n_dim) % 2 == 0, -1.0, 1.0)
    reps = P // n_dim
    cos = np.tile(np.cos(emb).T, (reps, 1)).astype(np.float32)
    sin = np.tile((np.sin(emb) * sign).T, (reps, 1)).astype(np.float32)
    return cos, sin


def _lay_out(np, a):
    W = {}

    def put(name, x):
        W[name] = np.ascontiguousarray(x)

    put("x", a["L0_attn_a_x"].reshape(T, P))
    put("ident", np.eye(P, dtype=np.float32))
    feature = np.arange(P)
    half_swap = (feature // 8) * 8 + (feature % 8 + 4) % 8
    put("la_wqk", np.stack([a["L0_attn_a_Wq"].T, a["L0_attn_a_Wq"][half_swap].T,
                            a["L0_attn_a_Wk"].T, a["L0_attn_a_Wk"][half_swap].T], axis=1))
    put("la_wv", np.stack([a["L0_attn_a_Wv"][(feature // 8) * 8 + e].T for e in range(8)], axis=1))
    put("la_wb", a["L0_attn_a_Wb"][feature // 8].T)
    put("la_bb", a["L0_attn_a_bb"][feature // 8].reshape(P, 1))
    put("la_wo", a["L0_attn_a_Wo"].T)
    put("la_bo", a["L0_attn_a_bo"].reshape(1, P))
    put("la_scale", a["L0_attn_a_scale"].reshape(1, P))
    cos, sin = _rotation(np, 8, True)
    put("la_cos", cos)
    put("la_sin", sin)
    same_head = (feature[:, None] // 8 == feature[None, :] // 8)
    pick = [same_head & (feature[None, :] % 8 == e) for e in range(8)] + [same_head]
    put("la_pick", np.stack(pick, axis=1).astype(np.float32))
    put("ffn_gain", a["L0_ffn_ln_gamma"].reshape(P, 1))
    put("ffn_shift", a["L0_ffn_ln_beta"].reshape(P, 1))
    put("fc1_q", a["L0_ffn_fc1_q"])
    put("fc1_scales", a["L0_ffn_fc1_scales"].reshape(1, -1))
    put("fc1_bias", a["L0_ffn_fc1_bias"].reshape(4, P).T)
    put("fc2_q", a["L0_ffn_fc2_q"])
    put("fc2_scales", a["L0_ffn_fc2_scales"])
    put("fc2_bias", a["L0_ffn_fc2_bias"].reshape(1, P))
    put("dr_ww", a["L0_attn_b_Ww"].T)
    put("dr_wr", a["L0_attn_b_Wr"].T)
    put("dr_dcol", np.repeat(a["L0_attn_b_decay"], 32).reshape(P, 1))
    put("dr_drow", a["L0_attn_b_decay"].reshape(1, 4))
    put("dr_lalpha", np.repeat(a["L0_attn_b_log_alpha"], 32).reshape(P, 1))
    row, col = np.arange(P)[:, None], np.arange(P)[None, :]
    put("dr_dist", np.abs(row - col).astype(np.float32))
    put("dr_place", (col % 64 + 0 * row).astype(np.float32))
    put("dr_tail", (63 - row % 64 + np.zeros((1, 4))).astype(np.float32))
    halves = [(row // (2 * b) == col // (2 * b)) & (row // b != col // b) for b in (1, 2, 4, 8, 16, 32)]
    put("dr_halves", np.stack([m & (row > col) for m in halves], axis=1).astype(np.float32))
    put("dr_above", np.stack([halves[0] & (col > row), (col > row) & (row // 64 == col // 64)], axis=1).astype(np.float32))
    put("dr_hmask", (row // 32 == np.arange(4)[None, :]).astype(np.float32))
    put("dr_blk", (row // 32 == col // 32).astype(np.float32))
    put("ca_wqkv", a["L1_attn_a_Wqkv"])
    put("ca_bqkv", a["L1_attn_a_bqkv"].reshape(1, 3 * P))
    put("ca_wproj", a["L1_attn_a_Wproj"])
    put("ca_bproj", a["L1_attn_a_bproj"].reshape(1, P))
    row, col = np.arange(P)[:, None], np.arange(P)[None, :]
    put("ca_mask", np.stack([np.where(col > row, -1e30, 0.0), np.where(row > col, -1e30, 0.0)], axis=1).astype(np.float32))
    put("ca_sel", (np.arange(P)[:, None] % 32 == np.arange(16)[None, :]).astype(np.float32))
    put("ba_gain", a["L1_attn_b_gamma"].reshape(P, 1))
    cos, sin = _rotation(np, 64, False)
    put("ba_cos", cos)
    put("ba_sin", sin)
    wq, wk, wv = a["L1_attn_b_Wq"], a["L1_attn_b_Wkv"][:, :1024], a["L1_attn_b_Wkv"][:, 1024:]
    inner = np.arange(1024)
    neighbour = inner ^ 1
    pairs = np.zeros((8, P, 6, P), np.float32)
    for n, w in enumerate((wq, wq[:, neighbour], wk, wk[:, neighbour], wv)):
        pairs[:, :, n, :] = w.reshape(P, 8, P).transpose(1, 0, 2)
    for h in range(16):
        at = 64 * (h % 2)
        pairs[h // 2, at:at + 64, 5, at:at + 64] = a["L1_attn_b_W_bilinear"][h]
    put("ba_w", pairs)
    put("ba_wo", np.tile(a["L1_attn_b_Wo"].reshape(16, 64, P), (1, 2, 1)).transpose(1, 0, 2))
    put("moe_gate", a["L1_ffn_gate_w"].T)
    put("moe_bias", a["L1_ffn_bias_e"].reshape(1, 16))
    ups = np.concatenate([a["L1_ffn_up_w"].reshape(16 * 64, P), a["L1_ffn_shared_up"]], axis=0)
    put("moe_up", ups.T.reshape(P, 10, P))
    downs = np.concatenate([a["L1_ffn_down_w"].transpose(0, 2, 1).reshape(16 * 64, P), a["L1_ffn_shared_down"].T], axis=0)
    put("moe_down", downs.reshape(10, P, P).transpose(1, 0, 2))
    for n in (4, 16):
        put(f"before{n}", np.tril(np.ones((n, n), np.float32), -1).reshape(1, n * n))
    return W


def kernel(**inputs):
    import numpy as _np
    import concourse.bacc as _bacc
    from concourse.bass_utils import run_bass_kernel_spmd as _run

    laid = _lay_out(_np, {k: _np.asarray(v) for k, v in inputs.items()})
    nc = _bacc.Bacc("TRN2", target_bir_lowering=False, num_devices=1)
    arrays, W = {}, {}
    for name, a in laid.items():
        arrays[f"in_{name}"] = a
        W[name] = nc.dram_tensor(f"in_{name}", a.shape, mybir.dt.from_np(a.dtype), kind="ExternalInput").ap()
    out = nc.dram_tensor("out_x", (T, P), F32, kind="ExternalOutput").ap()
    program(nc, W, out, FIRST, LAST)
    got = _run(nc, [arrays], core_ids=[0])
    return got.results[0]["out_x"].reshape(1, T, P)
```
